# Optimizing a Trainium2 kernel written in Bass

```python
import numpy as np
import jax
import jax.numpy as jnp

def _softmax(x, axis=-1):
    return jax.nn.softmax(x, axis=axis)

def _gelu(x):
    return jax.nn.gelu(x, approximate=True)

def _silu(x):
    return jax.nn.silu(x)

def _sigmoid(x):
    return jax.nn.sigmoid(x)

def _layernorm(x, axis=-1, eps=1e-05):
    m = jnp.mean(x, axis=axis, keepdims=True)
    v = jnp.var(x, axis=axis, keepdims=True)
    return (x - m) / jnp.sqrt(v + eps)

def _scatter_add(tgt, idx, src, axis=0):
    return tgt.at[idx].add(src)

def _segment_sum(src, seg, n):
    return jax.ops.segment_sum(src, seg, n)
kernel_name = 'mk_xattn_ffn_d1_seqx_r2_1772a6'

def setup_inputs(seed: int=0):
    np.random.seed(seed)
    _w = jnp.asarray

    def _rec_inputs():
        import jax
        import jax.numpy as jnp
        _rk = jax.random.key(seed)
        x = -0.0002928 + 1 * jax.random.normal(jax.random.fold_in(_rk, 1), (4, 2048, 512), jnp.float32)
        _lenS = 2048 - jax.random.randint(jax.random.fold_in(_rk, 7), (4,), 0, max(1, 2048 // 4) + 1, jnp.int32)
        _lenS2 = 154 - jax.random.randint(jax.random.fold_in(_rk, 8), (4,), 0, max(1, 154 // 4) + 1, jnp.int32)
        _ctx_1024P = jax.random.normal(jax.random.fold_in(_rk, 11), (4, 16, 512), jnp.float32)
        _ctx_1024c = jax.random.dirichlet(jax.random.fold_in(_rk, 511), 0.3 * jnp.ones((16,), jnp.float32), (4, 154))
        _ctx_1024t = jnp.einsum('bsk,bkd->bsd', _ctx_1024c, _ctx_1024P)
        _ctx_1024t = _ctx_1024t * jax.lax.rsqrt(jnp.mean(jnp.square(_ctx_1024t)) + 1e-12) * 0.953939
        ctx_1024 = -1.39393e-06 + 0.999914 * (_ctx_1024t + 0.3 * jax.random.normal(jax.random.fold_in(_rk, 611), (4, 154, 512), jnp.float32))
        return (x, ctx_1024)
    x, ctx_1024 = _rec_inputs()

    def _L0_xattn_setup():
        import jax, jax.numpy as jnp
        import numpy as np
        import math
        B, T, D = (2, 1024, 512)
        H = 16
        KV = 8
        NREP = H // KV
        DH = D // H
        DEPTH = 12
        LAMBDA_INIT = 0.8 - 0.6 * math.exp(-0.3 * DEPTH)
        EPS = 1e-05
        key = jax.random.key(seed)
        ks = jax.random.split(key, 9)
        s = 0.02
        return {'q': jax.random.normal(ks[0], (B, T, D), jnp.float32), 'k': jax.random.normal(ks[1], (B, T, D), jnp.float32), 'v': jax.random.normal(ks[2], (B, T, D), jnp.float32), 'Wq': jax.random.normal(ks[3], (2 * H * DH, D), jnp.float32) * s, 'Wk': jax.random.normal(ks[4], (2 * KV * DH, D), jnp.float32) * s, 'Wv': jax.random.normal(ks[5], (KV * DH, D), jnp.float32) * s, 'Wo': jax.random.normal(ks[6], (D, D), jnp.float32) * s, 'lam': jnp.asarray(LAMBDA_INIT, jnp.float32), 'g': jnp.ones((D,), jnp.float32)}
    _L0_xattn_all = _L0_xattn_setup()
    _L0_xattn_in = {k: v for k, v in _L0_xattn_all.items() if k in ('Wq', 'Wk', 'Wv', 'Wo', 'lam', 'g')}
    del _L0_xattn_all

    def _L0_ffn_setup():
        import jax, jax.numpy as jnp
        import numpy as np
        LN_EPS = 1e-05

        def layer_norm(x, g, b):
            mu = jnp.mean(x, axis=-1, keepdims=True)
            var = jnp.mean(jnp.square(x - mu), axis=-1, keepdims=True)
            return (x - mu) * jax.lax.rsqrt(var + LN_EPS) * g + b

        def ternary_quant(w):
            scale = 1.0 / jnp.clip(jnp.mean(jnp.abs(w)), 1e-05)
            wq = jnp.clip(jnp.round(w * scale), -1.0, 1.0) / scale
            return w + jax.lax.stop_gradient(wq - w)
        key = jax.random.key(seed)
        ks = jax.random.split(key, 3)
        dim, hidden = (512, 2048)
        B, S = (8, 512)
        x = jax.random.normal(ks[0], (B, S, dim), dtype=jnp.float32)
        w1 = jax.random.normal(ks[1], (hidden, dim), dtype=jnp.float32) * 0.02
        w2 = jax.random.normal(ks[2], (dim, hidden), dtype=jnp.float32) * 0.02
        return {'x': x, 'ln1_g': jnp.ones((dim,), jnp.float32), 'ln1_b': jnp.zeros((dim,), jnp.float32), 'w1': w1, 'b1': jnp.zeros((hidden,), jnp.float32), 'ln2_g': jnp.ones((hidden,), jnp.float32), 'ln2_b': jnp.zeros((hidden,), jnp.float32), 'w2': w2, 'b2': jnp.zeros((dim,), jnp.float32)}
    _L0_ffn_all = _L0_ffn_setup()
    _L0_ffn_in = {k: v for k, v in _L0_ffn_all.items() if k in ('ln1_g', 'ln1_b', 'w1', 'b1', 'ln2_g', 'ln2_b', 'w2', 'b2')}
    del _L0_ffn_all
    return {'x': x, 'ctx_1024': ctx_1024, 'L0_xattn_Wq': _L0_xattn_in['Wq'], 'L0_xattn_Wk': _L0_xattn_in['Wk'], 'L0_xattn_Wv': _L0_xattn_in['Wv'], 'L0_xattn_Wo': _L0_xattn_in['Wo'], 'L0_xattn_lam': _L0_xattn_in['lam'], 'L0_xattn_g': _L0_xattn_in['g'], 'L0_ffn_ln1_g': _L0_ffn_in['ln1_g'], 'L0_ffn_ln1_b': _L0_ffn_in['ln1_b'], 'L0_ffn_w1': _L0_ffn_in['w1'], 'L0_ffn_b1': _L0_ffn_in['b1'], 'L0_ffn_ln2_g': _L0_ffn_in['ln2_g'], 'L0_ffn_ln2_b': _L0_ffn_in['ln2_b'], 'L0_ffn_w2': _L0_ffn_in['w2'], 'L0_ffn_b2': _L0_ffn_in['b2']}

def reference(x, ctx_1024, L0_xattn_Wq, L0_xattn_Wk, L0_xattn_Wv, L0_xattn_Wo, L0_xattn_lam, L0_xattn_g, L0_ffn_ln1_g, L0_ffn_ln1_b, L0_ffn_w1, L0_ffn_b1, L0_ffn_ln2_g, L0_ffn_ln2_b, L0_ffn_w2, L0_ffn_b2):
    import jax
    import jax.numpy as jnp

    def _L0_xattn_ref(q, k, v, Wq, Wk, Wv, Wo, lam, g):
        import jax, jax.numpy as jnp
        import numpy as np
        import math
        B, T, D = (2, 1024, 512)
        H = 16
        KV = 8
        NREP = H // KV
        DH = D // H
        DEPTH = 12
        LAMBDA_INIT = 0.8 - 0.6 * math.exp(-0.3 * DEPTH)
        EPS = 1e-05
        bsz, tgt_len, _ = q.shape
        src_len = k.shape[1]
        qp = q @ Wq.T
        kp = k @ Wk.T
        vp = v @ Wv.T
        q1, q2 = jnp.split(qp, 2, axis=-1)
        k1, k2 = jnp.split(kp, 2, axis=-1)
        q1 = q1.reshape(bsz, tgt_len, H, DH).transpose(0, 2, 1, 3)
        q2 = q2.reshape(bsz, tgt_len, H, DH).transpose(0, 2, 1, 3)
        k1 = k1.reshape(bsz, src_len, KV, DH).transpose(0, 2, 1, 3)
        k2 = k2.reshape(bsz, src_len, KV, DH).transpose(0, 2, 1, 3)
        vh = vp.reshape(bsz, src_len, KV, DH).transpose(0, 2, 1, 3)
        k1 = jnp.repeat(k1, NREP, axis=1)
        k2 = jnp.repeat(k2, NREP, axis=1)
        vh = jnp.repeat(vh, NREP, axis=1)
        scaling = 1.0
        s1 = jnp.einsum('bhtd,bhsd->bhts', q1, k1) * scaling
        s2 = jnp.einsum('bhtd,bhsd->bhts', q2, k2) * scaling
        w1 = jax.nn.softmax(s1.astype(jnp.float32), axis=-1).astype(q.dtype)
        w2 = jax.nn.softmax(s2.astype(jnp.float32), axis=-1).astype(q.dtype)
        w = w1 - lam * w2
        attn = jnp.einsum('bhts,bhsd->bhtd', w, vh)
        attn = attn.transpose(0, 2, 1, 3).reshape(bsz, tgt_len, D)
        rms = jax.lax.rsqrt(jnp.mean(attn * attn, axis=-1, keepdims=True) + EPS)
        attn = attn * rms * g
        attn = attn * (1.0 - LAMBDA_INIT)
        return attn @ Wo.T

    def _L0_ffn_ref(x, ln1_g, ln1_b, w1, b1, ln2_g, ln2_b, w2, b2):
        import jax, jax.numpy as jnp
        import numpy as np
        LN_EPS = 1e-05

        def layer_norm(x, g, b):
            mu = jnp.mean(x, axis=-1, keepdims=True)
            var = jnp.mean(jnp.square(x - mu), axis=-1, keepdims=True)
            return (x - mu) * jax.lax.rsqrt(var + LN_EPS) * g + b

        def ternary_quant(w):
            scale = 1.0 / jnp.clip(jnp.mean(jnp.abs(w)), 1e-05)
            wq = jnp.clip(jnp.round(w * scale), -1.0, 1.0) / scale
            return w + jax.lax.stop_gradient(wq - w)
        h = layer_norm(x, ln1_g, ln1_b)
        h = jnp.einsum('bsd,hd->bsh', h, ternary_quant(w1)) + b1
        h = jax.nn.gelu(h, approximate=False)
        h = layer_norm(h, ln2_g, ln2_b)
        out = jnp.einsum('bsh,dh->bsd', h, ternary_quant(w2)) + b2
        return out
    x = x + _L0_xattn_ref(_layernorm(x, axis=-1), ctx_1024, ctx_1024, L0_xattn_Wq, L0_xattn_Wk, L0_xattn_Wv, L0_xattn_Wo, L0_xattn_lam, L0_xattn_g)
    x = x + _L0_ffn_ref(_layernorm(x, axis=-1), L0_ffn_ln1_g, L0_ffn_ln1_b, L0_ffn_w1, L0_ffn_b1, L0_ffn_ln2_g, L0_ffn_ln2_b, L0_ffn_w2, L0_ffn_b2)
    return x

_drawn_inputs = setup_inputs


def setup_inputs(seed=0):
    import zlib

    import numpy as np

    out = dict(_drawn_inputs(seed))
    spreads = {'L0_xattn_g': (1.0, 0.6),
     'L0_ffn_ln1_g': (1.0, 0.2),
     'L0_ffn_ln1_b': (0.0, 0.1),
     'L0_ffn_b1': (0.0, 0.1),
     'L0_ffn_ln2_g': (1.0, 0.2),
     'L0_ffn_ln2_b': (0.0, 0.1),
     'L0_ffn_b2': (0.0, 0.1)}
    factors = {}
    for name, (base, spread) in spreads.items():
        noise = np.random.default_rng([zlib.crc32(name.encode()), seed]).standard_normal(out[name].shape)
        drawn = base * np.exp(spread * noise) if base else spread * noise
        out[name] = jnp.asarray(drawn.astype(out[name].dtype))
    for name, factor in factors.items():
        out[name] = (out[name] * factor).astype(out[name].dtype)
    return out
```

```python
import math
from contextlib import ExitStack

import concourse.bass as bass
from concourse import mybir

F32 = mybir.dt.float32
F16 = mybir.dt.float16
ALU = mybir.AluOpType
ACT = mybir.ActivationFunctionType
AX = mybir.AxisListType

P = 128
D = 512
KD = D // P
BATCH, T, S = 4, 2048, 154
H, KV, DH = 16, 8, 32
HID = 2048
JH = HID // P
TB = 512
TT = TB // P
NBLK = BATCH * T // TB
BLK_PER_BATCH = T // TB
UNITS = 2 * H
KUNITS = 2 * KV
QM = UNITS * DH // P
UPT = P // DH
SR = S - P
SPAD = P + DH
STK = 3 * DH
STKM = STK + 2
MSCALE = 64.0
WSCALE = 256.0
ASCALE = 16.0
EPS = 1e-5
LAMBDA_INIT = 0.8 - 0.6 * math.exp(-0.3 * 12)
UPB = 3
TBLK = -(-UNITS // UPB)
NT = TT * TBLK
TSTEP = 4
ORDER = [m for p in range(QM // 2) for m in (p, p + QM // 2)]
QDMA = 3 * UPT * 16


def key_unit(u):
    return u // H * KV + (u % H) // (H // KV)


def wait(eng, sem, c, per, k):
    if isinstance(c, int) and c * per + k <= 0:
        return
    eng.wait_ge(sem, c * per + k)


def build(nc, x, ctx, wq, wk, wv, wo, lam, g, ln1_g, ln1_b, w1, b1, ln2_g, ln2_b, w2, b2, out):
    x_blk = x.rearrange("b t d -> (b t) d").rearrange("(c s p) d -> c p s d", s=TT, p=P)
    out_blk = out.rearrange("b t d -> (b t) d").rearrange("(c s p) d -> c p s d", s=TT, p=P)
    k_store = nc.dram_tensor("k_store", (BATCH, STKM, KUNITS, SPAD), F16, kind="Internal").ap()
    v_store = nc.dram_tensor("v_store", (BATCH, P, KV * DH + QM // 2 * P), F32, kind="Internal").ap()
    VM = KV * DH

    with ExitStack() as es:
        def sb(name, shape, dt):
            return es.enter_context(nc.sbuf_tensor(name, shape, dt))

        def sem(name):
            return es.enter_context(nc.semaphore(name))

        ps = es.enter_context(nc.psum_tensor("ps", [P, 8, 512], F32))
        B_SREST, B_Q, B_O, B_L = 4, 5, 6, 7
        B_H = 4

        wqT_hi, wqT_lo = sb("wqT_hi", [P, KD, 2 * H * DH], F16), sb("wqT_lo", [P, KD, 2 * H * DH], F16)
        woT_hi, woT_lo = sb("woT_hi", [P, KD, D], F16), sb("woT_lo", [P, KD, D], F16)
        w1T, w2T = sb("w1T", [P, KD, HID], F16), sb("w2T", [P, JH, D], F16)
        ident, ident16 = sb("ident", [P, P], F32), sb("ident16", [P, P], F16)
        ones, ones_rest = sb("ones", [P, P], F32), sb("ones_rest", [P, P], F32)
        neghalf = sb("neghalf", [P, TT], F32)
        neglam = sb("neglam", [P, 1], F32)
        vec_src = [(b1, JH), (ln2_g, JH), (ln2_b, JH), (g, KD), (ln1_g, KD), (ln1_b, KD)]
        NV = sum(n for _, n in vec_src)
        vec_cols = sb("vec_cols", [P, NV], F32)
        vec_at = [sum(n for _, n in vec_src[:i]) for i in range(len(vec_src))]
        bias1, g2_col, b2ln_col, g_col, g1_col, b1ln_col = (
            vec_cols[:, at:at + n] for at, (_, n) in zip(vec_at, vec_src))
        wabs, wmean = sb("wabs", [P, 2], F32), sb("wmean", [P, 2], F32)
        wscale, wstep = sb("wscale", [P, 2], F32), sb("wstep", [P, 2], F32)
        b1ln16 = sb("b1ln16", [P, KD, 2], F16)
        g2_row, out_const = sb("g2_row", [P, D], F32), sb("out_const", [P, D], F32)
        k_max, k_att = sb("k_max", [P, KUNITS, SPAD], F16), sb("k_att", [P, KUNITS, SPAD], F16)
        v_att = sb("v_att", [P, VM + QM // 2 * P], F32)
        stack_raw = sb("stack_raw", [P, UNITS * TB // 2], F32)
        stack = stack_raw[:].bitcast(F16).rearrange("p (u t) -> p u t", u=UNITS)
        ctxT = stack_raw[:, 0:KD * BATCH * S].rearrange("p (k b s) -> p k b s", k=KD, b=BATCH)
        o1 = KD * BATCH * S
        wkT = stack_raw[:, o1:o1 + KD * D].rearrange("p (k n) -> p k n", k=KD)
        wvT = stack_raw[:, o1 + KD * D:o1 + KD * (D + VM)].rearrange("p (k n) -> p k n", k=KD)
        o2 = o1 + KD * (D + VM)
        NSTG = 4
        stage = stack_raw[:, o2:o2 + NSTG * D].rearrange("p (n d) -> p n d", n=NSTG)
        arena = sb("arena", [P, 2 * HID * D // P], F32)
        w1n = arena[:, 0:JH * D].rearrange("p (r d) -> p r d", r=JH)
        w2n = arena[:, JH * D:2 * JH * D].rearrange("p (r h) -> p r h", r=KD)
        cut = [0]

        def part(words):
            cut[0] += words
            assert cut[0] <= 2 * HID * D // P
            return arena[:, cut[0] - words:cut[0]]

        x_in = part(TT * D).rearrange("p (s d) -> p s d", s=TT)
        x_res = part(TT * D).rearrange("p (s d) -> p s d", s=TT)
        xhat = part(TT * D).rearrange("p (s d) -> p s d", s=TT)
        probs_words = 2 * 5 * TB
        probs_raw = part(probs_words)
        probs = probs_raw.rearrange("p (b n t) -> p b n t", b=2, n=5)
        gelu_t = probs_raw[:, 0:2 * TB].rearrange("p (b t) -> p b t", b=2)
        gsq_t = probs_raw[:, 2 * TB:4 * TB].rearrange("p (b t) -> p b t", b=2)
        gg16 = probs_raw[:, 4 * TB:7 * TB].bitcast(F16).rearrange("p (b e t) -> p b e t", b=3, e=2)
        acc = probs_raw[:, 7 * TB:9 * TB].rearrange("p (e t) -> p e t", e=2)
        attn16 = part(KD * TB).bitcast(F16).rearrange("p (e k t) -> p e k t", e=2, k=KD)
        rows16 = sb("rows16", [P, 2, KD, TB], F16)
        q16 = sb("q16", [P, 2, 2, TB], F16)
        attn_raw = sb("attn_raw", [P, 7 * TB], F32)
        attn = attn_raw[:, 0:2 * TB].rearrange("p (b t) -> p b t", b=2)
        attn_sq = attn_raw[:, 2 * TB:4 * TB].rearrange("p (b t) -> p b t", b=2)
        inv_l, first, second = (attn_raw[:, n * TB:(n + 1) * TB] for n in (4, 5, 6))
        sq_acc = sb("sq_acc", [P, TB], F32)
        signs = attn_raw[:, 0:3 * TB].bitcast(F16).rearrange("p (n e t) -> p n e t", n=3, e=2)
        tern = attn_raw[:, 3 * TB:4 * TB].bitcast(F16).rearrange("p (n t) -> p n t", n=2)
        k16 = rows16[:].rearrange("p e k t -> p (e k t)")[:, 0:2 * BATCH * SPAD].rearrange(
            "p (e b s) -> p e b s", e=2, b=BATCH)
        vec_rows = sq_acc[0:NV, 0:P]
        v_new = attn_raw[:, 4 * TB:4 * TB + VM + QM // 2 * P]
        b2_bcast = q16[:].rearrange("p a b t -> p (a b t)").bitcast(F32)[:, 0:2 * D].rearrange("p (e d) -> p e d", e=2)
        krows = k_att[0:2]
        ln2_16 = sb("ln2_16", [P, 2, 2, JH], F16)
        lnb = sb("lnb", [P, 2, 2, P], F16)
        negmax = sb("negmax", [P, TT, UNITS], F32)
        negmax16 = sb("negmax16", [P, TT, P // UNITS, UNITS], F16)
        negmaxT = sb("negmaxT", [2 * UNITS, TB], F16)
        stats = sb("stats", [P, 2, TT, 6], F32)
        gate = sb("gate", [P, 1], F32)
        mv = sb("mv", [P, 2, TT, 2], F32)
        var = sb("var", [P, 4, TT], F32)
        rstd = sb("rstd", [P, 4, TT], F32)
        rms_scale = sb("rms_scale", [P, TT], F32)
        mean_g, meansq_g, var_g = sb("mean_g", [P, TT], F32), sb("meansq_g", [P, TT], F32), sb("var_g", [P, TT], F32)
        scale_g, shift_g = sb("scale_g", [P, TT], F32), sb("shift_g", [P, TT], F32)

        s_ident0, s_ident, s_consts = sem("ident_zero"), sem("ident_ready"), sem("consts_ready")
        s_vec, s_vect, s_vecc = sem("vectors_loaded"), sem("vectors_transposed"), sem("vectors_copied")
        s_w1, s_w2 = sem("w1_loaded"), sem("w2_loaded")
        s_stage = [sem(f"stage_loaded{n}") for n in range(NSTG)]
        s_tile, s_tile_hi, s_tile_out = sem("tile_transposed"), sem("tile_hi"), sem("tile_out")
        s_gcol = sem("g_scaled")
        s_kv, s_k_hi, s_k_lo = sem("kv_product"), sem("k_hi"), sem("k_lo")
        s_kst, s_vst, s_vnew = sem("k_stored"), sem("v_stored"), sem("v_new")
        s_krows, s_v0 = sem("key_rows"), sem("v_cleared")
        s_abs, s_abssum, s_scale = sem("abs_summed"), sem("abs_total"), sem("scale_step")
        s_sign, s_tern, s_ternT = sem("sign_ready"), sem("ternary_ready"), sem("ternary_transposed")
        s_ternC = [sem("ternary_copied_even"), sem("ternary_copied_odd")]
        s_b1ln, s_l2, s_lnb, s_lnrow, s_bias, s_rows = (sem(n) for n in (
            "b1ln_split", "ln2_split", "ln2_spread", "ln2_product", "bias_ready", "rows_ready"))
        s_xin, s_xres, s_kmax, s_katt, s_vatt = (sem(n) for n in (
            "x_in_loaded", "x_res_loaded", "k_max_loaded", "k_att_loaded", "v_att_loaded"))
        s_st1, s_ag1, s_var1, s_rstd1, s_xhat1 = (sem(n) for n in (
            "ln1_stats", "ln1_aggr", "ln1_var", "ln1_rstd", "ln1_rows"))
        s_xt, s_xt_hi, s_xt_lo = sem("x_transposed"), sem("x_hi"), sem("x_lo")
        s_q, s_q_hi, s_q_lo = sem("q_product"), sem("q_hi"), sem("q_lo")
        s_pair_seen = sem("q_pair_seen")
        s_qst = [sem("q_stacked0"), sem("q_stacked1")]
        s_t, s_tmax, s_nmhi, s_nmlo, s_nmt, s_nmc, s_nmst = (sem(n) for n in (
            "row_scores", "row_max", "negmax_hi", "negmax_lo", "negmax_transposed", "negmax_copied", "negmax_stacked"))
        s_s, s_p, s_pv, s_inv, s_ol, s_sec, s_att = (sem(n) for n in (
            "scores", "probs", "values_done", "inverse_sum", "sums_read", "second_ready", "attn_ready"))
        s_att_hi, s_att_lo, s_sq, s_sqsum = sem("attn_hi"), sem("attn_lo"), sem("attn_square"), sem("attn_square_sum")
        s_rms, s_var2, s_rstd2, s_rsc = sem("rms_sum"), sem("rms_var"), sem("rms_rstd"), sem("rms_scaled")
        s_wo, s_mid, s_st2, s_ag2, s_var3, s_rstd3, s_xhat2 = (sem(n) for n in (
            "out_projected", "mid_ready", "ln2_stats", "ln2_aggr", "ln2_var", "ln2_rstd", "ln2_rows"))
        s_ht, s_ht_hi, s_ht_lo = sem("h_transposed"), sem("h_hi"), sem("h_lo")
        s_f1, s_gelu, s_gsq, s_gg_hi, s_gg_lo, s_acc = (sem(n) for n in (
            "hidden", "gelu", "gelu_square", "gelu_hi", "gelu_lo", "gelu_summed"))
        s_f2, s_sums, s_gln, s_rstd4, s_const, s_out, s_stored = (sem(n) for n in (
            "ffn_out", "gelu_sums", "gelu_ln_step", "gelu_rstd", "const_added", "out_ready", "out_stored"))
        s_gstep, s_gscaled, s_shift = sem("gelu_ln_small_step"), sem("gelu_ln_scaled"), sem("shift_added")

        tiles = [(ctx[b, r:r + n, :], n, "ctx", (b, r)) for b in range(BATCH) for r, n in ((0, P), (P, SR))]
        tiles += [(wk[r * P:(r + 1) * P, :], P, "wk", r) for r in range(D // P)]
        tiles += [(wv[r * P:(r + 1) * P, :], P, "wv", r) for r in range(VM // P)]
        tiles += [(wq[r * P:(r + 1) * P, :], P, "wq", r) for r in range(QM)]
        tiles += [(wo[r * P:(r + 1) * P, :], P, "wo", r) for r in range(KD)]
        N_KV_TILES = 2 * BATCH + D // P + VM // P
        KGRP = [(m, pair) for m in range(KUNITS * DH // P) for pair in range(BATCH // 2)]
        NTERN = 2 * JH
        NVEC = len(vec_src) + 2

        def ternary_out(copy, n):
            src = ps[:, 4 + n % 4, 0:TB // 2].bitcast(F16).rearrange("p (k r) -> p k r", k=KD)
            if n < JH:
                return copy(w1T[:, :, n * P:(n + 1) * P], src)
            r, q = divmod(n - JH, KD)
            return copy(w2T[:, KD * q:KD * q + KD, r * P:(r + 1) * P], src)

        def natural(n):
            if n < JH:
                return w1n[:, n, :], 0
            r, q = divmod(n - JH, KD)
            return w2n[:, r, q * D:(q + 1) * D], 1

        block = es.enter_context(nc.Block())

        @block.sync
        def _(sp):
            def setup():
                for n, (src, rows, _, _) in enumerate(tiles):
                    if n >= NSTG:
                        sp.wait_ge(s_tile, n - NSTG + 1)
                    sp.dma_start(stage[0:rows, n % NSTG, :], src).then_inc(s_stage[n % NSTG], 16)
                    if n == 3:
                        for at, (src, n_rows) in zip(vec_at, vec_src):
                            sp.dma_start(vec_rows[at:at + n_rows, :], src.rearrange("(k p) -> k p", p=P)).then_inc(s_vec, 16)
                        sp.dma_start(neglam[:], lam.rearrange("(a b) -> a b", a=1).broadcast_to([P, 1])).then_inc(s_vec, 16)
                        sp.dma_start(out_const[:], b2.rearrange("(a d) -> a d", a=1).broadcast_to([P, D])).then_inc(s_vec, 16)
                    if n == N_KV_TILES - 1:
                        sp.dma_start(w1n, w1.rearrange("(r p) d -> p r d", p=P)).then_inc(s_w1, 16)
                        sp.dma_start(w2n, w2.rearrange("(r p) h -> p r h", p=P)).then_inc(s_w2, 16)
                sp.wait_ge(s_krows, 2)
                for b in range(BATCH):
                    sp.dma_start(k_store[b, STK:STKM, :, :], krows).then_inc(s_kst, 16)
                for m in range(KUNITS // UPT):
                    sp.wait_ge(s_k_lo, 2 * m + 2)
                    for b in range(BATCH):
                        for c3, e in enumerate((0, 0, 1)):
                            dst = k_store[b, DH * c3:DH * c3 + DH, UPT * m:UPT * m + UPT, :]
                            sp.dma_start(dst.rearrange("d u s -> u d s"), k16[:, e, b, :]).then_inc(s_kst, 16)
                for b in range(BATCH):
                    sp.wait_ge(s_vnew, 5 * b + 5)
                    sp.dma_start(v_store[b], v_new).then_inc(s_vst, 16)
                sp.wait_ge(s_kst, 16 * BATCH * (1 + 3 * KUNITS // UPT))
                sp.wait_ge(s_vst, 16 * BATCH)

            def batch_of(c):
                return c // BLK_PER_BATCH if isinstance(c, int) else sp.snap(c // BLK_PER_BATCH)

            def load_k_max(c, b):
                wait(sp, s_t, c, NT, 0)
                sp.dma_start(k_max[0:STKM], k_store[b]).then_inc(s_kmax, 16)

            def load_kv_att(c, b):
                wait(sp, s_pv, c, QM, 0)
                sp.dma_start(k_att[0:STKM], k_store[b]).then_inc(s_katt, 16)
                sp.dma_start(v_att[:], v_store[b]).then_inc(s_vatt, 16)

            def load_x_in(c):
                wait(sp, s_xhat1, c, TT, 0)
                sp.dma_start(x_in, x_blk[c]).then_inc(s_xin, 16)

            def load_x_res(c):
                wait(sp, s_stored, c, 16 * TT, 0)
                sp.dma_start(x_res, x_blk[c]).then_inc(s_xres, 16)

            def stack_queries(c, n, before):
                if before is None:
                    wait(sp, s_q_lo, c, QM, n + 1)
                else:
                    wait(sp, s_q_lo, c, QM, n + 1)
                    sp.sem_inc(s_pair_seen, 1)
                    wait(sp, s_s, before, 2 * QM, 2 * n + 2)
                for i in range(UPT):
                    for c3, e in enumerate((0, 1, 0)):
                        sp.dma_start(stack[DH * c3:DH * c3 + DH, UPT * ORDER[n] + i, :],
                                     q16[DH * i:DH * i + DH, n % 2, e, :]).then_inc(s_qst[n % 2], 16)

            def stack_maxima(c):
                wait(sp, s_nmc, c, 1, 1)
                for e in range(2):
                    sp.dma_start(stack[STK + e:STK + e + 1, :, :],
                                 negmaxT[UNITS * e:UNITS * (e + 1), :]).then_inc(s_nmst, 16)

            def store(c):
                for tt in range(TT):
                    wait(sp, s_out, c, TT, tt + 1)
                    sp.dma_start(out_blk[c][:, tt, :], x_res[:, tt, :]).then_inc(s_stored, 16)

            def iteration(i, ahead, ahead2):
                if ahead:
                    b = batch_of(i + 1)
                    load_k_max(i + 1, b)
                if ahead2:
                    load_x_in(i + 2)
                if ahead:
                    for n in range(QM):
                        stack_queries(i + 1, n, i)
                load_x_res(i)
                if ahead:
                    load_kv_att(i + 1, b)
                    stack_maxima(i + 1)
                store(i)

            setup()
            sp.wait_ge(s_tern, NTERN)
            sp.wait_ge(s_rows, 2)
            load_x_in(0)
            load_k_max(0, 0)
            load_kv_att(0, 0)
            for n in range(QM):
                stack_queries(0, n, None)
            load_x_in(1)
            stack_maxima(0)
            iteration(0, True, True)
            with sp.Fori(1, NBLK - 2) as i:
                iteration(i, True, True)
            iteration(NBLK - 2, True, False)
            iteration(NBLK - 1, False, False)
            sp.wait_ge(s_stored, NBLK * 16 * TT)

        @block.gpsimd
        def _(pool):
            def setup():
                pool.memset(ident[:], 0.0).then_inc(s_ident0, 1)
                pool.wait_ge(s_ident0, 1)
                pool.affine_select(out=ident[:], in_=ident[:], compare_op=ALU.not_equal, fill=1.0, base=0,
                                   pattern=[[-1, P]], channel_multiplier=1).then_inc(s_ident, 1)
                pool.memset(neghalf[:], -0.5).then_inc(s_ident, 1)
                pool.wait_ge(s_ident, 2)

            def power(slot, ready, done, c):
                wait(pool, ready, c, 1, 1)
                pool.tensor_tensor(rstd[:, slot, :], var[:, slot, :], neghalf[:], ALU.pow).then_inc(done, 1)

            def sum_squares(c):
                wait(pool, s_sq, c, KD, 2)
                wait(pool, s_rms, c, 1, 0)
                pool.tensor_tensor(sq_acc[:], attn_sq[:, 0, :], attn_sq[:, 1, :], ALU.add).then_inc(s_sqsum, 1)
                for mp in range(2, KD):
                    wait(pool, s_sq, c, KD, mp + 1)
                    wait(pool, s_sqsum, c, KD - 1, mp - 1)
                    pool.tensor_tensor(sq_acc[:], sq_acc[:], attn_sq[:, mp % 2, :], ALU.add).then_inc(s_sqsum, 1)

            def add_constant(c):
                wait(pool, s_xhat2, c, TT, TT)
                for tt in range(TT):
                    ins = pool.tensor_tensor(x_res[:, tt, :], x_res[:, tt, :], out_const[:], ALU.add)
                ins.then_inc(s_const, 1)

            def sum_gelu(c, j):
                wait(pool, s_gsq, c, JH, j + 1)
                if j == 1:
                    wait(pool, s_sums, c, 1, 0)
                    for e, src in ((0, gelu_t), (1, gsq_t)):
                        ins = pool.tensor_tensor(acc[:, e, :], src[:, 0, :], src[:, 1, :], ALU.add)
                else:
                    wait(pool, s_acc, c, JH - 1, j - 1)
                    for e, src in ((0, gelu_t), (1, gsq_t)):
                        ins = pool.tensor_tensor(acc[:, e, :], acc[:, e, :], src[:, j % 2, :], ALU.add)
                ins.then_inc(s_acc, 1)

            def iteration(i, ahead2):
                sum_squares(i)
                power(1, s_var2, s_rstd2, i)
                power(2, s_var3, s_rstd3, i)
                add_constant(i)
                for j in range(1, JH):
                    sum_gelu(i, j)
                    if j == 13 and ahead2:
                        power(0, s_var1, s_rstd1, i + 2)
                power(3, s_gln, s_rstd4, i)

            setup()
            power(0, s_var1, s_rstd1, 0)
            power(0, s_var1, s_rstd1, 1)
            iteration(0, True)
            with pool.Fori(1, NBLK - 2) as i:
                iteration(i, True)
            iteration(NBLK - 2, False)
            iteration(NBLK - 1, False)

        @block.scalar
        def _(act):
            def setup():
                act.wait_ge(s_gcol, 1)
                for n, (_, rows, kind, at) in enumerate(tiles):
                    act.wait_ge(s_tile, n + 1)
                    bank = ps[:, n % 4, :].rearrange("p (k r) -> p k r", k=KD)
                    if kind == "ctx":
                        b, r = at
                        act.copy(ctxT[:, :, b, r:r + rows], bank[:, :, 0:rows]).then_inc(s_tile_hi, 1)
                    elif kind in ("wk", "wv"):
                        dst = wkT if kind == "wk" else wvT
                        act.copy(dst[:, :, at * P:(at + 1) * P], bank).then_inc(s_tile_hi, 1)
                    elif kind == "wq":
                        act.mul(wqT_hi[:, :, at * P:(at + 1) * P], bank, WSCALE).then_inc(s_tile_hi, 1)
                    else:
                        for k in range(KD):
                            ins = act.activation(woT_hi[:, k, at * P:(at + 1) * P], bank[:, k, :], ACT.Identity,
                                                 scale=g_col[:, k:k + 1])
                        ins.then_inc(s_tile_hi, 1)
                for n, (m, pair) in enumerate(KGRP):
                    act.wait_ge(s_kv, n + 1)
                    if pair == 0 and m > 0:
                        act.wait_ge(s_kst, 16 * BATCH * (1 + 3 * m))
                    if n == 0:
                        act.wait_ge(s_v0, 1)
                    src = ps[:, n % 4, 0:2 * S].rearrange("p (b s) -> p b s", b=2)
                    act.copy(k16[:, 0, 2 * pair:2 * pair + 2, 0:S], src).then_inc(s_k_hi, 1)
                for n in range(1, NTERN, 2):
                    act.wait_ge(s_ternT, n + 1)
                    ternary_out(act.copy, n).then_inc(s_ternC[1], 1)

            def x_hi(c):
                for tt in range(TT):
                    wait(act, s_xt, c, TT, tt + 1)
                    act.copy(rows16[:, 0, :, tt * P:(tt + 1) * P],
                             ps[:, B_O + tt % 2, :].rearrange("p (k t) -> p k t", k=KD)).then_inc(s_xt_hi, 1)

            def q_hi(c, n):
                wait(act, s_q, c, QM, n + 1)
                wait(act, s_qst[n % 2], c, QDMA * QM // 2, QDMA * (n // 2))
                act.mul(q16[:, n % 2, 0, :], ps[:, B_Q, :], 1.0 / WSCALE).then_inc(s_q_hi, 1)

            def exponentials(c, gi):
                buf = gi % 2
                wait(act, s_s, c, 2 * QM, 2 * gi + 1)
                if gi >= 2:
                    wait(act, s_pv, c, QM, gi - 1)
                act.activation(probs[:, buf, 0:2, :], ps[:, 0:2, :], ACT.Exp).then_inc(s_p, 1)
                wait(act, s_s, c, 2 * QM, 2 * gi + 2)
                act.activation(probs[:, buf, 2:5, :], ps[:, 2:5, :], ACT.Exp).then_inc(s_p, 1)

            def attn_hi(c, mp):
                wait(act, s_att, c, KD, mp + 1)
                act.mul(attn16[:, 0, mp, :], attn[:, mp % 2, :], ASCALE).then_inc(s_att_hi, 1)
                if mp >= 2:
                    wait(act, s_sqsum, c, KD - 1, mp - 1)
                act.activation(attn_sq[:, mp % 2, :], attn[:, mp % 2, :], ACT.Square).then_inc(s_sq, 1)

            def h_hi(c):
                wait(act, s_ht, c, 1, 1)
                for k in range(KD):
                    act.activation(rows16[:, 0, k, :], ps[:, B_H + k, :], ACT.Identity,
                                   scale=g1_col[:, k:k + 1]).then_inc(s_ht_hi, 1)

            def gelu(c, j):
                wait(act, s_f1, c, JH, j + 1)
                if j >= 2:
                    wait(act, s_acc, c, JH - 1, max(1, j - 2))
                    wait(act, s_gg_lo, c, JH, j - 1)
                act.activation(gelu_t[:, j % 2, :], ps[:, B_H + j % 2, :], ACT.Gelu, bias=bias1[:, j:j + 1],
                               scale=wstep[:, 0:1]).then_inc(s_gelu, 1)
                wait(act, s_gelu, c, JH, j + 1)
                if j >= 3:
                    wait(act, s_f2, c, JH, j - 2)
                act.activation(gg16[:, j % 3, 0, :], gelu_t[:, j % 2, :], ACT.Identity,
                               scale=g2_col[:, j:j + 1]).then_inc(s_gg_hi, 1)
                act.activation(gsq_t[:, j % 2, :], gelu_t[:, j % 2, :], ACT.Square).then_inc(s_gsq, 1)

            def iteration(i, ahead):
                if ahead:
                    x_hi(i + 1)
                    q_hi(i + 1, 0)
                for gi in range(QM):
                    exponentials(i, gi)
                    if gi >= 3 and gi % 2 == 1:
                        attn_hi(i, (gi - 3) // 2)
                    if ahead and gi + 1 < QM:
                        q_hi(i + 1, gi + 1)
                attn_hi(i, KD - 1)
                h_hi(i)
                for j in range(JH):
                    gelu(i, j)

            setup()
            x_hi(0)
            for n in range(QM):
                q_hi(0, n)
            iteration(0, True)
            with act.Fori(1, NBLK - 2) as i:
                iteration(i, True)
            iteration(NBLK - 2, True)
            iteration(NBLK - 1, False)

        @block.vector
        def _(dve):
            def setup():
                dve.memset(ones[:], 1.0)
                dve.memset(ones_rest[:], 0.0)
                dve.memset(krows, MSCALE)
                dve.memset(k16, 0.0)
                dve.memset(negmax16[:], 0.0)
                dve.memset(v_new, 0.0).then_inc(s_v0, 1)
                dve.wait_ge(s_v0, 1)
                for i in range(UPT):
                    dve.memset(ones_rest[DH * i:DH * i + SR, DH * i:DH * i + DH], 1.0)
                dve.memset(krows[:, :, S:SPAD], 0.0).then_inc(s_krows, 2)
                dve.wait_ge(s_ident, 2)
                dve.tensor_copy(ident16[:], ident[:]).then_inc(s_consts, 1)
                dve.wait_ge(s_vec, 16 * NVEC)
                dve.wait_ge(s_vect, 1)
                dve.tensor_copy(vec_cols[:], ps[:, 4, 0:NV]).then_inc(s_vecc, 1)
                dve.wait_ge(s_vecc, 1)
                dve.tensor_scalar(g_col, g_col, WSCALE, None, ALU.mult)
                dve.tensor_scalar(neglam[:], neglam[:], -1.0, None, ALU.mult).then_inc(s_gcol, 1)
                for n, (_, rows, kind, at) in enumerate(tiles):
                    bank = ps[:, n % 4, :].rearrange("p (k r) -> p k r", k=KD)
                    if kind == "wq":
                        dve.wait_ge(s_tile_hi, n + 1)
                        cols = slice(at * P, (at + 1) * P)
                        dve.scalar_tensor_tensor(wqT_lo[:, :, cols], bank, WSCALE, wqT_hi[:, :, cols],
                                                 ALU.mult, ALU.subtract).then_inc(s_tile_out, 1)
                    elif kind == "wo":
                        dve.wait_ge(s_tile_hi, n + 1)
                        cols = slice(at * P, (at + 1) * P)
                        for k in range(KD):
                            ins = dve.scalar_tensor_tensor(woT_lo[:, k, cols], bank[:, k, :], g_col[:, k:k + 1],
                                                           woT_hi[:, k, cols], ALU.mult, ALU.subtract)
                        ins.then_inc(s_tile_out, 1)
                for n, (m, pair) in enumerate(KGRP):
                    dve.wait_ge(s_k_hi, n + 1)
                    src = ps[:, n % 4, 0:2 * S].rearrange("p (b s) -> p b s", b=2)
                    dve.tensor_tensor(k16[:, 1, 2 * pair:2 * pair + 2, 0:S], src,
                                      k16[:, 0, 2 * pair:2 * pair + 2, 0:S], ALU.subtract).then_inc(s_k_lo, 1)
                for b in range(BATCH):
                    dve.wait_ge(s_kv, len(KGRP) + b + 1)
                    if b > 0:
                        dve.wait_ge(s_vst, 16 * b)
                    bank = ps[:, b % 2, :]
                    dve.tensor_copy(v_new[:, 0:VM], bank[:, 0:VM]).then_inc(s_vnew, 1)
                    for i in range(UPT):
                        rows = slice(DH * i, DH * i + SR)
                        src = bank[rows, VM:2 * VM].rearrange("p (m e d) -> p m e d", e=2, d=DH)[:, :, i // 2, :]
                        dst = v_new[rows, VM:].rearrange("p (m e d) -> p m e d", e=UPT, d=DH)[:, :, i, :]
                        dve.tensor_copy(dst, src).then_inc(s_vnew, 1)
                dve.wait_ge(s_w1, 16)
                dve.tensor_reduce(wabs[:, 0:1], w1n, AX.XY, ALU.add, apply_absolute_value=True)
                dve.wait_ge(s_w2, 16)
                dve.tensor_reduce(wabs[:, 1:2], w2n, AX.XY, ALU.add, apply_absolute_value=True).then_inc(s_abs, 1)
                dve.wait_ge(s_abssum, 1)
                dve.tensor_scalar(wmean[:], ps[:, 2, 0:2], 1.0 / (HID * D), EPS, ALU.mult, ALU.max).then_inc(s_scale, 1)
                dve.wait_ge(s_scale, 1)
                dve.reciprocal(wscale[:], wmean[:]).then_inc(s_scale, 1)
                dve.wait_ge(s_scale, 2)
                dve.reciprocal(wstep[:], wscale[:]).then_inc(s_scale, 1)
                for n in range(NTERN + 2):
                    if n < NTERN:
                        src, w = natural(n)
                        if n >= 3:
                            dve.wait_ge(s_tern, n - 2)
                        dve.tensor_scalar(signs[:, n % 3, 0, :], src, wscale[:, w:w + 1], 0.5, ALU.mult, ALU.is_gt)
                        dve.tensor_scalar(signs[:, n % 3, 1, :], src, wscale[:, w:w + 1], -0.5, ALU.mult,
                                          ALU.is_lt).then_inc(s_sign, 1)
                    if 1 <= n <= NTERN:
                        dve.wait_ge(s_sign, n)
                        if n >= 3:
                            dve.wait_ge(s_ternT, n - 2)
                        dve.tensor_tensor(tern[:, (n - 1) % 2, :], signs[:, (n - 1) % 3, 0, :],
                                          signs[:, (n - 1) % 3, 1, :], ALU.subtract).then_inc(s_tern, 1)
                    if n >= 2 and n % 2 == 0:
                        dve.wait_ge(s_ternT, n - 1)
                        ternary_out(dve.tensor_copy, n - 2).then_inc(s_ternC[0], 1)
                dve.tensor_copy(b1ln16[:, :, 0], b1ln_col).then_inc(s_b1ln, 1)
                for e, col in ((0, g2_col), (1, b2ln_col)):
                    ins = dve.tensor_copy(ln2_16[:, e, 0, :], col[:])
                ins.then_inc(s_l2, 1)
                dve.wait_ge(s_b1ln, 1)
                dve.tensor_tensor(b1ln16[:, :, 1], b1ln_col, b1ln16[:, :, 0], ALU.subtract).then_inc(s_b1ln, 1)
                dve.wait_ge(s_l2, 1)
                for e, col in ((0, g2_col), (1, b2ln_col)):
                    ins = dve.tensor_tensor(ln2_16[:, e, 1, :], col[:], ln2_16[:, e, 0, :], ALU.subtract)
                ins.then_inc(s_l2, 1)
                dve.wait_ge(s_l2, 2)
                n = 0
                for j in range(JH):
                    for e in range(2):
                        if n >= 2:
                            dve.wait_ge(s_lnrow, n - 1)
                        for h in range(2):
                            ins = dve.tensor_scalar(lnb[:, n % 2, h, :], ones[:], ln2_16[:, e, h, j:j + 1], None, ALU.mult)
                        ins.then_inc(s_lnb, 1)
                        n += 1
                dve.wait_ge(s_lnrow, n)
                dve.tensor_copy(g2_row[:], ps[:, 0, :]).then_inc(s_rows, 1)
                dve.scalar_tensor_tensor(out_const[:], ps[:, 1, :], wstep[:, 1:2], out_const[:], ALU.mult,
                                         ALU.add).then_inc(s_rows, 1)
                dve.wait_ge(s_bias, 1)
                dve.tensor_copy(b2_bcast[:, 0, 0:2 * JH], ps[:, 3, 0:2 * JH]).then_inc(s_bias, 1)
                parts = b2_bcast[:, 0, 0:2 * JH].rearrange("p (j e) -> p j e", e=2)
                dve.wait_ge(s_bias, 2)
                dve.tensor_tensor(b2_bcast[:, 1, 0:JH], parts[:, :, 0], parts[:, :, 1], ALU.add).then_inc(s_bias, 1)
                dve.wait_ge(s_bias, 3)
                dve.scalar_tensor_tensor(bias1, b2_bcast[:, 1, 0:JH], wstep[:, 0:1], bias1, ALU.mult,
                                         ALU.add).then_inc(s_bias, 1)

            def ln1_stats(c):
                wait(dve, s_xin, c, 16, 16)
                for tt in range(TT):
                    ins = dve.bn_stats(stats[:, 0, tt, :], x_in[:, tt, :])
                ins.then_inc(s_st1, 1)
                wait(dve, s_st1, c, 1, 1)
                dve.memset(gate[:], 0.0)
                for tt in range(TT):
                    ins = dve.bn_aggr(mv[:, 0, tt, :], stats[:, 0, tt, :])
                ins.then_inc(s_ag1, 1)
                wait(dve, s_ag1, c, 1, 1)
                dve.tensor_scalar(var[:, 0, :], mv[:, 0, :, 1], EPS, None, ALU.add).then_inc(s_var1, 1)

            def ln1_rows(c, transposed):
                wait(dve, s_rstd1, c, 1, 1)
                if transposed:
                    wait(dve, *transposed)
                for tt in range(TT):
                    dve.tensor_scalar(xhat[:, tt, :], x_in[:, tt, :], mv[:, 0, tt, 0:1], rstd[:, 0, tt:tt + 1],
                                      ALU.subtract, ALU.mult).then_inc(s_xhat1, 1)

            def x_lo(c):
                for tt in range(TT):
                    wait(dve, s_xt_hi, c, TT, tt + 1)
                    cols = slice(tt * P, (tt + 1) * P)
                    dve.tensor_tensor(rows16[:, 1, :, cols], ps[:, B_O + tt % 2, :].rearrange("p (k t) -> p k t", k=KD),
                                      rows16[:, 0, :, cols], ALU.subtract).then_inc(s_xt_lo, 1)

            def q_lo(c, n):
                wait(dve, s_q_hi, c, QM, n + 1)
                dve.scalar_tensor_tensor(q16[:, n % 2, 1, :], ps[:, B_Q, :], 1.0 / WSCALE, q16[:, n % 2, 0, :],
                                         ALU.mult, ALU.subtract).then_inc(s_q_lo, 1)

            def row_max(c, tb):
                tt, b = divmod(tb, TBLK)
                u0, u1 = UPB * b, min(UPB * b + UPB, UNITS)
                wait(dve, s_t, c, NT, tb + 1)
                dve.tensor_reduce(negmax[:, tt, u0:u1],
                                  ps[:, B_O + tb % 2, 0:(u1 - u0) * S].rearrange("p (u s) -> p u s", s=S),
                                  AX.X, ALU.max, negate=True).then_inc(s_tmax, 1)

            def split_maxima(c):
                wait(dve, s_tmax, c, NT, NT)
                wait(dve, s_nmt, c, 1, 0)
                dve.tensor_scalar(negmax16[:, :, 0, :], negmax[:], 1.0 / MSCALE, None, ALU.mult).then_inc(s_nmhi, 1)
                wait(dve, s_nmhi, c, 1, 1)
                dve.scalar_tensor_tensor(negmax16[:, :, 1, :], negmax[:], 1.0 / MSCALE, negmax16[:, :, 0, :],
                                         ALU.mult, ALU.subtract).then_inc(s_nmlo, 1)

            def copy_maxima(c):
                wait(dve, s_nmt, c, 1, 1)
                wait(dve, s_nmst, c, 32, 0)
                dve.tensor_copy(negmaxT[:], ps[0:2 * UNITS, B_O, 0:TB // 2].bitcast(F16)).then_inc(s_nmc, 1)

            def normalise(c, gi):
                mp = gi // 2
                wait(dve, s_pv, c, QM, gi + 1)
                dve.reciprocal(inv_l, ps[:, B_L, :]).then_inc(s_inv, 1)
                wait(dve, s_inv, c, QM, gi + 1)
                if gi % 2 == 0:
                    dve.tensor_tensor(first, ps[:, B_O, :], inv_l, ALU.mult).then_inc(s_ol, 1)
                    return
                dve.tensor_tensor(second, ps[:, B_O, :], inv_l, ALU.mult).then_inc(s_ol, 1)
                wait(dve, s_ol, c, QM, gi + 1)
                if mp >= 2:
                    wait(dve, s_sq, c, KD, mp - 1)
                dve.scalar_tensor_tensor(attn[:, mp % 2, :], second, neglam[:, 0:1], first, ALU.mult,
                                         ALU.add).then_inc(s_att, 1)

            def attn_lo(c, mp):
                wait(dve, s_att_hi, c, KD, mp + 1)
                dve.scalar_tensor_tensor(attn16[:, 1, mp, :], attn[:, mp % 2, :], ASCALE, attn16[:, 0, mp, :],
                                         ALU.mult, ALU.subtract).then_inc(s_att_lo, 1)

            def mid_rows(c):
                wait(dve, s_rms, c, 1, 1)
                dve.tensor_scalar(var[:, 1, :], ps[:, B_Q, 0:TT], 1.0 / D, EPS, ALU.mult, ALU.add).then_inc(s_var2, 1)
                wait(dve, s_rstd2, c, 1, 1)
                dve.tensor_scalar(rms_scale[:], rstd[:, 1, :], (1.0 - LAMBDA_INIT) / (ASCALE * WSCALE), None,
                                  ALU.mult).then_inc(s_rsc, 1)
                wait(dve, s_rsc, c, 1, 1)
                wait(dve, s_xres, c, 16, 16)
                for tt in range(TT):
                    wait(dve, s_wo, c, TT, tt + 1)
                    dve.scalar_tensor_tensor(x_res[:, tt, :], ps[:, tt, :], rms_scale[:, tt:tt + 1], x_res[:, tt, :],
                                             ALU.mult, ALU.add).then_inc(s_mid, 1)
                    wait(dve, s_mid, c, TT, tt + 1)
                    dve.bn_stats(stats[:, 1, tt, :], x_res[:, tt, :]).then_inc(s_st2, 1)
                wait(dve, s_st2, c, TT, TT)
                dve.memset(gate[:], 0.0)
                for tt in range(TT):
                    ins = dve.bn_aggr(mv[:, 1, tt, :], stats[:, 1, tt, :])
                ins.then_inc(s_ag2, 1)
                wait(dve, s_ag2, c, 1, 1)
                dve.tensor_scalar(var[:, 2, :], mv[:, 1, :, 1], 1.0 + EPS, EPS * EPS, ALU.mult, ALU.add).then_inc(s_var3, 1)
                wait(dve, s_rstd3, c, 1, 1)
                for tt in range(TT):
                    dve.tensor_scalar(xhat[:, tt, :], x_res[:, tt, :], mv[:, 1, tt, 0:1], rstd[:, 2, tt:tt + 1],
                                      ALU.subtract, ALU.mult).then_inc(s_xhat2, 1)

            def h_lo(c):
                for k in range(KD):
                    wait(dve, s_ht_hi, c, KD, k + 1)
                    dve.scalar_tensor_tensor(rows16[:, 1, k, :], ps[:, B_H + k, :], g1_col[:, k:k + 1],
                                             rows16[:, 0, k, :], ALU.mult, ALU.subtract).then_inc(s_ht_lo, 1)

            def gelu_lo(c, j):
                wait(dve, s_gg_hi, c, JH, j + 1)
                dve.scalar_tensor_tensor(gg16[:, j % 3, 1, :], gelu_t[:, j % 2, :], g2_col[:, j:j + 1],
                                         gg16[:, j % 3, 0, :], ALU.mult, ALU.subtract).then_inc(s_gg_lo, 1)

            def finish(c):
                G = 4
                wait(dve, s_sums, c, 1, 1)
                dve.tensor_scalar(mean_g[:], ps[:, B_H, 0:TT], 1.0 / HID, None, ALU.mult).then_inc(s_gstep, 1)
                wait(dve, s_gstep, c, G, 1)
                dve.tensor_tensor(meansq_g[:], mean_g[:], mean_g[:], ALU.mult).then_inc(s_gstep, 1)
                wait(dve, s_gstep, c, G, 2)
                dve.scalar_tensor_tensor(var_g[:], ps[:, B_H, TT:2 * TT], 1.0 / HID, meansq_g[:], ALU.mult,
                                         ALU.subtract).then_inc(s_gstep, 1)
                wait(dve, s_gstep, c, G, 3)
                dve.tensor_scalar(var[:, 3, :], var_g[:], EPS, None, ALU.add).then_inc(s_gln, 1)
                wait(dve, s_rstd4, c, 1, 1)
                dve.tensor_scalar(scale_g[:], rstd[:, 3, :], wstep[:, 1:2], None, ALU.mult).then_inc(s_gstep, 1)
                wait(dve, s_gstep, c, G, 4)
                dve.scalar_tensor_tensor(shift_g[:], mean_g[:], -1.0, scale_g[:], ALU.mult, ALU.mult).then_inc(s_gscaled, 1)
                wait(dve, s_gscaled, c, 1, 1)
                wait(dve, s_const, c, 1, 1)
                for tt in range(TT):
                    ins = dve.scalar_tensor_tensor(x_res[:, tt, :], g2_row[:], shift_g[:, tt:tt + 1], x_res[:, tt, :],
                                                   ALU.mult, ALU.add)
                ins.then_inc(s_shift, 1)
                wait(dve, s_shift, c, 1, 1)
                wait(dve, s_f2, c, JH, JH)
                for tt in range(TT):
                    dve.scalar_tensor_tensor(x_res[:, tt, :], ps[:, tt, :], scale_g[:, tt:tt + 1], x_res[:, tt, :],
                                             ALU.mult, ALU.add).then_inc(s_out, 1)

            def iteration(i, ahead, ahead2):
                if ahead:
                    x_lo(i + 1)
                    q_lo(i + 1, 0)
                for gi in range(QM):
                    if gi >= 3 and gi % 2 == 1:
                        attn_lo(i, (gi - 3) // 2)
                    if ahead and gi + 1 < QM:
                        q_lo(i + 1, gi + 1)
                    if gi >= 1:
                        normalise(i, gi - 1)
                normalise(i, QM - 1)
                attn_lo(i, KD - 1)
                mid_rows(i)
                h_lo(i)
                for j in range(JH):
                    if ahead:
                        for tb in range(TSTEP * j, min(TSTEP * (j + 1), NT)):
                            row_max(i + 1, tb)
                        if TSTEP * j >= NT > TSTEP * (j - 1):
                            split_maxima(i + 1)
                        if TSTEP * (j - 1) >= NT > TSTEP * (j - 2):
                            copy_maxima(i + 1)
                    gelu_lo(i, j)
                    if ahead2 and j == 13:
                        ln1_stats(i + 2)
                if ahead2:
                    ln1_rows(i + 2, (s_ht, i, 1, 1))
                finish(i)

            setup()
            ln1_stats(0)
            ln1_rows(0, None)
            x_lo(0)
            for n in range(QM):
                q_lo(0, n)
            ln1_stats(1)
            ln1_rows(1, (s_xt, 0, TT, TT))
            for tb in range(NT):
                row_max(0, tb)
            split_maxima(0)
            copy_maxima(0)
            iteration(0, True, True)
            with dve.Fori(1, NBLK - 2) as i:
                iteration(i, True, True)
            iteration(NBLK - 2, True, False)
            iteration(NBLK - 1, False, False)

        @block.tensor
        def _(pe):
            def setup():
                pe.wait_ge(s_ident, 2)
                pe.wait_ge(s_vec, 16 * NVEC)
                pe.transpose(ps[:, 4, 0:NV], vec_rows, ident[0:NV, 0:NV]).then_inc(s_vect, 1)
                for n, (_, rows, kind, at) in enumerate(tiles):
                    pe.wait_ge(s_stage[n % NSTG], 16 * (n // NSTG + 1))
                    if n >= 4:
                        pe.wait_ge(s_tile_hi, n - 3)
                        lo_read = sum(t[2] in ("wq", "wo") for t in tiles[:n - 3])
                        if lo_read:
                            pe.wait_ge(s_tile_out, lo_read)
                    for k in range(KD):
                        ins = pe.transpose(ps[:, n % 4, k * P:k * P + rows], stage[0:rows, n % NSTG, k * P:(k + 1) * P],
                                           ident[0:rows, 0:rows])
                    ins.then_inc(s_tile, 1)
                pe.wait_ge(s_tile_hi, len(tiles))
                pe.wait_ge(s_tile_out, sum(t[2] in ("wq", "wo") for t in tiles))
                for n, (m, pair) in enumerate(KGRP):
                    if n >= 4:
                        pe.wait_ge(s_k_lo, n - 3)
                    for k in range(KD):
                        ins = pe.matmul(ps[:, n % 4, 0:2 * S], wkT[:, k, m * P:(m + 1) * P],
                                        ctxT[:, k, 2 * pair:2 * pair + 2, :], start=(k == 0), stop=(k == KD - 1))
                    ins.then_inc(s_kv, 1)
                pe.wait_ge(s_k_lo, len(KGRP))
                for b in range(BATCH):
                    if b >= 2:
                        pe.wait_ge(s_vnew, 5 * (b - 1))
                    for k in range(KD):
                        pe.matmul(ps[:, b % 2, 0:VM], ctxT[:, k, b, 0:P], wvT[:, k, :], start=(k == 0), stop=(k == KD - 1))
                    for i in range(UPT):
                        for k in range(KD):
                            ins = pe.matmul(ps[DH * i:DH * i + SR, b % 2, VM:2 * VM], ctxT[:, k, b, P:S], wvT[:, k, :],
                                            start=(k == 0), stop=(k == KD - 1))
                    ins.then_inc(s_kv, 1)
                pe.wait_ge(s_abs, 1)
                pe.matmul(ps[:, 2, 0:2], ones[:], wabs[:], start=True, stop=True).then_inc(s_abssum, 1)
                pe.wait_ge(s_consts, 1)
                for n in range(NTERN):
                    pe.wait_ge(s_tern, n + 1)
                    if n >= 4:
                        pe.wait_ge(s_ternC[n % 2], (n - 4) // 2 + 1)
                    for k in range(KD):
                        ins = pe.transpose(ps[:, 4 + n % 4, 0:TB // 2].bitcast(F16)[:, k * P:(k + 1) * P],
                                           tern[:, n % 2, k * P:(k + 1) * P], ident16[:])
                    ins.then_inc(s_ternT, 1)
                for half in range(2):
                    pe.wait_ge(s_ternC[half], NTERN // 2)
                n = 0
                for j in range(JH):
                    for e in range(2):
                        pe.wait_ge(s_lnb, n + 1)
                        for h in range(2):
                            ins = pe.matmul(ps[:, e, :], lnb[:, n % 2, h, :], w2T[:, j, :], start=(j == 0 and h == 0),
                                            stop=(j == JH - 1 and h == 1))
                        ins.then_inc(s_lnrow, 1)
                        n += 1
                pe.wait_ge(s_b1ln, 2)
                for j in range(JH):
                    for k in range(KD):
                        ins = pe.matmul(ps[:, 3, 2 * j:2 * j + 2], w1T[:, k, j * P:(j + 1) * P], b1ln16[:, k, :],
                                        start=(k == 0), stop=(k == KD - 1))
                ins.then_inc(s_bias, 1)
                pe.wait_ge(s_bias, 4)
                pe.wait_ge(s_rows, 2)

            def split_product(dst, w_hi, w_lo, r_hi, r_lo, first, last):
                pe.matmul(dst, w_hi, r_hi, start=first, stop=False)
                pe.matmul(dst, w_hi, r_lo, start=False, stop=False)
                return pe.matmul(dst, w_lo, r_hi, start=False, stop=last)

            def x_transposes(c):
                wait(pe, s_nmc, c, 1, 0)
                for tt in range(TT):
                    wait(pe, s_xhat1, c, TT, tt + 1)
                    if tt >= 2:
                        wait(pe, s_xt_lo, c, TT, tt - 1)
                    for k in range(KD):
                        ins = pe.transpose(ps[:, B_O + tt % 2, k * P:(k + 1) * P], xhat[:, tt, k * P:(k + 1) * P], ident[:])
                    ins.then_inc(s_xt, 1)

            def queries(c, n):
                m = ORDER[n]
                wait(pe, s_xt_lo, c, TT, TT)
                wait(pe, s_q_lo, c, QM, n)
                for k in range(KD):
                    cols = slice(m * P, (m + 1) * P)
                    ins = split_product(ps[:, B_Q, :], wqT_hi[:, k, cols], wqT_lo[:, k, cols], rows16[:, 0, k, :],
                                        rows16[:, 1, k, :], k == 0, k == KD - 1)
                ins.then_inc(s_q, 1)

            def row_scores(c, tb):
                tt, b = divmod(tb, TBLK)
                if tb == 0:
                    for half in range(2):
                        wait(pe, s_qst[half], c, QDMA * QM // 2, QDMA * QM // 2)
                    wait(pe, s_kmax, c, 16, 16)
                if tb >= 2:
                    wait(pe, s_tmax, c, NT, tb - 1)
                for w, u in enumerate(range(UPB * b, min(UPB * b + UPB, UNITS))):
                    ins = pe.matmul(ps[:, B_O + tb % 2, w * S:(w + 1) * S], stack[0:STK, u, tt * P:(tt + 1) * P],
                                    k_max[0:STK, key_unit(u), 0:S], start=True, stop=True)
                ins.then_inc(s_t, 1)

            def transpose_maxima(c):
                wait(pe, s_nmlo, c, 1, 1)
                for tt in range(TT):
                    ins = pe.transpose(ps[:, B_O, 0:TB // 2].bitcast(F16)[:, tt * P:(tt + 1) * P],
                                       negmax16[:, tt, :, :].rearrange("p e u -> p (e u)"), ident16[:])
                ins.then_inc(s_nmt, 1)

            def scores(c, gi):
                if gi == 0:
                    wait(pe, s_nmst, c, 32, 32)
                    wait(pe, s_katt, c, 16, 16)
                    wait(pe, s_out, c, TT, 0)
                else:
                    wait(pe, s_p, c, 2 * QM, 2 * gi)
                for i in range(UPT):
                    u = UPT * ORDER[gi] + i
                    ins = pe.matmul(ps[:, i, :], k_att[0:STKM, key_unit(u), 0:P], stack[0:STKM, u, :], start=True, stop=True)
                    if i == 1:
                        ins.then_inc(s_s, 1)
                for i in range(UPT):
                    u = UPT * ORDER[gi] + i
                    ins = pe.matmul(ps[DH * i:DH * i + DH, B_SREST, :], k_att[0:STKM, key_unit(u), P:SPAD],
                                    stack[0:STKM, u, :], start=True, stop=True)
                ins.then_inc(s_s, 1)

            def values(c, gi):
                m, buf = ORDER[gi] % (QM // 2), gi % 2
                wait(pe, s_p, c, 2 * QM, 2 * gi + 2)
                if gi == 0:
                    wait(pe, s_vatt, c, 16, 16)
                else:
                    wait(pe, s_ol, c, QM, gi)
                for i in range(UPT):
                    kv = (UPT * m + i) // (H // KV)
                    pe.matmul(ps[DH * i:DH * i + DH, B_O, :], v_att[:, kv * DH:(kv + 1) * DH], probs[:, buf, i, :],
                              start=True, stop=False)
                pe.matmul(ps[:, B_O, :], v_att[:, VM + m * P:VM + (m + 1) * P], probs[:, buf, 4, :], start=False, stop=True)
                for i in range(UPT):
                    pe.matmul(ps[DH * i:DH * i + DH, B_L, :], ones[:, 0:DH], probs[:, buf, i, :], start=True, stop=False)
                pe.matmul(ps[:, B_L, :], ones_rest[:], probs[:, buf, 4, :], start=False, stop=True).then_inc(s_pv, 1)

            def rms_sums(c, ahead):
                wait(pe, s_sqsum, c, KD - 1, KD - 1)
                if ahead:
                    wait(pe, s_q_lo, c + 1, QM, QM)
                for tt in range(TT):
                    ins = pe.matmul(ps[:, B_Q, tt:tt + 1], sq_acc[:, tt * P:(tt + 1) * P], ones[:, 0:1], start=True, stop=True)
                ins.then_inc(s_rms, 1)

            def out_projection(c):
                wait(pe, s_att_lo, c, KD, KD)
                for tt in range(TT):
                    cols = slice(tt * P, (tt + 1) * P)
                    for k in range(KD):
                        ins = split_product(ps[:, tt, :], attn16[:, 0, k, cols], attn16[:, 1, k, cols], woT_hi[:, k, :],
                                            woT_lo[:, k, :], k == 0, k == KD - 1)
                    ins.then_inc(s_wo, 1)

            def h_transposes(c):
                for tt in range(TT):
                    wait(pe, s_xhat2, c, TT, tt + 1)
                    for k in range(KD):
                        ins = pe.transpose(ps[:, B_H + k, tt * P:(tt + 1) * P], xhat[:, tt, k * P:(k + 1) * P], ident[:])
                ins.then_inc(s_ht, 1)

            def hidden(c, j):
                if j == 0:
                    wait(pe, s_ht_lo, c, KD, KD)
                if j >= 2:
                    wait(pe, s_gelu, c, JH, j - 1)
                for k in range(KD):
                    for e in range(2):
                        ins = pe.matmul(ps[:, B_H + j % 2, :], w1T[:, k, j * P:(j + 1) * P], rows16[:, e, k, :],
                                        start=(k == 0 and e == 0), stop=(k == KD - 1 and e == 1))
                ins.then_inc(s_f1, 1)

            def ffn_out(c, j):
                wait(pe, s_gg_lo, c, JH, j + 1)
                for tt in range(TT):
                    for e in range(2):
                        ins = pe.matmul(ps[:, tt, :], gg16[:, j % 3, e, tt * P:(tt + 1) * P], w2T[:, j, :],
                                        start=(j == 0 and e == 0), stop=(j == JH - 1 and e == 1))
                ins.then_inc(s_f2, 1)

            def gelu_sums(c):
                wait(pe, s_acc, c, JH - 1, JH - 1)
                for e in range(2):
                    for tt in range(TT):
                        ins = pe.matmul(ps[:, B_H, e * TT + tt:e * TT + tt + 1], acc[:, e, tt * P:(tt + 1) * P],
                                        ones[:, 0:1], start=True, stop=True)
                ins.then_inc(s_sums, 1)

            def iteration(i, ahead):
                if ahead:
                    x_transposes(i + 1)
                    queries(i + 1, 0)
                for gi in range(QM):
                    scores(i, gi)
                    if ahead and gi + 1 < QM:
                        queries(i + 1, gi + 1)
                    if gi >= 1:
                        values(i, gi - 1)
                values(i, QM - 1)
                rms_sums(i, ahead)
                out_projection(i)
                h_transposes(i)
                for j in range(JH):
                    hidden(i, j)
                    if ahead:
                        for tb in range(TSTEP * j, min(TSTEP * (j + 1), NT)):
                            row_scores(i + 1, tb)
                        if TSTEP * (j - 1) >= NT > TSTEP * (j - 2):
                            transpose_maxima(i + 1)
                    if j >= 2:
                        ffn_out(i, j - 2)
                ffn_out(i, JH - 2)
                ffn_out(i, JH - 1)
                gelu_sums(i)

            setup()
            x_transposes(0)
            for n in range(QM):
                queries(0, n)
            for tb in range(NT):
                row_scores(0, tb)
            transpose_maxima(0)
            iteration(0, True)
            with pe.Fori(1, NBLK - 2) as i:
                iteration(i, True)
            iteration(NBLK - 2, True)
            iteration(NBLK - 1, False)

    return nc


_INS = ["x", "ctx_1024", "L0_xattn_Wq", "L0_xattn_Wk", "L0_xattn_Wv", "L0_xattn_Wo", "L0_xattn_lam", "L0_xattn_g",
        "L0_ffn_ln1_g", "L0_ffn_ln1_b", "L0_ffn_w1", "L0_ffn_b1", "L0_ffn_ln2_g", "L0_ffn_ln2_b", "L0_ffn_w2",
        "L0_ffn_b2"]


def kernel(**inputs):
    import numpy as np
    import concourse.bacc as bacc
    from concourse.bass_utils import run_bass_kernel_spmd

    nc = bacc.Bacc("TRN2", target_bir_lowering=False, num_devices=1)
    arrays, args = {}, []
    for name in _INS:
        a = np.ascontiguousarray(inputs[name])
        if a.ndim == 0:
            a = a.reshape(1)
        arrays[f"in_{name}"] = a
        args.append(nc.dram_tensor(f"in_{name}", a.shape, mybir.dt.from_np(a.dtype), kind="ExternalInput").ap())
    out = nc.dram_tensor("out", (BATCH, T, D), F32, kind="ExternalOutput").ap()
    build(nc, *args, out)
    return run_bass_kernel_spmd(nc, [arrays], core_ids=[0]).results[0]["out"]
```

```python
import math
from contextlib import ExitStack

import concourse.bass as bass
from concourse import mybir

F32 = mybir.dt.float32
F16 = mybir.dt.float16
ALU = mybir.AluOpType
ACT = mybir.ActivationFunctionType
AX = mybir.AxisListType

P = 128
D = 512
KD = D // P
BATCH, T, S = 4, 2048, 154
H, KV, DH = 16, 8, 32
HID = 2048
JH = HID // P
TB = 512
TT = TB // P
NBLK = BATCH * T // TB
BLK_PER_BATCH = T // TB
UNITS = 2 * H
KUNITS = 2 * KV
QM = UNITS * DH // P
UPT = P // DH
SR = S - P
SPAD = P + DH
STK = 3 * DH
STKM = STK + 2
MSCALE = 64.0
WSCALE = 256.0
ASCALE = 16.0
EPS = 1e-5
LAMBDA_INIT = 0.8 - 0.6 * math.exp(-0.3 * 12)
UPB = 3
TBLK = -(-UNITS // UPB)
NT = TT * TBLK
TSTEP = 4
ORDER = [m for p in range(QM // 2) for m in (p, p + QM // 2)]
STEPS = [(w[0], int(w[1])) for w in (
    "q0 s0 q1 s1 v0 s2 v1 s3 v2 q2 a0 s4 v3 l0 s5 v4 q3 l1 a1 s6 v5 s7 v6 q4 a2 v7 a3").split()]
QLATE = 5
TFIRST = 1
TLAST = TFIRST + -(-NT // TSTEP) - 1
PAIR = 2 * UPT
QDMA = 3 * UPT * 16


def key_unit(slot):
    u = UPT * ORDER[slot // UPT] + slot % UPT
    return u // H * KV + (u % H) // (H // KV)


def maxima_beside(j):
    first = TSTEP * (j - TFIRST)
    return list(range(max(first, 0), max(min(first + TSTEP, NT), 0)))


def wait(eng, sem, c, per, k):
    if isinstance(c, int) and c * per + k <= 0:
        return
    eng.wait_ge(sem, c * per + k)


def build(nc, x, ctx, wq, wk, wv, wo, lam, g, ln1_g, ln1_b, w1, b1, ln2_g, ln2_b, w2, b2, out):
    x_blk = x.rearrange("b t d -> (b t) d").rearrange("(c s p) d -> c p s d", s=TT, p=P)
    out_blk = out.rearrange("b t d -> (b t) d").rearrange("(c s p) d -> c p s d", s=TT, p=P)
    k_store = nc.dram_tensor("k_store", (BATCH, STKM, KUNITS, SPAD), F16, kind="Internal").ap()
    v_store = nc.dram_tensor("v_store", (BATCH, P, KV * DH + QM // 2 * P), F32, kind="Internal").ap()
    VM = KV * DH

    with ExitStack() as es:
        def sb(name, shape, dt):
            return es.enter_context(nc.sbuf_tensor(name, shape, dt))

        def sem(name):
            return es.enter_context(nc.semaphore(name))

        ps = es.enter_context(nc.psum_tensor("ps", [P, 8, 512], F32))
        B_SREST, B_Q, B_O, B_L = 4, 5, 6, 7
        B_H = 4

        wqT_hi, wqT_lo = sb("wqT_hi", [P, KD, 2 * H * DH], F16), sb("wqT_lo", [P, KD, 2 * H * DH], F16)
        woT_hi, woT_lo = sb("woT_hi", [P, KD, D], F16), sb("woT_lo", [P, KD, D], F16)
        w1T, w2T = sb("w1T", [P, KD, HID], F16), sb("w2T", [P, JH, D], F16)
        ident, ident16 = sb("ident", [P, P], F32), sb("ident16", [P, P], F16)
        ones, ones_rest = sb("ones", [P, P], F32), sb("ones_rest", [P, P], F32)
        neghalf = sb("neghalf", [P, TT], F32)
        neglam = sb("neglam", [P, 1], F32)
        vec_src = [(b1, JH), (ln2_g, JH), (ln2_b, JH), (g, KD), (ln1_g, KD), (ln1_b, KD)]
        NV = sum(n for _, n in vec_src)
        vec_cols = sb("vec_cols", [P, NV], F32)
        vec_at = [sum(n for _, n in vec_src[:i]) for i in range(len(vec_src))]
        bias1, g2_col, b2ln_col, g_col, g1_col, b1ln_col = (
            vec_cols[:, at:at + n] for at, (_, n) in zip(vec_at, vec_src))
        wabs, wmean = sb("wabs", [P, 2], F32), sb("wmean", [P, 2], F32)
        wscale, wstep = sb("wscale", [P, 2], F32), sb("wstep", [P, 2], F32)
        b1ln16 = sb("b1ln16", [P, KD, 2], F16)
        g2_row, out_const = sb("g2_row", [P, D], F32), sb("out_const", [P, D], F32)
        k_max, k_att = sb("k_max", [P, KUNITS, SPAD], F16), sb("k_att", [P, KUNITS, SPAD], F16)
        v_att = sb("v_att", [P, VM + QM // 2 * P], F32)
        stack_raw = sb("stack_raw", [P, UNITS * TB // 2], F32)
        stack = stack_raw[:].bitcast(F16).rearrange("p (u t) -> p u t", u=UNITS)
        ctxT = stack_raw[:, 0:KD * BATCH * S].rearrange("p (k b s) -> p k b s", k=KD, b=BATCH)
        o1 = KD * BATCH * S
        wkT = stack_raw[:, o1:o1 + KD * D].rearrange("p (k n) -> p k n", k=KD)
        wvT = stack_raw[:, o1 + KD * D:o1 + KD * (D + VM)].rearrange("p (k n) -> p k n", k=KD)
        o2 = o1 + KD * (D + VM)
        NSTG = 4
        stage = stack_raw[:, o2:o2 + NSTG * D].rearrange("p (n d) -> p n d", n=NSTG)
        arena = sb("arena", [P, 2 * HID * D // P], F32)
        w1n = arena[:, 0:JH * D].rearrange("p (r d) -> p r d", r=JH)
        w2n = arena[:, JH * D:2 * JH * D].rearrange("p (r h) -> p r h", r=KD)
        cut = [0]

        def part(words):
            cut[0] += words
            assert cut[0] <= 2 * HID * D // P
            return arena[:, cut[0] - words:cut[0]]

        x_in = part(TT * D).rearrange("p (s d) -> p s d", s=TT)
        x_res = part(TT * D).rearrange("p (s d) -> p s d", s=TT)
        xhat = part(TT * D).rearrange("p (s d) -> p s d", s=TT)
        probs_words = 2 * 5 * TB
        probs_raw = part(probs_words)
        probs = probs_raw.rearrange("p (b n t) -> p b n t", b=2, n=5)
        gelu_t = probs_raw[:, 0:2 * TB].rearrange("p (b t) -> p b t", b=2)
        gsq_t = probs_raw[:, 2 * TB:4 * TB].rearrange("p (b t) -> p b t", b=2)
        gg16 = probs_raw[:, 4 * TB:7 * TB].bitcast(F16).rearrange("p (b e t) -> p b e t", b=3, e=2)
        acc = probs_raw[:, 7 * TB:9 * TB].rearrange("p (e t) -> p e t", e=2)
        attn16 = part(KD * TB).bitcast(F16).rearrange("p (e k t) -> p e k t", e=2, k=KD)
        q32 = part(2 * TB).rearrange("p (b t) -> p b t", b=2)
        xrows16 = part(KD * TB).bitcast(F16).rearrange("p (e k t) -> p e k t", e=2, k=KD)
        rows16 = sb("rows16", [P, 2, KD, TB], F16)
        q16 = sb("q16", [P, 2, 2, TB], F16)
        q_pair = [rows16[:, 0, :, :].rearrange("p (n e) t -> p n e t", e=2), q16]
        attn_raw = sb("attn_raw", [P, 9 * TB], F32)
        attn = attn_raw[:, 0:2 * TB].rearrange("p (b t) -> p b t", b=2)
        attn_sq = attn_raw[:, 2 * TB:4 * TB].rearrange("p (b t) -> p b t", b=2)
        o_first, l_first, cross_a, cross_b, l_prod = (attn_raw[:, n * TB:(n + 1) * TB] for n in range(4, 9))
        sq_acc = sb("sq_acc", [P, TB], F32)
        signs = attn_raw[:, 0:3 * TB].bitcast(F16).rearrange("p (n e t) -> p n e t", n=3, e=2)
        tern = attn_raw[:, 3 * TB:4 * TB].bitcast(F16).rearrange("p (n t) -> p n t", n=2)
        k16 = rows16[:].rearrange("p e k t -> p (e k t)")[:, 0:2 * BATCH * SPAD].rearrange(
            "p (e b s) -> p e b s", e=2, b=BATCH)
        vec_rows = sq_acc[0:NV, 0:P]
        v_new = attn_raw[:, 4 * TB:4 * TB + VM + QM // 2 * P]
        b2_bcast = q16[:].rearrange("p a b t -> p (a b t)").bitcast(F32)[:, 0:2 * D].rearrange("p (e d) -> p e d", e=2)
        krows = k_att[0:2]
        ln2_16 = sb("ln2_16", [P, 2, 2, JH], F16)
        lnb = sb("lnb", [P, 2, 2, P], F16)
        negmax = sb("negmax", [P, TT, UNITS], F32)
        negmax16 = sb("negmax16", [P, TT, P // UNITS, UNITS], F16)
        negmaxT = sb("negmaxT", [2 * UNITS, TB], F16)
        stats = sb("stats", [P, 2, TT, 6], F32)
        gate = sb("gate", [P, 1], F32)
        mv = sb("mv", [P, 2, TT, 2], F32)
        var = sb("var", [P, 4, TT], F32)
        rstd = sb("rstd", [P, 4, TT], F32)
        rms_scale = sb("rms_scale", [P, TT], F32)
        mean_g, meansq_g, var_g = sb("mean_g", [P, TT], F32), sb("meansq_g", [P, TT], F32), sb("var_g", [P, TT], F32)
        scale_g, shift_g = sb("scale_g", [P, TT], F32), sb("shift_g", [P, TT], F32)

        s_ident0, s_ident, s_consts = sem("ident_zero"), sem("ident_ready"), sem("consts_ready")
        s_vec, s_vect, s_vecc = sem("vectors_loaded"), sem("vectors_transposed"), sem("vectors_copied")
        s_w1, s_w2 = sem("w1_loaded"), sem("w2_loaded")
        s_stage = [sem(f"stage_loaded{n}") for n in range(NSTG)]
        s_tile, s_tile_hi, s_tile_out = sem("tile_transposed"), sem("tile_hi"), sem("tile_out")
        s_gcol = sem("g_scaled")
        s_kv, s_k_hi, s_k_lo = sem("kv_product"), sem("k_hi"), sem("k_lo")
        s_kst, s_vst, s_vnew = sem("k_stored"), sem("v_stored"), sem("v_new")
        s_krows, s_v0 = sem("key_rows"), sem("v_cleared")
        s_abs, s_abssum, s_scale = sem("abs_summed"), sem("abs_total"), sem("scale_step")
        s_sign, s_tern, s_ternT = sem("sign_ready"), sem("ternary_ready"), sem("ternary_transposed")
        s_ternC = [sem("ternary_copied_even"), sem("ternary_copied_odd")]
        s_b1ln, s_l2, s_lnb, s_lnrow, s_bias, s_rows = (sem(n) for n in (
            "b1ln_split", "ln2_split", "ln2_spread", "ln2_product", "bias_ready", "rows_ready"))
        s_xin, s_xres, s_kmax, s_katt, s_vatt = (sem(n) for n in (
            "x_in_loaded", "x_res_loaded", "k_max_loaded", "k_att_loaded", "v_att_loaded"))
        s_st1, s_ag1, s_var1, s_rstd1, s_xhat1 = (sem(n) for n in (
            "ln1_stats", "ln1_aggr", "ln1_var", "ln1_rstd", "ln1_rows"))
        s_xt, s_xt_hi, s_xt_lo = sem("x_transposed"), sem("x_hi"), sem("x_lo")
        s_q, s_q_hi, s_q_lo = sem("q_product"), sem("q_hi"), sem("q_lo")
        s_pair_seen = sem("q_pair_seen")
        s_qst = [sem("even_pair_stacked"), sem("odd_pair_stacked")]
        s_t, s_tmax, s_nmhi, s_nmlo, s_nmt, s_nmc, s_nmst = (sem(n) for n in (
            "row_scores", "row_max", "negmax_hi", "negmax_lo", "negmax_transposed", "negmax_copied", "negmax_stacked"))
        s_s, s_p, s_pv, s_ol1, s_o2, s_ol2, s_inv, s_att = (sem(n) for n in (
            "scores", "probs", "values_done", "first_copied", "second_values_read", "second_read", "inverse_sum", "attn_ready"))
        s_q32, s_y, s_diff = sem("q_copied"), sem("ffn_out_read"), sem("attn_unscaled")
        s_att_hi, s_att_lo, s_sq, s_sqsum = sem("attn_hi"), sem("attn_lo"), sem("attn_square"), sem("attn_square_sum")
        s_rms, s_var2, s_rstd2, s_rsc = sem("rms_sum"), sem("rms_var"), sem("rms_rstd"), sem("rms_scaled")
        s_wo, s_mid, s_st2, s_ag2, s_var3, s_rstd3, s_xhat2 = (sem(n) for n in (
            "out_projected", "mid_ready", "ln2_stats", "ln2_aggr", "ln2_var", "ln2_rstd", "ln2_rows"))
        s_ht, s_ht_hi, s_ht_lo = sem("h_transposed"), sem("h_hi"), sem("h_lo")
        s_f1, s_gelu, s_gsq, s_gg_hi, s_gg_lo, s_acc = (sem(n) for n in (
            "hidden", "gelu", "gelu_square", "gelu_hi", "gelu_lo", "gelu_summed"))
        s_f2, s_sums, s_gln, s_rstd4, s_const, s_out, s_stored = (sem(n) for n in (
            "ffn_out", "gelu_sums", "gelu_ln_step", "gelu_rstd", "const_added", "out_ready", "out_stored"))
        s_gstep, s_gscaled, s_shift = sem("gelu_ln_small_step"), sem("gelu_ln_scaled"), sem("shift_added")

        tiles = [(ctx[b, r:r + n, :], n, "ctx", (b, r)) for b in range(BATCH) for r, n in ((0, P), (P, SR))]
        tiles += [(wk[r * P:(r + 1) * P, :], P, "wk", r) for r in range(D // P)]
        tiles += [(wv[r * P:(r + 1) * P, :], P, "wv", r) for r in range(VM // P)]
        tiles += [(wq[r * P:(r + 1) * P, :], P, "wq", r) for r in range(QM)]
        tiles += [(wo[r * P:(r + 1) * P, :], P, "wo", r) for r in range(KD)]
        N_KV_TILES = 2 * BATCH + D // P + VM // P
        KGRP = [(m, pair) for m in range(KUNITS * DH // P) for pair in range(BATCH // 2)]
        NTERN = 2 * JH
        NVEC = len(vec_src) + 2

        def ternary_out(copy, n):
            src = ps[:, 4 + n % 4, 0:TB // 2].bitcast(F16).rearrange("p (k r) -> p k r", k=KD)
            if n < JH:
                return copy(w1T[:, :, n * P:(n + 1) * P], src)
            r, q = divmod(n - JH, KD)
            return copy(w2T[:, KD * q:KD * q + KD, r * P:(r + 1) * P], src)

        def natural(n):
            if n < JH:
                return w1n[:, n, :], 0
            r, q = divmod(n - JH, KD)
            return w2n[:, r, q * D:(q + 1) * D], 1

        block = es.enter_context(nc.Block())

        @block.sync
        def _(sp):
            def setup():
                for n, (src, rows, _, _) in enumerate(tiles):
                    if n >= NSTG:
                        sp.wait_ge(s_tile, n - NSTG + 1)
                    sp.dma_start(stage[0:rows, n % NSTG, :], src).then_inc(s_stage[n % NSTG], 16)
                    if n == 3:
                        for at, (src, n_rows) in zip(vec_at, vec_src):
                            sp.dma_start(vec_rows[at:at + n_rows, :], src.rearrange("(k p) -> k p", p=P)).then_inc(s_vec, 16)
                        sp.dma_start(neglam[:], lam.rearrange("(a b) -> a b", a=1).broadcast_to([P, 1])).then_inc(s_vec, 16)
                        sp.dma_start(out_const[:], b2.rearrange("(a d) -> a d", a=1).broadcast_to([P, D])).then_inc(s_vec, 16)
                    if n == N_KV_TILES - 1:
                        sp.dma_start(w1n, w1.rearrange("(r p) d -> p r d", p=P)).then_inc(s_w1, 16)
                        sp.dma_start(w2n, w2.rearrange("(r p) h -> p r h", p=P)).then_inc(s_w2, 16)
                sp.wait_ge(s_krows, 2)
                for b in range(BATCH):
                    sp.dma_start(k_store[b, STK:STKM, :, :], krows).then_inc(s_kst, 16)
                for m in range(KUNITS // UPT):
                    sp.wait_ge(s_k_lo, 2 * m + 2)
                    for b in range(BATCH):
                        for c3, e in enumerate((0, 0, 1)):
                            dst = k_store[b, DH * c3:DH * c3 + DH, UPT * m:UPT * m + UPT, :]
                            sp.dma_start(dst.rearrange("d u s -> u d s"), k16[:, e, b, :]).then_inc(s_kst, 16)
                for b in range(BATCH):
                    sp.wait_ge(s_vnew, 5 * b + 5)
                    sp.dma_start(v_store[b], v_new).then_inc(s_vst, 16)
                sp.wait_ge(s_kst, 16 * BATCH * (1 + 3 * KUNITS // UPT))
                sp.wait_ge(s_vst, 16 * BATCH)

            def batch_of(c):
                return c // BLK_PER_BATCH if isinstance(c, int) else sp.snap(c // BLK_PER_BATCH)

            def load_k_max(c, b):
                wait(sp, s_t, c, NT, 0)
                sp.dma_start(k_max[0:STKM], k_store[b]).then_inc(s_kmax, 16)

            def load_kv_att(c, b):
                wait(sp, s_pv, c, QM, 0)
                sp.dma_start(k_att[0:STKM], k_store[b]).then_inc(s_katt, 16)
                sp.dma_start(v_att[:], v_store[b]).then_inc(s_vatt, 16)

            def load_x_in(c):
                wait(sp, s_xt, c, TT, 0)
                sp.dma_start(x_in, x_blk[c]).then_inc(s_xin, 16)

            def load_x_res(c):
                wait(sp, s_stored, c, 16 * TT, 0)
                sp.dma_start(x_res, x_blk[c]).then_inc(s_xres, 16)

            def stack_queries(c, p, before):
                wait(sp, s_q_lo, c, QM, 2 * p + 2)
                if before is not None:
                    sp.sem_inc(s_pair_seen, 1)
                    wait(sp, s_s, before, 2 * QM, 4 * p + 4)
                for i in range(UPT):
                    slots = stack[:, PAIR * p:PAIR * (p + 1), :].rearrange("p (n i) t -> p n i t", n=2)
                    for c3, e in enumerate((0, 1, 0)):
                        sp.dma_start(slots[DH * c3:DH * c3 + DH, :, i, :],
                                     q_pair[p % 2][DH * i:DH * i + DH, :, e, :]).then_inc(s_qst[p % 2], 16)

            def stack_maxima(c):
                wait(sp, s_nmc, c, 1, 1)
                for e in range(2):
                    sp.dma_start(stack[STK + e:STK + e + 1, :, :],
                                 negmaxT[UNITS * e:UNITS * (e + 1), :]).then_inc(s_nmst, 16)

            def store(c):
                for tt in range(TT):
                    wait(sp, s_out, c, TT, tt + 1)
                    sp.dma_start(out_blk[c][:, tt, :], x_res[:, tt, :]).then_inc(s_stored, 16)

            def iteration(i, ahead, ahead2):
                if ahead:
                    b = batch_of(i + 1)
                    load_k_max(i + 1, b)
                if ahead2:
                    load_x_in(i + 2)
                if ahead:
                    for p in range(QLATE // 2):
                        stack_queries(i + 1, p, i)
                load_x_res(i)
                if ahead:
                    for p in range(QLATE // 2, QM // 2):
                        stack_queries(i + 1, p, i)
                    load_kv_att(i + 1, b)
                    stack_maxima(i + 1)
                store(i)

            setup()
            sp.wait_ge(s_tern, NTERN)
            sp.wait_ge(s_rows, 2)
            load_x_in(0)
            load_k_max(0, 0)
            load_kv_att(0, 0)
            load_x_in(1)
            for p in range(QM // 2):
                stack_queries(0, p, None)
            stack_maxima(0)
            iteration(0, True, True)
            with sp.Fori(1, NBLK - 2) as i:
                iteration(i, True, True)
            iteration(NBLK - 2, True, False)
            iteration(NBLK - 1, False, False)
            sp.wait_ge(s_stored, NBLK * 16 * TT)

        @block.gpsimd
        def _(pool):
            def setup():
                pool.memset(ident[:], 0.0).then_inc(s_ident0, 1)
                pool.wait_ge(s_ident0, 1)
                pool.affine_select(out=ident[:], in_=ident[:], compare_op=ALU.not_equal, fill=1.0, base=0,
                                   pattern=[[-1, P]], channel_multiplier=1).then_inc(s_ident, 1)
                pool.memset(neghalf[:], -0.5).then_inc(s_ident, 1)
                pool.wait_ge(s_ident, 2)

            def power(slot, ready, done, c):
                wait(pool, ready, c, 1, 1)
                pool.tensor_tensor(rstd[:, slot, :], var[:, slot, :], neghalf[:], ALU.pow).then_inc(done, 1)

            def q_lo(c, n):
                wait(pool, s_q_hi, c, QM, n + 1)
                pair = q_pair[n // 2 % 2]
                pool.tensor_tensor(pair[:, n % 2, 1, :], q32[:, n % 2, :], pair[:, n % 2, 0, :],
                                   ALU.subtract).then_inc(s_q_lo, 1)

            def sum_squares(c, mp):
                if mp == 0:
                    return
                wait(pool, s_sq, c, KD, mp + 1)
                if mp == 1:
                    wait(pool, s_rms, c, 1, 0)
                    pool.tensor_tensor(sq_acc[:], attn_sq[:, 0, :], attn_sq[:, 1, :], ALU.add).then_inc(s_sqsum, 1)
                else:
                    wait(pool, s_sqsum, c, KD - 1, mp - 1)
                    pool.tensor_tensor(sq_acc[:], sq_acc[:], attn_sq[:, mp % 2, :], ALU.add).then_inc(s_sqsum, 1)

            def add_constant(c):
                wait(pool, s_xhat2, c, TT, TT)
                for tt in range(TT):
                    ins = pool.tensor_tensor(x_res[:, tt, :], x_res[:, tt, :], out_const[:], ALU.add)
                ins.then_inc(s_const, 1)

            def sum_gelu(c, j):
                wait(pool, s_gsq, c, JH, j + 1)
                if j == 1:
                    wait(pool, s_sums, c, 1, 0)
                    for e, src in ((0, gelu_t), (1, gsq_t)):
                        ins = pool.tensor_tensor(acc[:, e, :], src[:, 0, :], src[:, 1, :], ALU.add)
                else:
                    wait(pool, s_acc, c, JH - 1, j - 1)
                    for e, src in ((0, gelu_t), (1, gsq_t)):
                        ins = pool.tensor_tensor(acc[:, e, :], acc[:, e, :], src[:, j % 2, :], ALU.add)
                ins.then_inc(s_acc, 1)

            def iteration(i, ahead, ahead2):
                for what, n in STEPS:
                    if what == "q" and ahead:
                        q_lo(i + 1, n)
                    elif what == "a":
                        sum_squares(i, n)
                    elif what == "l" and n == 0 and ahead2:
                        power(0, s_var1, s_rstd1, i + 2)
                power(1, s_var2, s_rstd2, i)
                if ahead:
                    q_lo(i + 1, QLATE)
                power(2, s_var3, s_rstd3, i)
                if ahead:
                    for n in range(QLATE + 1, QM):
                        q_lo(i + 1, n)
                add_constant(i)
                for j in range(1, JH):
                    sum_gelu(i, j)
                power(3, s_gln, s_rstd4, i)

            setup()
            power(0, s_var1, s_rstd1, 0)
            for n in range(QM):
                q_lo(0, n)
            power(0, s_var1, s_rstd1, 1)
            iteration(0, True, True)
            with pool.Fori(1, NBLK - 2) as i:
                iteration(i, True, True)
            iteration(NBLK - 2, True, False)
            iteration(NBLK - 1, False, False)

        @block.scalar
        def _(act):
            def setup():
                act.wait_ge(s_gcol, 1)
                for n, (_, rows, kind, at) in enumerate(tiles):
                    act.wait_ge(s_tile, n + 1)
                    bank = ps[:, n % 4, :].rearrange("p (k r) -> p k r", k=KD)
                    if kind == "ctx":
                        b, r = at
                        act.copy(ctxT[:, :, b, r:r + rows], bank[:, :, 0:rows]).then_inc(s_tile_hi, 1)
                    elif kind in ("wk", "wv"):
                        dst = wkT if kind == "wk" else wvT
                        act.copy(dst[:, :, at * P:(at + 1) * P], bank).then_inc(s_tile_hi, 1)
                    elif kind == "wq":
                        act.mul(wqT_hi[:, :, at * P:(at + 1) * P], bank, WSCALE).then_inc(s_tile_hi, 1)
                    else:
                        for k in range(KD):
                            ins = act.activation(woT_hi[:, k, at * P:(at + 1) * P], bank[:, k, :], ACT.Identity,
                                                 scale=g_col[:, k:k + 1])
                        ins.then_inc(s_tile_hi, 1)
                for n, (m, pair) in enumerate(KGRP):
                    act.wait_ge(s_kv, n + 1)
                    if pair == 0 and m > 0:
                        act.wait_ge(s_kst, 16 * BATCH * (1 + 3 * m))
                    if n == 0:
                        act.wait_ge(s_v0, 1)
                    src = ps[:, n % 4, 0:2 * S].rearrange("p (b s) -> p b s", b=2)
                    act.copy(k16[:, 0, 2 * pair:2 * pair + 2, 0:S], src).then_inc(s_k_hi, 1)
                for n in range(1, NTERN, 2):
                    act.wait_ge(s_ternT, n + 1)
                    ternary_out(act.copy, n).then_inc(s_ternC[1], 1)

            def x_hi(c):
                for tt in range(TT):
                    wait(act, s_xt, c, TT, tt + 1)
                    act.copy(xrows16[:, 0, :, tt * P:(tt + 1) * P],
                             ps[:, tt, :].rearrange("p (k t) -> p k t", k=KD)).then_inc(s_xt_hi, 1)

            def q_hi(c, n):
                p = n // 2
                wait(act, s_q, c, QM, n + 1)
                if n >= 2:
                    wait(act, s_q_lo, c, QM, n - 1)
                if n % 2 == 0:
                    wait(act, s_qst[p % 2], c, QDMA * QM // 4, QDMA * (p // 2))
                if n == 0:
                    wait(act, s_f1, c - 1, JH, 0)
                act.mul(q32[:, n % 2, :], ps[:, B_Q, :], 1.0 / WSCALE).then_inc(s_q32, 1)
                wait(act, s_q32, c, QM, n + 1)
                act.copy(q_pair[p % 2][:, n % 2, 0, :], q32[:, n % 2, :]).then_inc(s_q_hi, 1)

            def copy_first(c, gi):
                if gi % 2:
                    return
                wait(act, s_pv, c, QM, gi + 1)
                wait(act, s_ol2, c, KD, gi // 2)
                act.copy(o_first, ps[:, B_O, :])
                act.copy(l_first, ps[:, B_L, :]).then_inc(s_ol1, 1)

            def exponentials(c, gi):
                buf = gi % 2
                wait(act, s_s, c, 2 * QM, 2 * gi + 1)
                if gi >= 2:
                    wait(act, s_pv, c, QM, gi - 1)
                act.activation(probs[:, buf, 0:2, :], ps[:, 0:2, :], ACT.Exp).then_inc(s_p, 1)
                wait(act, s_s, c, 2 * QM, 2 * gi + 2)
                act.activation(probs[:, buf, 2:5, :], ps[:, 2:5, :], ACT.Exp).then_inc(s_p, 1)

            def attn_hi(c, mp):
                wait(act, s_att, c, KD, mp + 1)
                act.mul(attn16[:, 0, mp, :], attn[:, mp % 2, :], ASCALE).then_inc(s_att_hi, 1)
                if mp == 0:
                    pass
                elif mp == 1:
                    wait(act, s_rms, c, 1, 0)
                else:
                    wait(act, s_sqsum, c, KD - 1, mp - 1)
                act.activation(attn_sq[:, mp % 2, :], attn[:, mp % 2, :], ACT.Square).then_inc(s_sq, 1)

            def h_hi(c, ahead):
                wait(act, s_ht, c, 1, 1)
                if ahead:
                    wait(act, s_qst[0], c + 1, QDMA * QM // 4, QDMA * QM // 4)
                for k in range(KD):
                    act.activation(rows16[:, 0, k, :], ps[:, B_H + k, :], ACT.Identity,
                                   scale=g1_col[:, k:k + 1]).then_inc(s_ht_hi, 1)

            def gelu(c, j):
                wait(act, s_f1, c, JH, j + 1)
                if j >= 2:
                    wait(act, s_acc, c, JH - 1, max(1, j - 2))
                    wait(act, s_gg_lo, c, JH, j - 1)
                act.activation(gelu_t[:, j % 2, :], ps[:, B_H + j % 2, :], ACT.Gelu, bias=bias1[:, j:j + 1],
                               scale=wstep[:, 0:1]).then_inc(s_gelu, 1)
                wait(act, s_gelu, c, JH, j + 1)
                if j >= 3:
                    wait(act, s_f2, c, JH, j - 2)
                act.activation(gg16[:, j % 3, 0, :], gelu_t[:, j % 2, :], ACT.Identity,
                               scale=g2_col[:, j:j + 1]).then_inc(s_gg_hi, 1)
                act.activation(gsq_t[:, j % 2, :], gelu_t[:, j % 2, :], ACT.Square).then_inc(s_gsq, 1)

            def iteration(i, ahead, ahead2):
                for what, n in STEPS:
                    if what == "q" and ahead:
                        q_hi(i + 1, n)
                    elif what == "s":
                        exponentials(i, n)
                    elif what == "v":
                        copy_first(i, n)
                    elif what == "a":
                        attn_hi(i, n)
                if ahead:
                    for n in range(QLATE, QM):
                        q_hi(i + 1, n)
                h_hi(i, ahead)
                if ahead2:
                    x_hi(i + 2)
                for j in range(JH):
                    gelu(i, j)

            setup()
            x_hi(0)
            for n in range(QM):
                q_hi(0, n)
            x_hi(1)
            iteration(0, True, True)
            with act.Fori(1, NBLK - 2) as i:
                iteration(i, True, True)
            iteration(NBLK - 2, True, False)
            iteration(NBLK - 1, False, False)

        @block.vector
        def _(dve):
            def setup():
                dve.memset(ones[:], 1.0)
                dve.memset(ones_rest[:], 0.0)
                dve.memset(krows, MSCALE)
                dve.memset(k16, 0.0)
                dve.memset(negmax16[:], 0.0)
                dve.memset(v_new, 0.0).then_inc(s_v0, 1)
                dve.wait_ge(s_v0, 1)
                for i in range(UPT):
                    dve.memset(ones_rest[DH * i:DH * i + SR, DH * i:DH * i + DH], 1.0)
                dve.memset(krows[:, :, S:SPAD], 0.0).then_inc(s_krows, 2)
                dve.wait_ge(s_ident, 2)
                dve.tensor_copy(ident16[:], ident[:]).then_inc(s_consts, 1)
                dve.wait_ge(s_vec, 16 * NVEC)
                dve.wait_ge(s_vect, 1)
                dve.tensor_copy(vec_cols[:], ps[:, 4, 0:NV]).then_inc(s_vecc, 1)
                dve.wait_ge(s_vecc, 1)
                dve.tensor_scalar(g_col, g_col, WSCALE, None, ALU.mult)
                dve.tensor_scalar(neglam[:], neglam[:], -1.0, None, ALU.mult).then_inc(s_gcol, 1)
                for n, (_, rows, kind, at) in enumerate(tiles):
                    bank = ps[:, n % 4, :].rearrange("p (k r) -> p k r", k=KD)
                    if kind == "wq":
                        dve.wait_ge(s_tile_hi, n + 1)
                        cols = slice(at * P, (at + 1) * P)
                        dve.scalar_tensor_tensor(wqT_lo[:, :, cols], bank, WSCALE, wqT_hi[:, :, cols],
                                                 ALU.mult, ALU.subtract).then_inc(s_tile_out, 1)
                    elif kind == "wo":
                        dve.wait_ge(s_tile_hi, n + 1)
                        cols = slice(at * P, (at + 1) * P)
                        for k in range(KD):
                            ins = dve.scalar_tensor_tensor(woT_lo[:, k, cols], bank[:, k, :], g_col[:, k:k + 1],
                                                           woT_hi[:, k, cols], ALU.mult, ALU.subtract)
                        ins.then_inc(s_tile_out, 1)
                for n, (m, pair) in enumerate(KGRP):
                    dve.wait_ge(s_k_hi, n + 1)
                    src = ps[:, n % 4, 0:2 * S].rearrange("p (b s) -> p b s", b=2)
                    dve.tensor_tensor(k16[:, 1, 2 * pair:2 * pair + 2, 0:S], src,
                                      k16[:, 0, 2 * pair:2 * pair + 2, 0:S], ALU.subtract).then_inc(s_k_lo, 1)
                for b in range(BATCH):
                    dve.wait_ge(s_kv, len(KGRP) + b + 1)
                    if b > 0:
                        dve.wait_ge(s_vst, 16 * b)
                    bank = ps[:, b % 2, :]
                    dve.tensor_copy(v_new[:, 0:VM], bank[:, 0:VM]).then_inc(s_vnew, 1)
                    for i in range(UPT):
                        rows = slice(DH * i, DH * i + SR)
                        src = bank[rows, VM:2 * VM].rearrange("p (m e d) -> p m e d", e=2, d=DH)[:, :, i // 2, :]
                        dst = v_new[rows, VM:].rearrange("p (m e d) -> p m e d", e=UPT, d=DH)[:, :, i, :]
                        dve.tensor_copy(dst, src).then_inc(s_vnew, 1)
                dve.wait_ge(s_w1, 16)
                dve.tensor_reduce(wabs[:, 0:1], w1n, AX.XY, ALU.add, apply_absolute_value=True)
                dve.wait_ge(s_w2, 16)
                dve.tensor_reduce(wabs[:, 1:2], w2n, AX.XY, ALU.add, apply_absolute_value=True).then_inc(s_abs, 1)
                dve.wait_ge(s_abssum, 1)
                dve.tensor_scalar(wmean[:], ps[:, 2, 0:2], 1.0 / (HID * D), EPS, ALU.mult, ALU.max).then_inc(s_scale, 1)
                dve.wait_ge(s_scale, 1)
                dve.reciprocal(wscale[:], wmean[:]).then_inc(s_scale, 1)
                dve.wait_ge(s_scale, 2)
                dve.reciprocal(wstep[:], wscale[:]).then_inc(s_scale, 1)
                for n in range(NTERN + 2):
                    if n < NTERN:
                        src, w = natural(n)
                        if n >= 3:
                            dve.wait_ge(s_tern, n - 2)
                        dve.tensor_scalar(signs[:, n % 3, 0, :], src, wscale[:, w:w + 1], 0.5, ALU.mult, ALU.is_gt)
                        dve.tensor_scalar(signs[:, n % 3, 1, :], src, wscale[:, w:w + 1], -0.5, ALU.mult,
                                          ALU.is_lt).then_inc(s_sign, 1)
                    if 1 <= n <= NTERN:
                        dve.wait_ge(s_sign, n)
                        if n >= 3:
                            dve.wait_ge(s_ternT, n - 2)
                        dve.tensor_tensor(tern[:, (n - 1) % 2, :], signs[:, (n - 1) % 3, 0, :],
                                          signs[:, (n - 1) % 3, 1, :], ALU.subtract).then_inc(s_tern, 1)
                    if n >= 2 and n % 2 == 0:
                        dve.wait_ge(s_ternT, n - 1)
                        ternary_out(dve.tensor_copy, n - 2).then_inc(s_ternC[0], 1)
                dve.tensor_copy(b1ln16[:, :, 0], b1ln_col).then_inc(s_b1ln, 1)
                for e, col in ((0, g2_col), (1, b2ln_col)):
                    ins = dve.tensor_copy(ln2_16[:, e, 0, :], col[:])
                ins.then_inc(s_l2, 1)
                dve.wait_ge(s_b1ln, 1)
                dve.tensor_tensor(b1ln16[:, :, 1], b1ln_col, b1ln16[:, :, 0], ALU.subtract).then_inc(s_b1ln, 1)
                dve.wait_ge(s_l2, 1)
                for e, col in ((0, g2_col), (1, b2ln_col)):
                    ins = dve.tensor_tensor(ln2_16[:, e, 1, :], col[:], ln2_16[:, e, 0, :], ALU.subtract)
                ins.then_inc(s_l2, 1)
                dve.wait_ge(s_l2, 2)
                n = 0
                for j in range(JH):
                    for e in range(2):
                        if n >= 2:
                            dve.wait_ge(s_lnrow, n - 1)
                        for h in range(2):
                            ins = dve.tensor_scalar(lnb[:, n % 2, h, :], ones[:], ln2_16[:, e, h, j:j + 1], None, ALU.mult)
                        ins.then_inc(s_lnb, 1)
                        n += 1
                dve.wait_ge(s_lnrow, n)
                dve.tensor_copy(g2_row[:], ps[:, 0, :]).then_inc(s_rows, 1)
                dve.scalar_tensor_tensor(out_const[:], ps[:, 1, :], wstep[:, 1:2], out_const[:], ALU.mult,
                                         ALU.add).then_inc(s_rows, 1)
                dve.wait_ge(s_bias, 1)
                dve.tensor_copy(b2_bcast[:, 0, 0:2 * JH], ps[:, 3, 0:2 * JH]).then_inc(s_bias, 1)
                parts = b2_bcast[:, 0, 0:2 * JH].rearrange("p (j e) -> p j e", e=2)
                dve.wait_ge(s_bias, 2)
                dve.tensor_tensor(b2_bcast[:, 1, 0:JH], parts[:, :, 0], parts[:, :, 1], ALU.add).then_inc(s_bias, 1)
                dve.wait_ge(s_bias, 3)
                dve.scalar_tensor_tensor(bias1, b2_bcast[:, 1, 0:JH], wstep[:, 0:1], bias1, ALU.mult,
                                         ALU.add).then_inc(s_bias, 1)

            def ln1_stats(c):
                wait(dve, s_xin, c, 16, 16)
                for tt in range(TT):
                    ins = dve.bn_stats(stats[:, 0, tt, :], x_in[:, tt, :])
                ins.then_inc(s_st1, 1)
                wait(dve, s_st1, c, 1, 1)
                dve.memset(gate[:], 0.0)
                for tt in range(TT):
                    ins = dve.bn_aggr(mv[:, 0, tt, :], stats[:, 0, tt, :])
                ins.then_inc(s_ag1, 1)
                wait(dve, s_ag1, c, 1, 1)
                dve.tensor_scalar(var[:, 0, :], mv[:, 0, :, 1], EPS, None, ALU.add).then_inc(s_var1, 1)

            def ln1_rows(c):
                wait(dve, s_rstd1, c, 1, 1)
                for tt in range(TT):
                    dve.tensor_scalar(x_in[:, tt, :], x_in[:, tt, :], mv[:, 0, tt, 0:1], rstd[:, 0, tt:tt + 1],
                                      ALU.subtract, ALU.mult).then_inc(s_xhat1, 1)

            def x_lo(c):
                for tt in range(TT):
                    wait(dve, s_xt_hi, c, TT, tt + 1)
                    cols = slice(tt * P, (tt + 1) * P)
                    dve.tensor_tensor(xrows16[:, 1, :, cols], ps[:, tt, :].rearrange("p (k t) -> p k t", k=KD),
                                      xrows16[:, 0, :, cols], ALU.subtract).then_inc(s_xt_lo, 1)

            def row_max(c, tb):
                b, tt = divmod(tb, TT)
                u0, u1 = UPB * b, min(UPB * b + UPB, UNITS)
                wait(dve, s_t, c, NT, tb + 1)
                dve.tensor_reduce(negmax[:, tt, u0:u1],
                                  ps[:, B_O + tb % 2, 0:(u1 - u0) * S].rearrange("p (u s) -> p u s", s=S),
                                  AX.X, ALU.max, negate=True).then_inc(s_tmax, 1)

            def split_maxima(c):
                wait(dve, s_tmax, c, NT, NT)
                wait(dve, s_nmt, c, 1, 0)
                dve.tensor_scalar(negmax16[:, :, 0, :], negmax[:], 1.0 / MSCALE, None, ALU.mult).then_inc(s_nmhi, 1)
                wait(dve, s_nmhi, c, 1, 1)
                dve.scalar_tensor_tensor(negmax16[:, :, 1, :], negmax[:], 1.0 / MSCALE, negmax16[:, :, 0, :],
                                         ALU.mult, ALU.subtract).then_inc(s_nmlo, 1)

            def copy_maxima(c):
                wait(dve, s_nmt, c, 1, 1)
                wait(dve, s_nmst, c, 32, 0)
                dve.tensor_copy(negmaxT[:], ps[0:2 * UNITS, B_O, 0:TB // 2].bitcast(F16)).then_inc(s_nmc, 1)

            def normalise(c, gi):
                mp = gi // 2
                if gi % 2 == 0:
                    return
                wait(dve, s_ol1, c, KD, mp + 1)
                wait(dve, s_pv, c, QM, gi + 1)
                wait(dve, s_att, c, KD, mp)
                dve.tensor_tensor(cross_b, ps[:, B_O, :], l_first, ALU.mult).then_inc(s_o2, 1)
                dve.tensor_tensor(cross_a, ps[:, B_L, :], o_first, ALU.mult)
                dve.tensor_tensor(l_prod, ps[:, B_L, :], l_first, ALU.mult).then_inc(s_ol2, 1)
                wait(dve, s_ol2, c, KD, mp + 1)
                dve.scalar_tensor_tensor(cross_a, cross_b, neglam[:, 0:1], cross_a, ALU.mult, ALU.add).then_inc(s_diff, 1)
                dve.reciprocal(l_prod, l_prod).then_inc(s_inv, 1)
                wait(dve, s_inv, c, KD, mp + 1)
                if mp >= 2:
                    wait(dve, s_sq, c, KD, mp - 1)
                dve.tensor_tensor(attn[:, mp % 2, :], cross_a, l_prod, ALU.mult).then_inc(s_att, 1)

            def attn_lo(c, mp):
                wait(dve, s_att_hi, c, KD, mp + 1)
                dve.scalar_tensor_tensor(attn16[:, 1, mp, :], attn[:, mp % 2, :], ASCALE, attn16[:, 0, mp, :],
                                         ALU.mult, ALU.subtract).then_inc(s_att_lo, 1)

            def mid_rows(c):
                wait(dve, s_rms, c, 1, 1)
                dve.tensor_scalar(var[:, 1, :], ps[:, B_O, 0:TT], 1.0 / D, EPS, ALU.mult, ALU.add).then_inc(s_var2, 1)
                wait(dve, s_rstd2, c, 1, 1)
                dve.tensor_scalar(rms_scale[:], rstd[:, 1, :], (1.0 - LAMBDA_INIT) / (ASCALE * WSCALE), None,
                                  ALU.mult).then_inc(s_rsc, 1)
                wait(dve, s_rsc, c, 1, 1)
                wait(dve, s_xres, c, 16, 16)
                for tt in range(TT + 1):
                    if tt < TT:
                        wait(dve, s_wo, c, TT, tt + 1)
                        dve.scalar_tensor_tensor(x_res[:, tt, :], ps[:, tt, :], rms_scale[:, tt:tt + 1],
                                                 x_res[:, tt, :], ALU.mult, ALU.add).then_inc(s_mid, 1)
                    if tt > 0:
                        wait(dve, s_mid, c, TT, tt)
                        dve.bn_stats(stats[:, 1, tt - 1, :], x_res[:, tt - 1, :]).then_inc(s_st2, 1)
                wait(dve, s_st2, c, TT, TT)
                dve.memset(gate[:], 0.0)
                for tt in range(TT):
                    ins = dve.bn_aggr(mv[:, 1, tt, :], stats[:, 1, tt, :])
                ins.then_inc(s_ag2, 1)
                wait(dve, s_ag2, c, 1, 1)
                dve.tensor_scalar(var[:, 2, :], mv[:, 1, :, 1], 1.0 + EPS, EPS * EPS, ALU.mult, ALU.add).then_inc(s_var3, 1)
                wait(dve, s_rstd3, c, 1, 1)
                for tt in range(TT):
                    dve.tensor_scalar(xhat[:, tt, :], x_res[:, tt, :], mv[:, 1, tt, 0:1], rstd[:, 2, tt:tt + 1],
                                      ALU.subtract, ALU.mult).then_inc(s_xhat2, 1)

            def h_lo(c):
                for k in range(KD):
                    wait(dve, s_ht_hi, c, KD, k + 1)
                    dve.scalar_tensor_tensor(rows16[:, 1, k, :], ps[:, B_H + k, :], g1_col[:, k:k + 1],
                                             rows16[:, 0, k, :], ALU.mult, ALU.subtract).then_inc(s_ht_lo, 1)

            def gelu_lo(c, j):
                wait(dve, s_gg_hi, c, JH, j + 1)
                dve.scalar_tensor_tensor(gg16[:, j % 3, 1, :], gelu_t[:, j % 2, :], g2_col[:, j:j + 1],
                                         gg16[:, j % 3, 0, :], ALU.mult, ALU.subtract).then_inc(s_gg_lo, 1)

            def finish(c):
                G = 4
                wait(dve, s_sums, c, 1, 1)
                dve.tensor_scalar(mean_g[:], ps[:, B_H, 0:TT], 1.0 / HID, None, ALU.mult).then_inc(s_gstep, 1)
                wait(dve, s_gstep, c, G, 1)
                dve.tensor_tensor(meansq_g[:], mean_g[:], mean_g[:], ALU.mult).then_inc(s_gstep, 1)
                wait(dve, s_gstep, c, G, 2)
                dve.scalar_tensor_tensor(var_g[:], ps[:, B_H, TT:2 * TT], 1.0 / HID, meansq_g[:], ALU.mult,
                                         ALU.subtract).then_inc(s_gstep, 1)
                wait(dve, s_gstep, c, G, 3)
                dve.tensor_scalar(var[:, 3, :], var_g[:], EPS, None, ALU.add).then_inc(s_gln, 1)
                wait(dve, s_rstd4, c, 1, 1)
                dve.tensor_scalar(scale_g[:], rstd[:, 3, :], wstep[:, 1:2], None, ALU.mult).then_inc(s_gstep, 1)
                wait(dve, s_gstep, c, G, 4)
                dve.scalar_tensor_tensor(shift_g[:], mean_g[:], -1.0, scale_g[:], ALU.mult, ALU.mult).then_inc(s_gscaled, 1)
                wait(dve, s_const, c, 1, 1)
                wait(dve, s_f2, c, JH, JH)
                for tt in range(TT):
                    dve.scalar_tensor_tensor(x_res[:, tt, :], ps[:, tt, :], scale_g[:, tt:tt + 1], x_res[:, tt, :],
                                             ALU.mult, ALU.add).then_inc(s_y, 1)
                wait(dve, s_gscaled, c, 1, 1)
                for tt in range(TT):
                    wait(dve, s_y, c, TT, tt + 1)
                    dve.scalar_tensor_tensor(x_res[:, tt, :], g2_row[:], shift_g[:, tt:tt + 1], x_res[:, tt, :],
                                             ALU.mult, ALU.add).then_inc(s_out, 1)

            def iteration(i, ahead, ahead2):
                for what, n in STEPS:
                    if what == "v":
                        normalise(i, n)
                    elif what == "a":
                        attn_lo(i, n)
                    elif what == "l" and ahead2:
                        (ln1_rows if n else ln1_stats)(i + 2)
                mid_rows(i)
                h_lo(i)
                if ahead2:
                    x_lo(i + 2)
                for j in range(JH):
                    beside = maxima_beside(j) if ahead else []
                    for tb in beside[:TSTEP // 2]:
                        row_max(i + 1, tb)
                    gelu_lo(i, j)
                    for tb in beside[TSTEP // 2:]:
                        row_max(i + 1, tb)
                    if ahead and j == TLAST:
                        split_maxima(i + 1)
                    if ahead and j == TLAST + 1:
                        copy_maxima(i + 1)
                finish(i)

            setup()
            ln1_stats(0)
            ln1_rows(0)
            x_lo(0)
            ln1_stats(1)
            ln1_rows(1)
            x_lo(1)
            for tb in range(NT):
                row_max(0, tb)
            split_maxima(0)
            copy_maxima(0)
            iteration(0, True, True)
            with dve.Fori(1, NBLK - 2) as i:
                iteration(i, True, True)
            iteration(NBLK - 2, True, False)
            iteration(NBLK - 1, False, False)

        @block.tensor
        def _(pe):
            def setup():
                pe.wait_ge(s_ident, 2)
                pe.wait_ge(s_vec, 16 * NVEC)
                pe.transpose(ps[:, 4, 0:NV], vec_rows, ident[0:NV, 0:NV]).then_inc(s_vect, 1)
                for n, (_, rows, kind, at) in enumerate(tiles):
                    pe.wait_ge(s_stage[n % NSTG], 16 * (n // NSTG + 1))
                    if n >= 4:
                        pe.wait_ge(s_tile_hi, n - 3)
                        lo_read = sum(t[2] in ("wq", "wo") for t in tiles[:n - 3])
                        if lo_read:
                            pe.wait_ge(s_tile_out, lo_read)
                    for k in range(KD):
                        ins = pe.transpose(ps[:, n % 4, k * P:k * P + rows], stage[0:rows, n % NSTG, k * P:(k + 1) * P],
                                           ident[0:rows, 0:rows])
                    ins.then_inc(s_tile, 1)
                pe.wait_ge(s_tile_hi, len(tiles))
                pe.wait_ge(s_tile_out, sum(t[2] in ("wq", "wo") for t in tiles))
                for n, (m, pair) in enumerate(KGRP):
                    if n >= 4:
                        pe.wait_ge(s_k_lo, n - 3)
                    for k in range(KD):
                        ins = pe.matmul(ps[:, n % 4, 0:2 * S], wkT[:, k, m * P:(m + 1) * P],
                                        ctxT[:, k, 2 * pair:2 * pair + 2, :], start=(k == 0), stop=(k == KD - 1))
                    ins.then_inc(s_kv, 1)
                pe.wait_ge(s_k_lo, len(KGRP))
                for b in range(BATCH):
                    if b >= 2:
                        pe.wait_ge(s_vnew, 5 * (b - 1))
                    for k in range(KD):
                        pe.matmul(ps[:, b % 2, 0:VM], ctxT[:, k, b, 0:P], wvT[:, k, :], start=(k == 0), stop=(k == KD - 1))
                    for i in range(UPT):
                        for k in range(KD):
                            ins = pe.matmul(ps[DH * i:DH * i + SR, b % 2, VM:2 * VM], ctxT[:, k, b, P:S], wvT[:, k, :],
                                            start=(k == 0), stop=(k == KD - 1))
                    ins.then_inc(s_kv, 1)
                pe.wait_ge(s_abs, 1)
                pe.matmul(ps[:, 2, 0:2], ones[:], wabs[:], start=True, stop=True).then_inc(s_abssum, 1)
                pe.wait_ge(s_consts, 1)
                for n in range(NTERN):
                    pe.wait_ge(s_tern, n + 1)
                    if n >= 4:
                        pe.wait_ge(s_ternC[n % 2], (n - 4) // 2 + 1)
                    for k in range(KD):
                        ins = pe.transpose(ps[:, 4 + n % 4, 0:TB // 2].bitcast(F16)[:, k * P:(k + 1) * P],
                                           tern[:, n % 2, k * P:(k + 1) * P], ident16[:])
                    ins.then_inc(s_ternT, 1)
                for half in range(2):
                    pe.wait_ge(s_ternC[half], NTERN // 2)
                n = 0
                for j in range(JH):
                    for e in range(2):
                        pe.wait_ge(s_lnb, n + 1)
                        for h in range(2):
                            ins = pe.matmul(ps[:, e, :], lnb[:, n % 2, h, :], w2T[:, j, :], start=(j == 0 and h == 0),
                                            stop=(j == JH - 1 and h == 1))
                        ins.then_inc(s_lnrow, 1)
                        n += 1
                pe.wait_ge(s_b1ln, 2)
                for j in range(JH):
                    for k in range(KD):
                        ins = pe.matmul(ps[:, 3, 2 * j:2 * j + 2], w1T[:, k, j * P:(j + 1) * P], b1ln16[:, k, :],
                                        start=(k == 0), stop=(k == KD - 1))
                ins.then_inc(s_bias, 1)
                pe.wait_ge(s_bias, 4)
                pe.wait_ge(s_rows, 2)

            def split_product(dst, w_hi, w_lo, r_hi, r_lo, first, last):
                pe.matmul(dst, w_hi, r_hi, start=first, stop=False)
                pe.matmul(dst, w_hi, r_lo, start=False, stop=False)
                return pe.matmul(dst, w_lo, r_hi, start=False, stop=last)

            def x_transposes(c):
                wait(pe, s_xt_lo, c, TT, 0)
                for tt in range(TT):
                    wait(pe, s_xhat1, c, TT, tt + 1)
                    for k in range(KD):
                        ins = pe.transpose(ps[:, tt, k * P:(k + 1) * P], x_in[:, tt, k * P:(k + 1) * P], ident[:])
                    ins.then_inc(s_xt, 1)

            def queries(c, n):
                m = ORDER[n]
                wait(pe, s_xt_lo, c, TT, TT)
                wait(pe, s_q32, c, QM, n)
                for k in range(KD):
                    cols = slice(m * P, (m + 1) * P)
                    ins = split_product(ps[:, B_Q, :], wqT_hi[:, k, cols], wqT_lo[:, k, cols], xrows16[:, 0, k, :],
                                        xrows16[:, 1, k, :], k == 0, k == KD - 1)
                ins.then_inc(s_q, 1)

            def row_scores(c, tb):
                b, tt = divmod(tb, TT)
                u0, u1 = UPB * b, min(UPB * b + UPB, UNITS)
                if tb == 0:
                    wait(pe, s_kmax, c, 16, 16)
                p = (u1 - 1) // PAIR
                if tt == 0 and (b == 0 or p > (u0 - 1) // PAIR):
                    wait(pe, s_qst[p % 2], c, QDMA * QM // 4, QDMA * (p // 2 + 1))
                if tb >= 2:
                    wait(pe, s_tmax, c, NT, tb - 1)
                for w, u in enumerate(range(u0, u1)):
                    ins = pe.matmul(ps[:, B_O + tb % 2, w * S:(w + 1) * S], stack[0:STK, u, tt * P:(tt + 1) * P],
                                    k_max[0:STK, key_unit(u), 0:S], start=True, stop=True)
                ins.then_inc(s_t, 1)

            def transpose_maxima(c):
                wait(pe, s_nmlo, c, 1, 1)
                for tt in range(TT):
                    ins = pe.transpose(ps[:, B_O, 0:TB // 2].bitcast(F16)[:, tt * P:(tt + 1) * P],
                                       negmax16[:, tt, :, :].rearrange("p e u -> p (e u)"), ident16[:])
                ins.then_inc(s_nmt, 1)

            def scores(c, gi):
                if gi == 0:
                    wait(pe, s_nmst, c, 32, 32)
                    wait(pe, s_katt, c, 16, 16)
                else:
                    wait(pe, s_p, c, 2 * QM, 2 * gi)
                for i in range(UPT):
                    u = UPT * gi + i
                    if gi == 0 and not (isinstance(c, int) and c == 0):
                        wait(pe, s_y, c - 1, TT, i + 1)
                    ins = pe.matmul(ps[:, i, :], k_att[0:STKM, key_unit(u), 0:P], stack[0:STKM, u, :], start=True, stop=True)
                    if i == 1:
                        ins.then_inc(s_s, 1)
                for i in range(UPT):
                    u = UPT * gi + i
                    ins = pe.matmul(ps[DH * i:DH * i + DH, B_SREST, :], k_att[0:STKM, key_unit(u), P:SPAD],
                                    stack[0:STKM, u, :], start=True, stop=True)
                ins.then_inc(s_s, 1)

            def values(c, gi):
                m, buf = ORDER[gi] % (QM // 2), gi % 2
                wait(pe, s_p, c, 2 * QM, 2 * gi + 2)
                if gi == 0:
                    wait(pe, s_vatt, c, 16, 16)
                elif gi % 2:
                    wait(pe, s_ol1, c, KD, gi // 2 + 1)
                else:
                    wait(pe, s_o2, c, KD, gi // 2)
                for i in range(UPT):
                    kv = (UPT * m + i) // (H // KV)
                    pe.matmul(ps[DH * i:DH * i + DH, B_O, :], v_att[:, kv * DH:(kv + 1) * DH], probs[:, buf, i, :],
                              start=True, stop=False)
                pe.matmul(ps[:, B_O, :], v_att[:, VM + m * P:VM + (m + 1) * P], probs[:, buf, 4, :], start=False, stop=True)
                if gi % 2 == 0 and gi > 0:
                    wait(pe, s_ol2, c, KD, gi // 2)
                for i in range(UPT):
                    pe.matmul(ps[DH * i:DH * i + DH, B_L, :], ones[:, 0:DH], probs[:, buf, i, :], start=True, stop=False)
                pe.matmul(ps[:, B_L, :], ones_rest[:], probs[:, buf, 4, :], start=False, stop=True).then_inc(s_pv, 1)

            def rms_sums(c):
                wait(pe, s_sqsum, c, KD - 1, KD - 1)
                wait(pe, s_o2, c, KD, KD)
                for tt in range(TT):
                    ins = pe.matmul(ps[:, B_O, tt:tt + 1], sq_acc[:, tt * P:(tt + 1) * P], ones[:, 0:1], start=True, stop=True)
                ins.then_inc(s_rms, 1)

            def out_projection(c, tt, pairs):
                wait(pe, s_att_lo, c, KD, pairs[-1] + 1)
                cols = slice(tt * P, (tt + 1) * P)
                for k in pairs:
                    ins = split_product(ps[:, tt, :], attn16[:, 0, k, cols], attn16[:, 1, k, cols], woT_hi[:, k, :],
                                        woT_lo[:, k, :], k == 0, k == KD - 1)
                if pairs[-1] == KD - 1:
                    ins.then_inc(s_wo, 1)

            def h_transposes(c, ahead):
                if ahead:
                    wait(pe, s_q32, c + 1, QM, QM)
                for tt in range(TT):
                    wait(pe, s_xhat2, c, TT, tt + 1)
                    for k in range(KD):
                        ins = pe.transpose(ps[:, B_H + k, tt * P:(tt + 1) * P], xhat[:, tt, k * P:(k + 1) * P], ident[:])
                ins.then_inc(s_ht, 1)

            def hidden(c, j):
                if j >= 2:
                    wait(pe, s_gelu, c, JH, j - 1)
                for k in range(KD):
                    if j == 0:
                        wait(pe, s_ht_lo, c, KD, k + 1 if k else 2)
                    for e in range(2):
                        ins = pe.matmul(ps[:, B_H + j % 2, :], w1T[:, k, j * P:(j + 1) * P], rows16[:, e, k, :],
                                        start=(k == 0 and e == 0), stop=(k == KD - 1 and e == 1))
                ins.then_inc(s_f1, 1)

            def ffn_out(c, j, ahead2=False):
                wait(pe, s_gg_lo, c, JH, j + 1)
                if j == 0 and ahead2:
                    wait(pe, s_xt_lo, c + 2, TT, TT)
                for tt in range(TT):
                    for e in range(2):
                        ins = pe.matmul(ps[:, tt, :], gg16[:, j % 3, e, tt * P:(tt + 1) * P], w2T[:, j, :],
                                        start=(j == 0 and e == 0), stop=(j == JH - 1 and e == 1))
                ins.then_inc(s_f2, 1)

            def gelu_sums(c):
                wait(pe, s_acc, c, JH - 1, JH - 1)
                for e in range(2):
                    for tt in range(TT):
                        ins = pe.matmul(ps[:, B_H, e * TT + tt:e * TT + tt + 1], acc[:, e, tt * P:(tt + 1) * P],
                                        ones[:, 0:1], start=True, stop=True)
                ins.then_inc(s_sums, 1)

            def iteration(i, ahead, ahead2):
                for what, n in STEPS:
                    if what == "q" and ahead:
                        queries(i + 1, n)
                    elif what == "s":
                        scores(i, n)
                    elif what == "v":
                        values(i, n)
                for tt in range(TT):
                    out_projection(i, tt, (0, 1, 2))
                out_projection(i, 0, (3,))
                out_projection(i, 1, (3,))
                rms_sums(i)
                out_projection(i, 2, (3,))
                out_projection(i, 3, (3,))
                if ahead:
                    for n in range(QLATE, QM):
                        queries(i + 1, n)
                h_transposes(i, ahead)
                if ahead2:
                    wait(pe, s_mid, i, TT, TT)
                    x_transposes(i + 2)
                for j in range(JH):
                    beside = maxima_beside(j) if ahead else []
                    hidden(i, j)
                    for tb in beside[:TSTEP // 2]:
                        row_scores(i + 1, tb)
                    if j >= 2:
                        ffn_out(i, j - 2, ahead2)
                    for tb in beside[TSTEP // 2:]:
                        row_scores(i + 1, tb)
                    if ahead and j == TLAST + 1:
                        transpose_maxima(i + 1)
                ffn_out(i, JH - 2)
                ffn_out(i, JH - 1)
                gelu_sums(i)

            setup()
            x_transposes(0)
            for n in range(QM):
                queries(0, n)
            x_transposes(1)
            for tb in range(NT):
                row_scores(0, tb)
            transpose_maxima(0)
            iteration(0, True, True)
            with pe.Fori(1, NBLK - 2) as i:
                iteration(i, True, True)
            iteration(NBLK - 2, True, False)
            iteration(NBLK - 1, False, False)

    return nc


_INS = ["x", "ctx_1024", "L0_xattn_Wq", "L0_xattn_Wk", "L0_xattn_Wv", "L0_xattn_Wo", "L0_xattn_lam", "L0_xattn_g",
        "L0_ffn_ln1_g", "L0_ffn_ln1_b", "L0_ffn_w1", "L0_ffn_b1", "L0_ffn_ln2_g", "L0_ffn_ln2_b", "L0_ffn_w2",
        "L0_ffn_b2"]


def kernel(**inputs):
    import numpy as np
    import concourse.bacc as bacc
    from concourse.bass_utils import run_bass_kernel_spmd

    nc = bacc.Bacc("TRN2", target_bir_lowering=False, num_devices=1)
    arrays, args = {}, []
    for name in _INS:
        a = np.ascontiguousarray(inputs[name])
        if a.ndim == 0:
            a = a.reshape(1)
        arrays[f"in_{name}"] = a
        args.append(nc.dram_tensor(f"in_{name}", a.shape, mybir.dt.from_np(a.dtype), kind="ExternalInput").ap())
    out = nc.dram_tensor("out", (BATCH, T, D), F32, kind="ExternalOutput").ap()
    build(nc, *args, out)
    return run_bass_kernel_spmd(nc, [arrays], core_ids=[0]).results[0]["out"]
```

```python
import math
from contextlib import ExitStack

import concourse.bass as bass
from concourse import mybir

F32 = mybir.dt.float32
F16 = mybir.dt.float16
ALU = mybir.AluOpType
ACT = mybir.ActivationFunctionType
AX = mybir.AxisListType

P = 128
D = 512
KD = D // P
BATCH, T, S = 4, 2048, 154
H, KV, DH = 16, 8, 32
HID = 2048
JH = HID // P
TB = 512
TT = TB // P
NBLK = BATCH * T // TB
BLK_PER_BATCH = T // TB
UNITS = 2 * H
KUNITS = 2 * KV
QM = UNITS * DH // P
UPT = P // DH
SR = S - P
SPAD = P + DH
STK = 3 * DH
STKM = STK + 2
MSCALE = 64.0
WSCALE = 256.0
ASCALE = 16.0
PSCALE = 1024.0
VSCALE = 16.0
OSCALE = PSCALE * VSCALE
EPS = 1e-5
LAMBDA_INIT = 0.8 - 0.6 * math.exp(-0.3 * 12)
UPB = 3
TBLK = -(-UNITS // UPB)
NT = TT * TBLK
TSTEP = 4
ORDER = [m for p in range(QM // 2) for m in (p, p + QM // 2)]
STEPS = [(w[0], int(w[1])) for w in (
    "q0 q1 s0 q2 s1 v0 s2 v1 s3 v2 s4 a0 v3 q3 l0 s5 v4 q4 l1 s6 a1 v5 q5 s7 v6 a2 v7 a3").split()]
WFIRST = 13
PROLOGUE = [(w.rstrip("0123456789"), int(w.lstrip("tqmrxys") or 0)) for w in (
    " ".join(f"t{n}" for n in range(18)) + " xs t18 t19 xr t20 t21 xt t22 t23 q0 t24 t25 q1 t26 t27 q2 t28 t29 "
    "q3 t30 t31 q4 ys r0 m0 yr q5 m1 q6 q7 yt m2 m3").split()]
MSHARE = [range(0, 8), range(8, 20), range(20, 32), range(32, NT)]
QLATE = 6
WCHUNK = 4
TFIRST = 1
TLAST = TFIRST + -(-NT // TSTEP) - 1
PAIR = 2 * UPT
QDMA = 3 * UPT * 16


def key_unit(slot):
    u = UPT * ORDER[slot // UPT] + slot % UPT
    return u // H * KV + (u % H) // (H // KV)


def maxima_beside(j):
    first = TSTEP * (j - TFIRST)
    return list(range(max(first, 0), max(min(first + TSTEP, NT), 0)))


def wait(eng, sem, c, per, k):
    if isinstance(c, int) and c * per + k <= 0:
        return
    eng.wait_ge(sem, c * per + k)


def build(nc, x, ctx, wq, wk, wv, wo, lam, g, ln1_g, ln1_b, w1, b1, ln2_g, ln2_b, w2, b2, out):
    x_blk = x.rearrange("b t d -> (b t) d").rearrange("(c s p) d -> c p s d", s=TT, p=P)
    out_blk = out.rearrange("b t d -> (b t) d").rearrange("(c s p) d -> c p s d", s=TT, p=P)
    k_store = nc.dram_tensor("k_store", (STKM, KUNITS, BATCH, SPAD), F16, kind="Internal").ap()
    v_store = nc.dram_tensor("v_store", (BATCH, P, KV * DH + QM // 2 * P), F32, kind="Internal").ap()
    VM = KV * DH

    with ExitStack() as es:
        def sb(name, shape, dt):
            return es.enter_context(nc.sbuf_tensor(name, shape, dt))

        def sem(name):
            return es.enter_context(nc.semaphore(name))

        ps = es.enter_context(nc.psum_tensor("ps", [P, 8, 512], F32))
        B_SREST, B_Q, B_O, B_L = 4, 5, 6, 7

        def value_banks(gi):
            return (B_SREST, TT - 1) if gi == QM - 1 else (B_O, B_L)

        def query_bank(n):
            return B_L if n in (1, QM - 1) else B_Q

        B_H = 4

        wqT_hi, wqT_lo = sb("wqT_hi", [P, KD, 2 * H * DH], F16), sb("wqT_lo", [P, KD, 2 * H * DH], F16)
        woT_hi, woT_lo = sb("woT_hi", [P, KD, D], F16), sb("woT_lo", [P, KD, D], F16)
        w1T, w2T = sb("w1T", [P, KD, HID], F16), sb("w2T", [P, JH, D], F16)
        ident, ident16 = sb("ident", [P, P], F32), sb("ident16", [P, P], F16)
        ones, ones_rest = sb("ones", [P, P], F32), sb("ones_rest", [P, P], F16)
        neghalf = sb("neghalf", [P, TT], F32)
        neglam = sb("neglam", [P, 1], F32)
        vec_src = [(b1, JH), (ln2_g, JH), (ln2_b, JH), (g, KD), (ln1_g, KD), (ln1_b, KD)]
        NV = sum(n for _, n in vec_src)
        vec_cols = sb("vec_cols", [P, NV], F32)
        vec_at = [sum(n for _, n in vec_src[:i]) for i in range(len(vec_src))]
        bias1, g2_col, b2ln_col, g_col, g1_col, b1ln_col = (
            vec_cols[:, at:at + n] for at, (_, n) in zip(vec_at, vec_src))
        wabs, wmean = sb("wabs", [P, 2, WCHUNK], F32), sb("wmean", [P, 2], F32)
        wtotal = sb("wtotal", [P, 2], F32)
        wscale, wstep = sb("wscale", [P, 2], F32), sb("wstep", [P, 2], F32)
        b1ln16 = sb("b1ln16", [P, KD, 2], F16)
        g2_row, out_const = sb("g2_row", [P, D], F32), sb("out_const", [P, D], F32)
        k_max, k_att = sb("k_max", [P, KUNITS, SPAD], F16), sb("k_att", [P, KUNITS, SPAD], F16)
        v_att = sb("v_att", [P, VM + QM // 2 * P], F32)
        stack_raw = sb("stack_raw", [P, UNITS * TB // 2], F32)
        stack = stack_raw[:].bitcast(F16).rearrange("p (u t) -> p u t", u=UNITS)
        ctxT = stack_raw[:, 0:KD * BATCH * S].rearrange("p (k b s) -> p k b s", k=KD, b=BATCH)
        o1 = KD * BATCH * S
        wkT = stack_raw[:, o1:o1 + KD * D].rearrange("p (k n) -> p k n", k=KD)
        wvT = stack_raw[:, o1 + KD * D:o1 + KD * (D + VM)].rearrange("p (k n) -> p k n", k=KD)
        o2 = o1 + KD * (D + VM)
        NSTG = 5
        stage = stack_raw[:, o2:o2 + NSTG * D].rearrange("p (n d) -> p n d", n=NSTG)
        arena = sb("arena", [P, 2 * HID * D // P], F32)
        w1n = arena[:, 0:JH * D].rearrange("p (r d) -> p r d", r=JH)
        w2n = arena[:, JH * D:2 * JH * D].rearrange("p (r h) -> p r h", r=KD)
        cut = [0]

        def part(words):
            cut[0] += words
            assert cut[0] <= 2 * HID * D // P
            return arena[:, cut[0] - words:cut[0]]

        x_in = part(TT * D).rearrange("p (s d) -> p s d", s=TT)
        q32 = part(2 * TB).rearrange("p (b t) -> p b t", b=2)
        xrows16 = part(KD * TB).bitcast(F16).rearrange("p (e k t) -> p e k t", e=2, k=KD)
        xhat = part(TT * D).rearrange("p (s d) -> p s d", s=TT)
        x_res = part(TT * D).rearrange("p (s d) -> p s d", s=TT)
        probs_words = 2 * 5 * TB
        probs_raw = part(probs_words)
        probs = probs_raw.rearrange("p (b n t) -> p b n t", b=2, n=5)
        p16 = sb("p16", [P, 2, 2, TB], F16)
        gelu_t = probs_raw[:, 0:2 * TB].rearrange("p (b t) -> p b t", b=2)
        gsq_t = probs_raw[:, 2 * TB:4 * TB].rearrange("p (b t) -> p b t", b=2)
        gg16 = probs_raw[:, 4 * TB:7 * TB].bitcast(F16).rearrange("p (b e t) -> p b e t", b=3, e=2)
        acc = probs_raw[:, 7 * TB:9 * TB].rearrange("p (e t) -> p e t", e=2)
        negmax = probs_raw[:, 9 * TB:9 * TB + TT * UNITS].rearrange("p (t u) -> p t u", t=TT)
        negmax16 = probs_raw[:, 9 * TB + TT * UNITS:9 * TB + TT * (UNITS + P // 2)].bitcast(F16).rearrange(
            "p (t e u) -> p t e u", t=TT, u=UNITS)
        attn16 = part(KD * TB).bitcast(F16).rearrange("p (e k t) -> p e k t", e=2, k=KD)
        rows16 = sb("rows16", [P, 2, KD, TB], F16)
        q16 = sb("q16", [P, 2, 2, TB], F16)
        q_pair = [rows16[:, 0, :, :].rearrange("p (n e) t -> p n e t", e=2), q16]
        attn_raw = sb("attn_raw", [P, 9 * TB], F32)
        attn = attn_raw[:, 0:2 * TB].rearrange("p (b t) -> p b t", b=2)
        attn_sq = attn_raw[:, 2 * TB:4 * TB].rearrange("p (b t) -> p b t", b=2)
        o_first, l_first, cross_a, cross_b, l_prod = (attn_raw[:, n * TB:(n + 1) * TB] for n in range(4, 9))
        sq_acc = sb("sq_acc", [P, TB], F32)
        negmaxT = sq_acc[0:2 * UNITS, 0:TB // 2].bitcast(F16)
        signs = attn_raw[:, 0:4 * TB].bitcast(F16).rearrange("p (n e t) -> p n e t", n=4, e=2)
        tern = attn_raw[:, 4 * TB:6 * TB].bitcast(F16).rearrange("p (n t) -> p n t", n=4)
        k16 = attn_raw[:, 0:KV * BATCH * SPAD // 2].bitcast(F16).rearrange(
            "p (m e b s) -> p m e b s", m=KUNITS // UPT, e=2, b=BATCH)
        vec_rows = sq_acc[0:NV, 0:P]
        v_new = attn_raw[:, 6 * TB:].rearrange("p (b n) -> p b n", b=2)
        bias_sums = attn_raw[:, TB:TB + 4 * JH].rearrange("p (e j) -> p e j", e=2)
        ln2_rows = attn_raw[0:4, 0:D]
        pick = sq_acc[0:4, P:3 * P].rearrange("p (e n) -> p e n", e=2)
        krows = k_att[0:2]
        ln2_16 = sb("ln2_16", [P, 2, 2, JH], F16)
        stats = sb("stats", [P, 2, TT, 6], F32)
        gate = sb("gate", [P, 1], F32)
        table = sb("table", [P, 2], F32)
        mv = sb("mv", [P, 2, TT, 2], F32)
        var = sb("var", [P, 4, TT], F32)
        rstd = sb("rstd", [P, 4, TT], F32)
        rms_scale = sb("rms_scale", [P, TT], F32)
        mean_g, meansq_g, var_g = sb("mean_g", [P, TT], F32), sb("meansq_g", [P, TT], F32), sb("var_g", [P, TT], F32)
        scale_g, shift_g = sb("scale_g", [P, TT], F32), sb("shift_g", [P, TT], F32)

        s_ident0, s_ident, s_consts = sem("ident_zero"), sem("ident_ready"), sem("consts_ready")
        s_vec, s_vect, s_vecc = sem("vectors_loaded"), sem("vectors_transposed"), sem("vectors_copied")
        s_w = [sem(f"ffn_weights_loaded{n}") for n in range(2 * WCHUNK)]
        s_stage = [sem(f"stage_loaded{n}") for n in range(NSTG)]
        s_tile, s_tile_hi, s_tile_out = sem("tile_transposed"), sem("tile_hi"), sem("tile_out")
        s_gcol = sem("g_scaled")
        s_kv, s_k_hi, s_k_lo = sem("kv_product"), sem("k_hi"), sem("k_lo")
        s_kst, s_vst = sem("k_stored"), [sem("v_stored0"), sem("v_stored1")]
        s_krst, s_vnew = sem("key_rows_stored"), sem("v_new")
        s_krows, s_v0 = sem("key_rows"), sem("v_cleared")
        s_aabs = sem("abs_summed_by_scalar")
        s_abs, s_abssum, s_scale = sem("abs_summed"), sem("abs_total"), sem("scale_step")
        s_sign, s_ternT, s_ternC = sem("sign_ready"), sem("ternary_transposed"), sem("ternary_copied")
        s_tern = [sem("even_ternary_ready"), sem("odd_ternary_ready")]
        s_b1ln, s_l2, s_pick, s_lnrow, s_lncopy, s_spread, s_bias, s_rows = (sem(n) for n in (
            "b1ln_split", "ln2_split", "pick_ready", "ln2_product", "ln2_copied", "ln2_spread", "bias_ready", "rows_ready"))
        s_xin, s_xres, s_kmax, s_katt, s_vatt = (sem(n) for n in (
            "x_in_loaded", "x_res_loaded", "k_max_loaded", "k_att_loaded", "v_att_loaded"))
        s_st1, s_ag1, s_var1, s_rstd1, s_xhat1 = (sem(n) for n in (
            "ln1_stats", "ln1_aggr", "ln1_var", "ln1_rstd", "ln1_rows"))
        s_xt, s_xt_hi, s_xt_lo = sem("x_transposed"), sem("x_hi"), sem("x_lo")
        s_q, s_q_hi, s_q_lo = sem("q_product"), sem("q_hi"), sem("q_lo")
        s_pair_seen = sem("q_pair_seen")
        s_qst = [sem("even_pair_stacked"), sem("odd_pair_stacked")]
        s_t, s_tmax, s_nmhi, s_nmlo, s_nmt, s_nmc, s_nmst = (sem(n) for n in (
            "row_scores", "row_max", "negmax_hi", "negmax_lo", "negmax_transposed", "negmax_copied", "negmax_stacked"))
        s_s, s_p, s_r_hi, s_r_lo, s_pv, s_ol1, s_o2, s_ol2, s_inv, s_att = (sem(n) for n in (
            "scores", "probs", "rest_probs_hi", "rest_probs_lo", "values_done", "first_copied", "second_values_read", "second_read", "inverse_sum", "attn_ready"))
        s_q32, s_y, s_diff = sem("q_copied"), sem("ffn_out_read"), sem("attn_unscaled")
        s_att_hi, s_att_lo, s_sq, s_sqsum = sem("attn_hi"), sem("attn_lo"), sem("attn_square"), sem("attn_square_sum")
        s_rms, s_var2, s_rstd2, s_rsc = sem("rms_sum"), sem("rms_var"), sem("rms_rstd"), sem("rms_scaled")
        s_wo, s_mid, s_st2, s_ag2, s_var3, s_rstd3, s_xhat2 = (sem(n) for n in (
            "out_projected", "mid_ready", "ln2_stats", "ln2_aggr", "ln2_var", "ln2_rstd", "ln2_rows"))
        s_ht, s_ht_hi, s_ht_lo = sem("h_transposed"), sem("h_hi"), sem("h_lo")
        s_f1, s_gelu, s_gsq, s_gg_hi, s_gg_lo, s_acc = (sem(n) for n in (
            "hidden", "gelu", "gelu_square", "gelu_hi", "gelu_lo", "gelu_summed"))
        s_f2, s_sums, s_gln, s_rstd4, s_const, s_out, s_stored = (sem(n) for n in (
            "ffn_out", "gelu_sums", "gelu_ln_step", "gelu_rstd", "const_added", "out_ready", "out_stored"))
        s_gstep, s_gscaled, s_shift = sem("gelu_ln_small_step"), sem("gelu_ln_scaled"), sem("shift_added")

        tiles = [(ctx[b, r:r + n, :], n, "ctx", (b, r)) for b in range(BATCH) for r, n in ((0, P), (P, SR))]
        tiles += [(wk[r * P:(r + 1) * P, :], P, "wk", r) for r in range(D // P)]
        tiles += [(wv[r * P:(r + 1) * P, :], P, "wv", r) for r in range(VM // P)]
        tiles += [(wq[r * P:(r + 1) * P, :], P, "wq", r) for r in range(QM)]
        tiles += [(wo[r * P:(r + 1) * P, :], P, "wo", r) for r in range(KD)]
        N_KV_TILES = 2 * BATCH + D // P + VM // P
        KGRP = [(m, pair) for m in range(KUNITS * DH // P) for pair in range(BATCH // 2)]
        NTERN = 2 * JH
        NVEC = len(vec_src) + 2
        T_WQ, T_WO = N_KV_TILES, N_KV_TILES + QM
        TERN_BANK = (4, 6)
        WLAG = 1
        VEC_AT = N_KV_TILES - 3

        def keys_beside(n):
            return [g for g in range(len(KGRP)) if T_WQ + g // 2 == n]

        def sums_beside(n, odd):
            return [g for g in range(odd, 2 * WCHUNK, 2) if T_WQ + WLAG + g == n]

        def values_beside(n):
            return [b for b in range(BATCH) if T_WQ + len(KGRP) // 2 + b == n]

        def ternary_out(copy, n):
            src = ps[:, TERN_BANK[n % 2], 0:TB // 2].bitcast(F16).rearrange("p (k r) -> p k r", k=KD)
            if n < JH:
                return copy(w1T[:, :, n * P:(n + 1) * P], src)
            r, q = divmod(n - JH, KD)
            return copy(w2T[:, KD * q:KD * q + KD, r * P:(r + 1) * P], src)

        def ffn_piece(g):
            return arena[:, g * JH * D // WCHUNK:(g + 1) * JH * D // WCHUNK]

        def natural(n):
            if n < JH:
                return w1n[:, n, :], 0
            r, q = divmod(n - JH, KD)
            return w2n[:, r, q * D:(q + 1) * D], 1

        block = es.enter_context(nc.Block())

        @block.sync
        def _(sp):
            def store_keys(m):
                sp.wait_ge(s_k_lo, 2 * m + 2)
                for c3, e in enumerate((0, 0, 1)):
                    dst = k_store[DH * c3:DH * c3 + DH, UPT * m:UPT * m + UPT, :, :]
                    sp.dma_start(dst.rearrange("d u b s -> u d (b s)"), k16[:, m, e, :, :].rearrange(
                        "p b s -> p (b s)")).then_inc(s_kst, 16)

            def setup():
                for n, (src, rows, _, _) in enumerate(tiles):
                    if n >= NSTG:
                        sp.wait_ge(s_tile, n - NSTG + 1)
                    sp.dma_start(stage[0:rows, n % NSTG, :], src).then_inc(s_stage[n % NSTG], 16)
                    if n == VEC_AT:
                        for at, (src, n_rows) in zip(vec_at, vec_src):
                            sp.dma_start(vec_rows[at:at + n_rows, :], src.rearrange("(k p) -> k p", p=P)).then_inc(s_vec, 16)
                        sp.dma_start(neglam[:], lam.rearrange("(a b) -> a b", a=1).broadcast_to([P, 1])).then_inc(s_vec, 16)
                        sp.dma_start(out_const[:], b2.rearrange("(a d) -> a d", a=1).broadcast_to([P, D])).then_inc(s_vec, 16)
                    c = n - WFIRST
                    if 0 <= c < WCHUNK:
                        sp.dma_start(w1n[:, c * JH // WCHUNK:(c + 1) * JH // WCHUNK, :], w1.rearrange(
                            "(c r p) d -> c p r d", p=P, c=WCHUNK)[c]).then_inc(s_w[c], 16)
                    elif WCHUNK <= c < 2 * WCHUNK:
                        r = c - WCHUNK
                        sp.dma_start(w2n[:, r, :], w2.rearrange("(r p) h -> r p h", p=P)[r]).then_inc(s_w[c], 16)
                    if n == T_WQ:
                        sp.wait_ge(s_krows, 2)
                        for b in range(BATCH):
                            sp.dma_start(k_store[STK:STKM, :, b, :], krows).then_inc(s_krst, 16)
                    if 0 <= n - T_WQ - NSTG < KUNITS // UPT:
                        store_keys(n - T_WQ - NSTG)
                for b in range(BATCH):
                    sp.wait_ge(s_vnew, 9 * b + 9)
                    sp.dma_start(v_store[b], v_new[:, b % 2, :]).then_inc(s_vst[b % 2], 16)
                sp.wait_ge(s_sign, JH)
                load_x_in(0)
                sp.wait_ge(s_krst, 16 * BATCH)
                sp.wait_ge(s_kst, 16 * 3 * KUNITS // UPT)
                for half in range(2):
                    sp.wait_ge(s_vst[half], 16 * BATCH // 2)
                load_k_max(0, 0)
                load_kv_att(0, 0)
                load_x_in(1)
                sp.wait_ge(s_sign, NTERN)

            def batch_of(c):
                return c // BLK_PER_BATCH if isinstance(c, int) else sp.snap(c // BLK_PER_BATCH)

            def load_k_max(c, b):
                wait(sp, s_t, c, NT, 0)
                sp.dma_start(k_max[0:STKM], k_store[:, :, b, :]).then_inc(s_kmax, 16)

            def load_kv_att(c, b):
                wait(sp, s_pv, c, QM, 0)
                sp.dma_start(k_att[0:STKM], k_store[:, :, b, :]).then_inc(s_katt, 16)
                sp.dma_start(v_att[:], v_store[b]).then_inc(s_vatt, 16)

            def load_x_in(c):
                wait(sp, s_xt, c, TT, 0)
                sp.dma_start(x_in, x_blk[c]).then_inc(s_xin, 16)

            def load_x_res(c):
                wait(sp, s_stored, c, 16 * TT, 0)
                sp.dma_start(x_res, x_blk[c]).then_inc(s_xres, 16)

            def stack_queries(c, p, before):
                wait(sp, s_q_lo, c, QM, 2 * p + 2)
                if before is not None:
                    sp.sem_inc(s_pair_seen, 1)
                    wait(sp, s_s, before, 2 * QM, 4 * p + 4)
                for i in range(UPT):
                    slots = stack[:, PAIR * p:PAIR * (p + 1), :].rearrange("p (n i) t -> p n i t", n=2)
                    for c3, e in enumerate((0, 1, 0)):
                        sp.dma_start(slots[DH * c3:DH * c3 + DH, :, i, :],
                                     q_pair[p % 2][DH * i:DH * i + DH, :, e, :]).then_inc(s_qst[p % 2], 16)

            def stack_maxima(c):
                wait(sp, s_nmc, c, 1, 1)
                for e in range(2):
                    sp.dma_start(stack[STK + e:STK + e + 1, :, :],
                                 negmaxT[UNITS * e:UNITS * (e + 1), :]).then_inc(s_nmst, 16)

            def store(c):
                for tt in range(TT):
                    wait(sp, s_out, c, TT, tt + 1)
                    sp.dma_start(out_blk[c][:, tt, :], x_res[:, tt, :]).then_inc(s_stored, 16)

            def iteration(i, ahead, ahead2):
                if ahead:
                    b = batch_of(i + 1)
                    load_k_max(i + 1, b)
                if ahead2:
                    load_x_in(i + 2)
                if ahead:
                    for p in range(QLATE // 2):
                        stack_queries(i + 1, p, i)
                load_x_res(i)
                if ahead:
                    for p in range(QLATE // 2, QM // 2):
                        stack_queries(i + 1, p, i)
                    load_kv_att(i + 1, b)
                    stack_maxima(i + 1)
                store(i)

            setup()
            for p in range(QM // 2):
                stack_queries(0, p, None)
            stack_maxima(0)
            iteration(0, True, True)
            with sp.Fori(1, NBLK - 2) as i:
                iteration(i, True, True)
            iteration(NBLK - 2, True, False)
            iteration(NBLK - 1, False, False)
            sp.wait_ge(s_stored, NBLK * 16 * TT)

        @block.gpsimd
        def _(pool):
            def setup():
                pool.memset(ident[:], 0.0).then_inc(s_ident0, 1)
                pool.wait_ge(s_ident0, 1)
                pool.affine_select(out=ident[:], in_=ident[:], compare_op=ALU.not_equal, fill=1.0, base=0,
                                   pattern=[[-1, P]], channel_multiplier=1).then_inc(s_ident, 1)
                pool.memset(neghalf[:], -0.5).then_inc(s_ident, 1)
                pool.wait_ge(s_ident, 2)

            def power(slot, ready, done, c, parts=1):
                for n in range(parts):
                    cols = slice(n * TT // parts, (n + 1) * TT // parts)
                    wait(pool, ready, c, parts, n + 1)
                    pool.tensor_tensor(rstd[:, slot, cols], var[:, slot, cols], neghalf[:, cols], ALU.pow).then_inc(done, 1)

            def q_lo(c, n):
                wait(pool, s_q_hi, c, QM, n + 1)
                pair = q_pair[n // 2 % 2]
                pool.tensor_tensor(pair[:, n % 2, 1, :], q32[:, n % 2, :], pair[:, n % 2, 0, :],
                                   ALU.subtract).then_inc(s_q_lo, 1)

            def sum_squares(c, mp):
                if mp == 0:
                    return
                wait(pool, s_sq, c, KD, mp + 1)
                if mp == 1:
                    wait(pool, s_rms, c, 1, 0)
                    pool.tensor_tensor(sq_acc[:], attn_sq[:, 0, :], attn_sq[:, 1, :], ALU.add).then_inc(s_sqsum, 1)
                else:
                    wait(pool, s_sqsum, c, KD - 1, mp - 1)
                    pool.tensor_tensor(sq_acc[:], sq_acc[:], attn_sq[:, mp % 2, :], ALU.add).then_inc(s_sqsum, 1)

            def add_constant(c):
                wait(pool, s_xhat2, c, TT, TT)
                for tt in range(TT):
                    ins = pool.tensor_tensor(x_res[:, tt, :], x_res[:, tt, :], out_const[:], ALU.add)
                ins.then_inc(s_const, 1)

            def sum_gelu(c, j):
                wait(pool, s_gsq, c, JH, j + 1)
                if j == 1:
                    wait(pool, s_sums, c, 1, 0)
                    for e, src in ((0, gelu_t), (1, gsq_t)):
                        ins = pool.tensor_tensor(acc[:, e, :], src[:, 0, :], src[:, 1, :], ALU.add)
                else:
                    wait(pool, s_acc, c, JH - 1, j - 1)
                    for e, src in ((0, gelu_t), (1, gsq_t)):
                        ins = pool.tensor_tensor(acc[:, e, :], acc[:, e, :], src[:, j % 2, :], ALU.add)
                ins.then_inc(s_acc, 1)

            def iteration(i, ahead, ahead2):
                for what, n in STEPS:
                    if what == "q" and ahead:
                        q_lo(i + 1, n)
                    elif what == "a":
                        sum_squares(i, n)
                    elif what == "l" and n == 0 and ahead2:
                        power(0, s_var1, s_rstd1, i + 2)
                power(1, s_var2, s_rstd2, i)
                if ahead:
                    q_lo(i + 1, QLATE)
                power(2, s_var3, s_rstd3, i, 2)
                if ahead:
                    for n in range(QLATE + 1, QM):
                        q_lo(i + 1, n)
                add_constant(i)
                for j in range(1, JH):
                    sum_gelu(i, j)
                power(3, s_gln, s_rstd4, i)

            def ternary(n):
                pool.wait_ge(s_sign, n + 1)
                if n >= 4:
                    pool.wait_ge(s_ternT, n - 3)
                pool.tensor_tensor(tern[:, n % 4, :], signs[:, n % 4, 0, :], signs[:, n % 4, 1, :],
                                   ALU.subtract).then_inc(s_tern[1], 1)

            setup()
            for at, (what, n) in enumerate(PROLOGUE):
                if what == "t" and n % 2:
                    ternary(n)
                    if PROLOGUE[at - 2][0] == "q":
                        q_lo(0, PROLOGUE[at - 2][1])
                elif what == "xs":
                    power(0, s_var1, s_rstd1, 0)
                elif what == "q" and PROLOGUE[at + 1][0] != "t":
                    q_lo(0, n)
                elif what == "ys":
                    power(0, s_var1, s_rstd1, 1)
            iteration(0, True, True)
            with pool.Fori(1, NBLK - 2) as i:
                iteration(i, True, True)
            iteration(NBLK - 2, True, False)
            iteration(NBLK - 1, False, False)

        @block.scalar
        def _(act):
            def setup():
                act.wait_ge(s_consts, 1)
                for n, (_, rows, kind, at) in enumerate(tiles):
                    act.wait_ge(s_tile, n + 1)
                    bank = ps[:, n % 4, :].rearrange("p (k r) -> p k r", k=KD)
                    if kind == "ctx":
                        b, r = at
                        act.copy(ctxT[:, :, b, r:r + rows], bank[:, :, 0:rows]).then_inc(s_tile_hi, 1)
                    elif kind in ("wk", "wv"):
                        dst = wkT if kind == "wk" else wvT
                        act.copy(dst[:, :, at * P:(at + 1) * P], bank).then_inc(s_tile_hi, 1)
                    elif kind == "wq":
                        act.mul(wqT_hi[:, :, at * P:(at + 1) * P], bank, WSCALE).then_inc(s_tile_hi, 1)
                    else:
                        act.wait_ge(s_gcol, 1)
                        for k in range(KD):
                            ins = act.activation(woT_hi[:, k, at * P:(at + 1) * P], bank[:, k, :], ACT.Identity,
                                                 scale=g_col[:, k:k + 1])
                        ins.then_inc(s_tile_hi, 1)
                    for g in keys_beside(n):
                        m, pair = KGRP[g]
                        act.wait_ge(s_kv, g + 1)
                        if g == 0:
                            act.wait_ge(s_v0, 1)
                        src = ps[:, 4 + g % 2, 0:2 * S].rearrange("p (b s) -> p b s", b=2)
                        act.copy(k16[:, m, 0, 2 * pair:2 * pair + 2, 0:S], src).then_inc(s_k_hi, 1)

                    for g in sums_beside(n, 0):
                        act.wait_ge(s_w[g], 16)
                        if g:
                            act.wait_ge(s_aabs, g // 2)
                        act.activation(q16[:].rearrange("p a b t -> p (a b t)"), ffn_piece(g), ACT.Abs,
                                       accum_out=wabs[:, g // WCHUNK, g % WCHUNK:g % WCHUNK + 1]).then_inc(s_aabs, 1)

            def x_hi(c):
                for tt in range(TT):
                    wait(act, s_xt, c, TT, tt + 1)
                    act.copy(xrows16[:, 0, :, tt * P:(tt + 1) * P],
                             ps[:, tt, :].rearrange("p (k t) -> p k t", k=KD)).then_inc(s_xt_hi, 1)

            def q_hi(c, n):
                p = n // 2
                wait(act, s_q, c, QM, n + 1)
                if n >= 2:
                    wait(act, s_q_lo, c, QM, n - 1)
                if n % 2 == 0:
                    wait(act, s_qst[p % 2], c, QDMA * QM // 4, QDMA * (p // 2))
                if n == 0:
                    wait(act, s_f1, c - 1, JH, 0)
                act.mul(q32[:, n % 2, :], ps[:, query_bank(n), :], 1.0 / WSCALE).then_inc(s_q32, 1)
                wait(act, s_q32, c, QM, n + 1)
                act.copy(q_pair[p % 2][:, n % 2, 0, :], q32[:, n % 2, :]).then_inc(s_q_hi, 1)

            def copy_first(c, gi):
                if gi % 2:
                    return
                wait(act, s_pv, c, QM, gi + 1)
                wait(act, s_ol2, c, KD, gi // 2)
                act.copy(o_first, ps[:, B_O, :])
                act.copy(l_first, ps[:, B_L, :]).then_inc(s_ol1, 1)

            def exponentials(c, gi):
                buf = gi % 2
                wait(act, s_s, c, 2 * QM, 2 * gi + 1)
                if gi >= 2:
                    wait(act, s_pv, c, QM, gi - 1)
                act.activation(probs[:, buf, 0:2, :], ps[:, 0:2, :], ACT.Exp).then_inc(s_p, 1)
                wait(act, s_s, c, 2 * QM, 2 * gi + 2)
                act.activation(probs[:, buf, 2:5, :], ps[:, 2:5, :], ACT.Exp).then_inc(s_p, 1)
                wait(act, s_p, c, 2 * QM, 2 * gi + 2)
                act.mul(p16[:, buf, 0, :], probs[:, buf, 4, :], PSCALE).then_inc(s_r_hi, 1)

            def attn_hi(c, mp):
                wait(act, s_att, c, KD, mp + 1)
                act.mul(attn16[:, 0, mp, :], attn[:, mp % 2, :], ASCALE / OSCALE).then_inc(s_att_hi, 1)
                if mp == 1:
                    wait(act, s_rms, c, 1, 0)
                elif mp >= 2:
                    wait(act, s_sqsum, c, KD - 1, mp - 1)
                act.activation(attn_sq[:, mp % 2, :], attn[:, mp % 2, :], ACT.Square,
                               scale=1.0 / OSCALE).then_inc(s_sq, 1)

            def h_hi(c, ahead):
                wait(act, s_ht, c, 1, 1)
                if ahead:
                    wait(act, s_qst[0], c + 1, QDMA * QM // 4, QDMA * QM // 4)
                for k in range(KD):
                    act.activation(rows16[:, 0, k, :], ps[:, B_H + k, :], ACT.Identity,
                                   scale=g1_col[:, k:k + 1]).then_inc(s_ht_hi, 1)

            def gelu(c, j):
                wait(act, s_f1, c, JH, j + 1)
                if j >= 2:
                    wait(act, s_acc, c, JH - 1, max(1, j - 2))
                    wait(act, s_gg_lo, c, JH, j - 1)
                act.activation(gelu_t[:, j % 2, :], ps[:, B_H + j % 2, :], ACT.Gelu, bias=bias1[:, j:j + 1],
                               scale=wstep[:, 0:1]).then_inc(s_gelu, 1)
                wait(act, s_gelu, c, JH, j + 1)
                if j >= 3:
                    wait(act, s_f2, c, JH, j - 2)
                act.activation(gg16[:, j % 3, 0, :], gelu_t[:, j % 2, :], ACT.Identity,
                               scale=g2_col[:, j:j + 1]).then_inc(s_gg_hi, 1)
                act.activation(gsq_t[:, j % 2, :], gelu_t[:, j % 2, :], ACT.Square).then_inc(s_gsq, 1)

            def load_table(function):
                act.activation(table[:, 1:2], table[:, 0:1], function)

            def iteration(i, ahead, ahead2):
                for what, n in STEPS:
                    if what == "q" and ahead:
                        q_hi(i + 1, n)
                    elif what == "s":
                        exponentials(i, n)
                    elif what == "v":
                        copy_first(i, n)
                    elif what == "a":
                        attn_hi(i, n)
                if ahead:
                    for n in range(QLATE, QM):
                        q_hi(i + 1, n)
                load_table(ACT.Gelu)
                h_hi(i, ahead)
                if ahead2:
                    x_hi(i + 2)
                for j in range(JH):
                    gelu(i, j)
                load_table(ACT.Exp)

            setup()
            for what, n in PROLOGUE:
                if what == "t":
                    act.wait_ge(s_ternT, n + 1)
                    ternary_out(act.copy, n).then_inc(s_ternC, 1)
                elif what == "xt":
                    x_hi(0)
                elif what == "q":
                    q_hi(0, n)
                elif what == "yt":
                    x_hi(1)
            iteration(0, True, True)
            with act.Fori(1, NBLK - 2) as i:
                iteration(i, True, True)
            iteration(NBLK - 2, True, False)
            iteration(NBLK - 1, False, False)

        @block.vector
        def _(dve):
            def setup():
                dve.memset(ones[:], 1.0)
                dve.memset(ones_rest[:], 0.0)
                dve.memset(krows, MSCALE)
                dve.memset(k16.rearrange("p m e b s -> p (m e b) s")[:, :, S:SPAD], 0.0)
                dve.memset(table[:], 0.0)
                dve.memset(pick[:, 0, :], 0.0)
                dve.memset(v_new, 0.0).then_inc(s_v0, 1)
                dve.wait_ge(s_v0, 1)
                dve.memset(pick[0:2, 0, :], 1.0).then_inc(s_pick, 1)
                dve.wait_ge(s_pick, 1)
                dve.tensor_scalar(pick[:, 1, :], pick[:, 0, :], -1.0, 1.0, ALU.mult, ALU.add).then_inc(s_pick, 1)
                for i in range(UPT):
                    dve.memset(ones_rest[DH * i:DH * i + SR, DH * i:DH * i + DH], 1.0 / PSCALE)
                dve.memset(krows[:, :, S:SPAD], 0.0).then_inc(s_krows, 2)
                dve.wait_ge(s_ident, 2)
                dve.tensor_copy(ident16[:], ident[:]).then_inc(s_consts, 1)
                dve.wait_ge(s_vec, 16 * NVEC)
                dve.wait_ge(s_vect, 1)
                dve.tensor_copy(vec_cols[:], ps[:, 4, 0:NV]).then_inc(s_vecc, 1)
                dve.wait_ge(s_vecc, 1)
                dve.tensor_scalar(g_col, g_col, WSCALE, None, ALU.mult)
                dve.tensor_scalar(neglam[:], neglam[:], -1.0, None, ALU.mult).then_inc(s_gcol, 1)
                for n, (_, rows, kind, at) in enumerate(tiles):
                    bank = ps[:, n % 4, :].rearrange("p (k r) -> p k r", k=KD)
                    if kind == "wq":
                        dve.wait_ge(s_tile_hi, n + 1)
                        cols = slice(at * P, (at + 1) * P)
                        dve.scalar_tensor_tensor(wqT_lo[:, :, cols], bank, WSCALE, wqT_hi[:, :, cols],
                                                 ALU.mult, ALU.subtract).then_inc(s_tile_out, 1)
                    elif kind == "wo":
                        dve.wait_ge(s_tile_hi, n + 1)
                        cols = slice(at * P, (at + 1) * P)
                        for k in range(KD):
                            ins = dve.scalar_tensor_tensor(woT_lo[:, k, cols], bank[:, k, :], g_col[:, k:k + 1],
                                                           woT_hi[:, k, cols], ALU.mult, ALU.subtract)
                        ins.then_inc(s_tile_out, 1)
                    for g in keys_beside(n):
                        m, pair = KGRP[g]
                        dve.wait_ge(s_k_hi, g + 1)
                        src = ps[:, 4 + g % 2, 0:2 * S].rearrange("p (b s) -> p b s", b=2)
                        dve.tensor_tensor(k16[:, m, 1, 2 * pair:2 * pair + 2, 0:S], src,
                                          k16[:, m, 0, 2 * pair:2 * pair + 2, 0:S], ALU.subtract).then_inc(s_k_lo, 1)
                    for g in sums_beside(n, 1):
                        dve.wait_ge(s_w[g], 16)
                        dve.tensor_reduce(wabs[:, g // WCHUNK, g % WCHUNK:g % WCHUNK + 1], ffn_piece(g), AX.X, ALU.add,
                                          apply_absolute_value=True).then_inc(s_abs, 1)
                    for b in values_beside(n):
                        dve.wait_ge(s_kv, len(KGRP) + b + 1)
                        if b >= 2:
                            dve.wait_ge(s_vst[b % 2], 16 * (b // 2))
                        bank = ps[:, 6 + b % 2, :]
                        dve.tensor_scalar(v_new[:, b % 2, 0:VM], bank[:, 0:VM], OSCALE, None, ALU.mult).then_inc(s_vnew, 1)
                        for e in range(2):
                            if e:
                                dve.wait_ge(s_vnew, 9 * b + 5)
                            for i in range(UPT):
                                rows = slice(DH * i, DH * i + SR)
                                src = bank[rows, VM:2 * VM].rearrange("p (m e d) -> p m e d", e=2, d=DH)[:, :, i // 2, :]
                                hi, lo = (v_new[rows, b % 2, VM:].bitcast(F16).rearrange(
                                    "p (h m e d) -> p h m e d", h=2, e=UPT, d=DH)[:, h, :, i, :] for h in range(2))
                                if e == 0:
                                    dve.tensor_scalar(hi, src, VSCALE, None, ALU.mult).then_inc(s_vnew, 1)
                                else:
                                    dve.scalar_tensor_tensor(lo, src, VSCALE, hi, ALU.mult, ALU.subtract).then_inc(s_vnew, 1)
                dve.tensor_copy(b1ln16[:, :, 0], b1ln_col).then_inc(s_b1ln, 1)
                for e, col in ((0, g2_col), (1, b2ln_col)):
                    ins = dve.tensor_copy(ln2_16[:, e, 0, :], col[:])
                ins.then_inc(s_l2, 1)
                dve.wait_ge(s_b1ln, 1)
                dve.tensor_tensor(b1ln16[:, :, 1], b1ln_col, b1ln16[:, :, 0], ALU.subtract).then_inc(s_b1ln, 1)
                dve.wait_ge(s_l2, 1)
                for e, col in ((0, g2_col), (1, b2ln_col)):
                    ins = dve.tensor_tensor(ln2_16[:, e, 1, :], col[:], ln2_16[:, e, 0, :], ALU.subtract)
                ins.then_inc(s_l2, 1)
                dve.wait_ge(s_abssum, 1)
                dve.tensor_reduce(wtotal[:], ps[:, 5, 0:2 * WCHUNK].rearrange("p (w c) -> p w c", w=2), AX.X,
                                  ALU.add).then_inc(s_scale, 1)
                dve.wait_ge(s_scale, 1)
                dve.tensor_scalar(wmean[:], wtotal[:], 1.0 / (HID * D), EPS, ALU.mult, ALU.max).then_inc(s_scale, 1)
                dve.wait_ge(s_scale, 2)
                dve.reciprocal(wscale[:], wmean[:]).then_inc(s_scale, 1)
                dve.wait_ge(s_scale, 3)
                dve.reciprocal(wstep[:], wscale[:]).then_inc(s_scale, 1)
                dve.wait_ge(s_kst, 16 * 3 * KUNITS // UPT)

            def ternary(n):
                src, w = natural(n)
                if n >= 4:
                    dve.wait_ge(s_tern[n % 2], n // 2 - 1)
                dve.tensor_scalar(signs[:, n % 4, 0, :], src, wscale[:, w:w + 1], 0.5, ALU.mult, ALU.is_gt)
                dve.tensor_scalar(signs[:, n % 4, 1, :], src, wscale[:, w:w + 1], -0.5, ALU.mult,
                                  ALU.is_lt).then_inc(s_sign, 1)
                if n % 2:
                    n -= 1
                    dve.wait_ge(s_sign, n + 1)
                    if n >= 4:
                        dve.wait_ge(s_ternT, n - 3)
                    dve.tensor_tensor(tern[:, n % 4, :], signs[:, n % 4, 0, :], signs[:, n % 4, 1, :],
                                      ALU.subtract).then_inc(s_tern[0], 1)

            def ternary_vectors():
                dve.wait_ge(s_lnrow, 1)
                dve.tensor_copy(ln2_rows, ps[0:4, 0, :]).then_inc(s_lncopy, 1)
                dve.wait_ge(s_bias, 1)
                dve.tensor_copy(bias_sums[:, 0, :], ps[:, 3, 0:2 * JH]).then_inc(s_bias, 1)
                parts = bias_sums[:, 0, :].rearrange("p (j e) -> p j e", e=2)
                dve.wait_ge(s_bias, 2)
                dve.tensor_tensor(bias_sums[:, 1, 0:JH], parts[:, :, 0], parts[:, :, 1], ALU.add).then_inc(s_bias, 1)
                dve.wait_ge(s_bias, 3)
                dve.scalar_tensor_tensor(bias1, bias_sums[:, 1, 0:JH], wstep[:, 0:1], bias1, ALU.mult,
                                         ALU.add).then_inc(s_bias, 1)
                dve.wait_ge(s_spread, 1)
                dve.tensor_copy(g2_row[:], ps[:, 1, :]).then_inc(s_rows, 1)
                dve.scalar_tensor_tensor(out_const[:], ps[:, 2, :], wstep[:, 1:2], out_const[:], ALU.mult,
                                         ALU.add).then_inc(s_rows, 1)

            def ln1_stats(c):
                wait(dve, s_xin, c, 16, 16)
                for tt in range(TT):
                    ins = dve.bn_stats(stats[:, 0, tt, :], x_in[:, tt, :])
                ins.then_inc(s_st1, 1)
                wait(dve, s_st1, c, 1, 1)
                dve.memset(gate[:], 0.0)
                for tt in range(TT):
                    ins = dve.bn_aggr(mv[:, 0, tt, :], stats[:, 0, tt, :])
                ins.then_inc(s_ag1, 1)
                wait(dve, s_ag1, c, 1, 1)
                dve.tensor_scalar(var[:, 0, :], mv[:, 0, :, 1], EPS, None, ALU.add).then_inc(s_var1, 1)

            def ln1_rows(c):
                wait(dve, s_rstd1, c, 1, 1)
                for tt in range(TT):
                    dve.tensor_scalar(x_in[:, tt, :], x_in[:, tt, :], mv[:, 0, tt, 0:1], rstd[:, 0, tt:tt + 1],
                                      ALU.subtract, ALU.mult).then_inc(s_xhat1, 1)

            def x_lo(c):
                for tt in range(TT):
                    wait(dve, s_xt_hi, c, TT, tt + 1)
                    cols = slice(tt * P, (tt + 1) * P)
                    dve.tensor_tensor(xrows16[:, 1, :, cols], ps[:, tt, :].rearrange("p (k t) -> p k t", k=KD),
                                      xrows16[:, 0, :, cols], ALU.subtract).then_inc(s_xt_lo, 1)

            def row_max(c, tb):
                b, tt = divmod(tb, TT)
                u0, u1 = UPB * b, min(UPB * b + UPB, UNITS)
                wait(dve, s_t, c, NT, tb + 1)
                dve.tensor_reduce(negmax[:, tt, u0:u1],
                                  ps[:, B_O + tb % 2, 0:(u1 - u0) * S].rearrange("p (u s) -> p u s", s=S),
                                  AX.X, ALU.max, negate=True).then_inc(s_tmax, 1)

            def split_maxima(c):
                wait(dve, s_tmax, c, NT, NT)
                wait(dve, s_nmt, c, 1, 0)
                dve.memset(negmax16[:, :, 2:, :], 0.0)
                dve.tensor_scalar(negmax16[:, :, 0, :], negmax, 1.0 / MSCALE, None, ALU.mult).then_inc(s_nmhi, 1)
                wait(dve, s_nmhi, c, 1, 1)
                dve.scalar_tensor_tensor(negmax16[:, :, 1, :], negmax, 1.0 / MSCALE, negmax16[:, :, 0, :],
                                         ALU.mult, ALU.subtract).then_inc(s_nmlo, 1)

            def copy_maxima(c):
                wait(dve, s_nmt, c, 1, 1)
                wait(dve, s_nmst, c, 32, 0)
                dve.tensor_copy(negmaxT, ps[0:2 * UNITS, B_O, 0:TB // 2].bitcast(F16)).then_inc(s_nmc, 1)

            def rest_lo(c, gi):
                wait(dve, s_r_hi, c, QM, gi + 1)
                dve.scalar_tensor_tensor(p16[:, gi % 2, 1, :], probs[:, gi % 2, 4, :], PSCALE, p16[:, gi % 2, 0, :],
                                         ALU.mult, ALU.subtract).then_inc(s_r_lo, 1)

            def normalise(c, gi):
                mp = gi // 2
                if gi % 2 == 0:
                    return
                b_o, b_l = value_banks(gi)
                wait(dve, s_ol1, c, KD, mp + 1)
                wait(dve, s_pv, c, QM, gi + 1)
                wait(dve, s_att, c, KD, mp)
                dve.tensor_tensor(cross_b, ps[:, b_o, :], l_first, ALU.mult).then_inc(s_o2, 1)
                dve.tensor_tensor(cross_a, ps[:, b_l, :], o_first, ALU.mult)
                dve.tensor_tensor(l_prod, ps[:, b_l, :], l_first, ALU.mult).then_inc(s_ol2, 1)
                wait(dve, s_ol2, c, KD, mp + 1)
                dve.scalar_tensor_tensor(cross_a, cross_b, neglam[:, 0:1], cross_a, ALU.mult, ALU.add).then_inc(s_diff, 1)
                dve.reciprocal(l_prod, l_prod).then_inc(s_inv, 1)
                wait(dve, s_inv, c, KD, mp + 1)
                if mp >= 2:
                    wait(dve, s_sq, c, KD, mp - 1)
                dve.tensor_tensor(attn[:, mp % 2, :], cross_a, l_prod, ALU.mult).then_inc(s_att, 1)

            def attn_lo(c, mp):
                wait(dve, s_att_hi, c, KD, mp + 1)
                dve.scalar_tensor_tensor(attn16[:, 1, mp, :], attn[:, mp % 2, :], ASCALE / OSCALE, attn16[:, 0, mp, :],
                                         ALU.mult, ALU.subtract).then_inc(s_att_lo, 1)

            def mid_rows(c):
                wait(dve, s_rms, c, 1, 1)
                dve.tensor_scalar(var[:, 1, :], ps[:, B_O, 0:TT], 1.0 / D, EPS, ALU.mult, ALU.add).then_inc(s_var2, 1)
                wait(dve, s_rstd2, c, 1, 1)
                dve.tensor_scalar(rms_scale[:], rstd[:, 1, :], (1.0 - LAMBDA_INIT) / (ASCALE * WSCALE), None,
                                  ALU.mult).then_inc(s_rsc, 1)
                wait(dve, s_rsc, c, 1, 1)
                wait(dve, s_xres, c, 16, 16)
                def mid(half):
                    for tt in (2 * half, 2 * half + 1):
                        wait(dve, s_wo, c, TT, tt + 1)
                        dve.scalar_tensor_tensor(x_res[:, tt, :], ps[:, tt, :], rms_scale[:, tt:tt + 1],
                                                 x_res[:, tt, :], ALU.mult, ALU.add).then_inc(s_mid, 1)

                def variances(half):
                    tts = slice(2 * half, 2 * half + 2)
                    for tt in (2 * half, 2 * half + 1):
                        wait(dve, s_mid, c, TT, tt + 1)
                        dve.bn_stats(stats[:, 1, tt, :], x_res[:, tt, :]).then_inc(s_st2, 1)
                    wait(dve, s_st2, c, TT, 2 * half + 2)
                    dve.memset(gate[:], 0.0)
                    for tt in (2 * half, 2 * half + 1):
                        ins = dve.bn_aggr(mv[:, 1, tt, :], stats[:, 1, tt, :])
                    ins.then_inc(s_ag2, 1)
                    wait(dve, s_ag2, c, 2, half + 1)
                    dve.tensor_scalar(var[:, 2, tts], mv[:, 1, tts, 1], 1.0 + EPS, EPS * EPS, ALU.mult,
                                      ALU.add).then_inc(s_var3, 1)

                mid(0)
                variances(0)
                mid(1)
                variances(1)
                for tt in range(TT):
                    wait(dve, s_rstd3, c, 2, tt // 2 + 1)
                    dve.tensor_scalar(xhat[:, tt, :], x_res[:, tt, :], mv[:, 1, tt, 0:1], rstd[:, 2, tt:tt + 1],
                                      ALU.subtract, ALU.mult).then_inc(s_xhat2, 1)

            def h_lo(c):
                for k in range(KD):
                    wait(dve, s_ht_hi, c, KD, k + 1)
                    dve.scalar_tensor_tensor(rows16[:, 1, k, :], ps[:, B_H + k, :], g1_col[:, k:k + 1],
                                             rows16[:, 0, k, :], ALU.mult, ALU.subtract).then_inc(s_ht_lo, 1)

            def gelu_lo(c, j):
                wait(dve, s_gg_hi, c, JH, j + 1)
                dve.scalar_tensor_tensor(gg16[:, j % 3, 1, :], gelu_t[:, j % 2, :], g2_col[:, j:j + 1],
                                         gg16[:, j % 3, 0, :], ALU.mult, ALU.subtract).then_inc(s_gg_lo, 1)

            def finish(c):
                G = 4
                wait(dve, s_sums, c, 1, 1)
                dve.tensor_scalar(mean_g[:], ps[:, B_H, 0:TT], 1.0 / HID, None, ALU.mult).then_inc(s_gstep, 1)
                wait(dve, s_gstep, c, G, 1)
                dve.tensor_tensor(meansq_g[:], mean_g[:], mean_g[:], ALU.mult).then_inc(s_gstep, 1)
                wait(dve, s_gstep, c, G, 2)
                dve.scalar_tensor_tensor(var_g[:], ps[:, B_H, TT:2 * TT], 1.0 / HID, meansq_g[:], ALU.mult,
                                         ALU.subtract).then_inc(s_gstep, 1)
                wait(dve, s_gstep, c, G, 3)
                dve.tensor_scalar(var[:, 3, :], var_g[:], EPS, None, ALU.add).then_inc(s_gln, 1)
                wait(dve, s_rstd4, c, 1, 1)
                dve.tensor_scalar(scale_g[:], rstd[:, 3, :], wstep[:, 1:2], None, ALU.mult).then_inc(s_gstep, 1)
                wait(dve, s_gstep, c, G, 4)
                dve.scalar_tensor_tensor(shift_g[:], mean_g[:], -1.0, scale_g[:], ALU.mult, ALU.mult).then_inc(s_gscaled, 1)
                wait(dve, s_const, c, 1, 1)
                wait(dve, s_f2, c, JH, JH)
                for tt in range(TT):
                    dve.scalar_tensor_tensor(x_res[:, tt, :], ps[:, tt, :], scale_g[:, tt:tt + 1], x_res[:, tt, :],
                                             ALU.mult, ALU.add).then_inc(s_y, 1)
                wait(dve, s_gscaled, c, 1, 1)
                for tt in range(TT):
                    wait(dve, s_y, c, TT, tt + 1)
                    dve.scalar_tensor_tensor(x_res[:, tt, :], g2_row[:], shift_g[:, tt:tt + 1], x_res[:, tt, :],
                                             ALU.mult, ALU.add).then_inc(s_out, 1)

            def iteration(i, ahead, ahead2):
                for what, n in STEPS:
                    if what == "s":
                        rest_lo(i, n)
                    elif what == "v":
                        normalise(i, n)
                    elif what == "a":
                        attn_lo(i, n)
                    elif what == "l" and ahead2:
                        (ln1_rows if n else ln1_stats)(i + 2)
                mid_rows(i)
                h_lo(i)
                if ahead2:
                    x_lo(i + 2)
                for j in range(JH):
                    beside = maxima_beside(j) if ahead else []
                    for tb in beside[:TSTEP // 2]:
                        row_max(i + 1, tb)
                    gelu_lo(i, j)
                    for tb in beside[TSTEP // 2:]:
                        row_max(i + 1, tb)
                    if ahead and j == TLAST:
                        split_maxima(i + 1)
                    if ahead and j == TLAST + 1:
                        copy_maxima(i + 1)
                finish(i)

            setup()
            for what, n in PROLOGUE:
                if what == "t":
                    ternary(n)
                elif what in ("xs", "ys"):
                    ln1_stats(0 if what == "xs" else 1)
                elif what in ("xr", "yr"):
                    ln1_rows(0 if what == "xr" else 1)
                elif what in ("xt", "yt"):
                    x_lo(0 if what == "xt" else 1)
                elif what == "r":
                    ternary_vectors()
                elif what == "m":
                    for tb in MSHARE[n]:
                        row_max(0, tb)
            split_maxima(0)
            copy_maxima(0)
            iteration(0, True, True)
            with dve.Fori(1, NBLK - 2) as i:
                iteration(i, True, True)
            iteration(NBLK - 2, True, False)
            iteration(NBLK - 1, False, False)

        @block.tensor
        def _(pe):
            def setup():
                pe.wait_ge(s_ident, 2)
                for n, (_, rows, kind, at) in enumerate(tiles):
                    pe.wait_ge(s_stage[n % NSTG], 16 * (n // NSTG + 1))
                    if n >= 4:
                        pe.wait_ge(s_tile_hi, n - 3)
                        lo_read = sum(t[2] in ("wq", "wo") for t in tiles[:n - 3])
                        if lo_read:
                            pe.wait_ge(s_tile_out, lo_read)
                    for k in range(KD):
                        ins = pe.transpose(ps[:, n % 4, k * P:k * P + rows], stage[0:rows, n % NSTG, k * P:(k + 1) * P],
                                           ident[0:rows, 0:rows])
                    ins.then_inc(s_tile, 1)
                    if n == N_KV_TILES - 1:
                        pe.wait_ge(s_vec, 16 * NVEC)
                        pe.transpose(ps[:, 4, 0:NV], vec_rows, ident[0:NV, 0:NV]).then_inc(s_vect, 1)
                    for g in keys_beside(n):
                        m, pair = KGRP[g]
                        if g == 0:
                            pe.wait_ge(s_tile_hi, T_WQ - VM // P)
                            pe.wait_ge(s_vecc, 1)
                        if g >= 2:
                            pe.wait_ge(s_k_lo, g - 1)
                        for k in range(KD):
                            ins = pe.matmul(ps[:, 4 + g % 2, 0:2 * S], wkT[:, k, m * P:(m + 1) * P],
                                            ctxT[:, k, 2 * pair:2 * pair + 2, :], start=(k == 0), stop=(k == KD - 1))
                        ins.then_inc(s_kv, 1)
                    for b in values_beside(n):
                        if b == 0:
                            pe.wait_ge(s_tile_hi, T_WQ)
                        if b >= 2:
                            pe.wait_ge(s_vnew, 9 * (b - 1))
                        bank = ps[:, 6 + b % 2, :]
                        for k in range(KD):
                            pe.matmul(bank[:, 0:VM], ctxT[:, k, b, 0:P], wvT[:, k, :], start=(k == 0), stop=(k == KD - 1))
                        for i in range(UPT):
                            for k in range(KD):
                                ins = pe.matmul(bank[DH * i:DH * i + SR, VM:2 * VM], ctxT[:, k, b, P:S], wvT[:, k, :],
                                                start=(k == 0), stop=(k == KD - 1))
                        ins.then_inc(s_kv, 1)
                pe.wait_ge(s_abs, WCHUNK)
                pe.wait_ge(s_aabs, WCHUNK)
                pe.wait_ge(s_k_lo, len(KGRP))
                pe.matmul(ps[:, 5, 0:2 * WCHUNK], ones[:], wabs[:].rearrange("p w c -> p (w c)"), start=True,
                          stop=True).then_inc(s_abssum, 1)
                pe.wait_ge(s_consts, 1)
                pe.wait_ge(s_vnew, 9 * BATCH)
                pe.wait_ge(s_tile_hi, len(tiles))
                pe.wait_ge(s_tile_out, sum(t[2] in ("wq", "wo") for t in tiles))

            def ternary(n):
                pe.wait_ge(s_tern[n % 2], n // 2 + 1)
                if n >= 2:
                    pe.wait_ge(s_ternC, n - 1)
                for k in range(KD):
                    ins = pe.transpose(ps[:, TERN_BANK[n % 2], 0:TB // 2].bitcast(F16)[:, k * P:(k + 1) * P],
                                       tern[:, n % 4, k * P:(k + 1) * P], ident16[:])
                ins.then_inc(s_ternT, 1)

            def ternary_vectors():
                pe.wait_ge(s_ternC, NTERN)
                pe.wait_ge(s_xt_lo, TT)
                pe.wait_ge(s_l2, 2)
                for j in range(JH):
                    ins = pe.matmul(ps[0:4, 0, :], ln2_16[:, :, :, j].rearrange("p e h -> p (e h)"), w2T[:, j, :],
                                    start=(j == 0), stop=(j == JH - 1))
                ins.then_inc(s_lnrow, 1)
                pe.wait_ge(s_b1ln, 2)
                for j in range(JH):
                    for k in range(KD):
                        ins = pe.matmul(ps[:, 3, 2 * j:2 * j + 2], w1T[:, k, j * P:(j + 1) * P], b1ln16[:, k, :],
                                        start=(k == 0), stop=(k == KD - 1))
                ins.then_inc(s_bias, 1)
                pe.wait_ge(s_lncopy, 1)
                pe.wait_ge(s_pick, 2)
                for e in range(2):
                    ins = pe.matmul(ps[:, 1 + e, :], pick[:, e, :], ln2_rows, start=True, stop=True)
                ins.then_inc(s_spread, 1)

            def split_product(dst, w_hi, w_lo, r_hi, r_lo, first, last):
                pe.matmul(dst, w_hi, r_hi, start=first, stop=False)
                pe.matmul(dst, w_hi, r_lo, start=False, stop=False)
                return pe.matmul(dst, w_lo, r_hi, start=False, stop=last)

            def x_transposes(c):
                wait(pe, s_xt_lo, c, TT, 0)
                for tt in range(TT):
                    wait(pe, s_xhat1, c, TT, tt + 1)
                    for k in range(KD):
                        ins = pe.transpose(ps[:, tt, k * P:(k + 1) * P], x_in[:, tt, k * P:(k + 1) * P], ident[:])
                    ins.then_inc(s_xt, 1)

            def queries(c, n):
                m = ORDER[n]
                wait(pe, s_xt_lo, c, TT, TT)
                if n == 1:
                    wait(pe, s_tmax, c, NT, 0)
                elif n < QM - 1:
                    wait(pe, s_q32, c, QM, {0: -1, 2: 1}.get(n, n))
                for k in range(KD):
                    cols = slice(m * P, (m + 1) * P)
                    ins = split_product(ps[:, query_bank(n), :], wqT_hi[:, k, cols], wqT_lo[:, k, cols], xrows16[:, 0, k, :],
                                        xrows16[:, 1, k, :], k == 0, k == KD - 1)
                ins.then_inc(s_q, 1)

            def row_scores(c, tb):
                b, tt = divmod(tb, TT)
                u0, u1 = UPB * b, min(UPB * b + UPB, UNITS)
                if tb == 0:
                    wait(pe, s_kmax, c, 16, 16)
                p = (u1 - 1) // PAIR
                if tt == 0 and (b == 0 or p > (u0 - 1) // PAIR):
                    wait(pe, s_qst[p % 2], c, QDMA * QM // 4, QDMA * (p // 2 + 1))
                if tb >= 2:
                    wait(pe, s_tmax, c, NT, tb - 1)
                for w, u in enumerate(range(u0, u1)):
                    ins = pe.matmul(ps[:, B_O + tb % 2, w * S:(w + 1) * S], stack[0:STK, u, tt * P:(tt + 1) * P],
                                    k_max[0:STK, key_unit(u), 0:S], start=True, stop=True)
                ins.then_inc(s_t, 1)

            def transpose_maxima(c):
                wait(pe, s_nmlo, c, 1, 1)
                for tt in range(TT):
                    ins = pe.transpose(ps[:, B_O, 0:TB // 2].bitcast(F16)[:, tt * P:(tt + 1) * P],
                                       negmax16[:, tt, :, :].rearrange("p e u -> p (e u)"), ident16[:])
                ins.then_inc(s_nmt, 1)

            def scores(c, gi):
                if gi == 0:
                    wait(pe, s_nmst, c, 32, 32)
                    wait(pe, s_katt, c, 16, 16)
                else:
                    wait(pe, s_p, c, 2 * QM, 2 * gi)
                for i in range(UPT):
                    u = UPT * gi + i
                    if gi == 0 and not (isinstance(c, int) and c == 0):
                        wait(pe, s_y, c - 1, TT, i + 1)
                    ins = pe.matmul(ps[:, i, :], k_att[0:STKM, key_unit(u), 0:P], stack[0:STKM, u, :], start=True, stop=True)
                    if i == 1:
                        ins.then_inc(s_s, 1)
                for i in range(UPT):
                    u = UPT * gi + i
                    ins = pe.matmul(ps[DH * i:DH * i + DH, B_SREST, :], k_att[0:STKM, key_unit(u), P:SPAD],
                                    stack[0:STKM, u, :], start=True, stop=True)
                ins.then_inc(s_s, 1)

            def values(c, gi, ahead):
                m, buf = ORDER[gi] % (QM // 2), gi % 2
                b_o, b_l = value_banks(gi)
                wait(pe, s_p, c, 2 * QM, 2 * gi + 2)
                if gi == 0:
                    wait(pe, s_vatt, c, 16, 16)
                elif gi % 2 and gi < QM - 1:
                    wait(pe, s_ol1, c, KD, gi // 2 + 1)
                else:
                    wait(pe, s_o2, c, KD, gi // 2)
                for i in range(UPT):
                    kv = (UPT * m + i) // (H // KV)
                    pe.matmul(ps[DH * i:DH * i + DH, b_o, :], v_att[:, kv * DH:(kv + 1) * DH], probs[:, buf, i, :],
                              start=True, stop=False)
                if gi % 2 == 0 and gi > 0:
                    wait(pe, s_ol2, c, KD, gi // 2)
                if gi == 0 and ahead:
                    wait(pe, s_q32, c + 1, QM, 2)
                for i in range(UPT):
                    pe.matmul(ps[DH * i:DH * i + DH, b_l, :], ones[:, 0:DH], probs[:, buf, i, :], start=True, stop=False)
                wait(pe, s_r_lo, c, QM, gi + 1)
                v_hi, v_lo = (v_att[:, VM:].bitcast(F16).rearrange("p (h n) -> p h n", h=2)[:, h, m * P:(m + 1) * P]
                              for h in range(2))
                split_product(ps[:, b_o, :], v_hi, v_lo, p16[:, buf, 0, :], p16[:, buf, 1, :], False, True)
                pe.matmul(ps[:, b_l, :], ones_rest[:], p16[:, buf, 0, :], start=False, stop=False)
                pe.matmul(ps[:, b_l, :], ones_rest[:], p16[:, buf, 1, :], start=False, stop=True).then_inc(s_pv, 1)

            def rms_sums(c):
                wait(pe, s_sqsum, c, KD - 1, KD - 1)
                wait(pe, s_o2, c, KD, KD)
                for tt in range(TT):
                    ins = pe.matmul(ps[:, B_O, tt:tt + 1], sq_acc[:, tt * P:(tt + 1) * P], ones[:, 0:1], start=True, stop=True)
                ins.then_inc(s_rms, 1)

            def out_projection(c, tt, pairs):
                wait(pe, s_att_lo, c, KD, pairs[-1] + 1)
                cols = slice(tt * P, (tt + 1) * P)
                for k in pairs:
                    ins = split_product(ps[:, tt, :], attn16[:, 0, k, cols], attn16[:, 1, k, cols], woT_hi[:, k, :],
                                        woT_lo[:, k, :], k == 0, k == KD - 1)
                if pairs[-1] == KD - 1:
                    ins.then_inc(s_wo, 1)

            def h_transposes(c, ahead):
                if ahead:
                    wait(pe, s_q32, c + 1, QM, QM)
                for tt in range(TT):
                    wait(pe, s_xhat2, c, TT, tt + 1)
                    for k in range(KD):
                        ins = pe.transpose(ps[:, B_H + k, tt * P:(tt + 1) * P], xhat[:, tt, k * P:(k + 1) * P], ident[:])
                ins.then_inc(s_ht, 1)

            def hidden(c, j):
                if j >= 2:
                    wait(pe, s_gelu, c, JH, j - 1)
                for k in range(KD):
                    if j == 0:
                        wait(pe, s_ht_lo, c, KD, k + 1 if k else 2)
                    for e in range(2):
                        ins = pe.matmul(ps[:, B_H + j % 2, :], w1T[:, k, j * P:(j + 1) * P], rows16[:, e, k, :],
                                        start=(k == 0 and e == 0), stop=(k == KD - 1 and e == 1))
                ins.then_inc(s_f1, 1)

            def ffn_out(c, j, ahead2=False):
                wait(pe, s_gg_lo, c, JH, j + 1)
                if j == 0 and ahead2:
                    wait(pe, s_xt_lo, c + 2, TT, TT)
                for tt in range(TT):
                    for e in range(2):
                        ins = pe.matmul(ps[:, tt, :], gg16[:, j % 3, e, tt * P:(tt + 1) * P], w2T[:, j, :],
                                        start=(j == 0 and e == 0), stop=(j == JH - 1 and e == 1))
                ins.then_inc(s_f2, 1)

            def gelu_sums(c):
                wait(pe, s_acc, c, JH - 1, JH - 1)
                for e in range(2):
                    for tt in range(TT):
                        ins = pe.matmul(ps[:, B_H, e * TT + tt:e * TT + tt + 1], acc[:, e, tt * P:(tt + 1) * P],
                                        ones[:, 0:1], start=True, stop=True)
                ins.then_inc(s_sums, 1)

            def iteration(i, ahead, ahead2):
                for what, n in STEPS:
                    if what == "q" and ahead:
                        queries(i + 1, n)
                    elif what == "s":
                        scores(i, n)
                    elif what == "v":
                        values(i, n, ahead)
                for tt in range(TT):
                    if tt == TT - 1:
                        wait(pe, s_ol2, i, KD, KD)
                    out_projection(i, tt, (0, 1, 2))
                out_projection(i, 0, (3,))
                out_projection(i, 1, (3,))
                rms_sums(i)
                out_projection(i, 2, (3,))
                out_projection(i, 3, (3,))
                if ahead:
                    for n in range(QLATE, QM):
                        if n == QM - 1:
                            wait(pe, s_ol2, i, KD, KD)
                        queries(i + 1, n)
                h_transposes(i, ahead)
                if ahead2:
                    wait(pe, s_mid, i, TT, TT)
                    x_transposes(i + 2)
                for j in range(JH):
                    beside = maxima_beside(j) if ahead else []
                    hidden(i, j)
                    for tb in beside[:TSTEP // 2]:
                        row_scores(i + 1, tb)
                    if j >= 2:
                        ffn_out(i, j - 2, ahead2)
                    for tb in beside[TSTEP // 2:]:
                        row_scores(i + 1, tb)
                    if ahead and j == TLAST + 1:
                        transpose_maxima(i + 1)
                ffn_out(i, JH - 2)
                ffn_out(i, JH - 1)
                gelu_sums(i)

            setup()
            for what, n in PROLOGUE:
                if what == "t":
                    ternary(n)
                elif what == "xt":
                    x_transposes(0)
                elif what == "q":
                    if n == 0:
                        pe.wait_ge(s_scale, 1)
                    if n == QM - 1:
                        pe.wait_ge(s_tmax, MSHARE[1][-1] + 1)
                    queries(0, n)
                elif what == "r":
                    ternary_vectors()
                elif what == "m":
                    if n == 2:
                        pe.wait_ge(s_q32, QM)
                    for tb in MSHARE[n]:
                        row_scores(0, tb)
                elif what == "yt":
                    pe.wait_ge(s_bias, 4)
                    pe.wait_ge(s_rows, 2)
                    x_transposes(1)
            transpose_maxima(0)
            iteration(0, True, True)
            with pe.Fori(1, NBLK - 2) as i:
                iteration(i, True, True)
            iteration(NBLK - 2, True, False)
            iteration(NBLK - 1, False, False)

    return nc


_INS = ["x", "ctx_1024", "L0_xattn_Wq", "L0_xattn_Wk", "L0_xattn_Wv", "L0_xattn_Wo", "L0_xattn_lam", "L0_xattn_g",
        "L0_ffn_ln1_g", "L0_ffn_ln1_b", "L0_ffn_w1", "L0_ffn_b1", "L0_ffn_ln2_g", "L0_ffn_ln2_b", "L0_ffn_w2",
        "L0_ffn_b2"]


def kernel(**inputs):
    import numpy as np
    import concourse.bacc as bacc
    from concourse.bass_utils import run_bass_kernel_spmd

    nc = bacc.Bacc("TRN2", target_bir_lowering=False, num_devices=1)
    arrays, args = {}, []
    for name in _INS:
        a = np.ascontiguousarray(inputs[name])
        if a.ndim == 0:
            a = a.reshape(1)
        arrays[f"in_{name}"] = a
        args.append(nc.dram_tensor(f"in_{name}", a.shape, mybir.dt.from_np(a.dtype), kind="ExternalInput").ap())
    out = nc.dram_tensor("out", (BATCH, T, D), F32, kind="ExternalOutput").ap()
    build(nc, *args, out)
    return run_bass_kernel_spmd(nc, [arrays], core_ids=[0]).results[0]["out"]
```
